# Optimizing a Trainium2 kernel written in Bass

```python
import numpy as np
import jax
import jax.numpy as jnp

def _softmax(x, axis=-1):
    return jax.nn.softmax(x, axis=axis)

def _gelu(x):
    return jax.nn.gelu(x, approximate=True)

def _silu(x):
    return jax.nn.silu(x)

def _sigmoid(x):
    return jax.nn.sigmoid(x)

def _layernorm(x, axis=-1, eps=1e-05):
    m = jnp.mean(x, axis=axis, keepdims=True)
    v = jnp.var(x, axis=axis, keepdims=True)
    return (x - m) / jnp.sqrt(v + eps)

def _scatter_add(tgt, idx, src, axis=0):
    return tgt.at[idx].add(src)

def _segment_sum(src, seg, n):
    return jax.ops.segment_sum(src, seg, n)
kernel_name = 'mk_recurrent_d2_jaxref_r8_4d73da'

def setup_inputs(seed: int=0):
    np.random.seed(seed)
    _w = jnp.asarray

    def _L0_attn_setup():
        import jax, jax.numpy as jnp
        import numpy as np
        B, N, E, H = (1, 512, 256, 16)
        D = E // H
        DEGREE = 4
        LN_EPS = 1e-05
        ROPE_BASE = 10000.0

        def rope_cos_sin(n, d):
            inv_freq = 1.0 / ROPE_BASE ** (jnp.arange(0, d, 2, dtype=jnp.float32) / d)
            t = jnp.arange(n, dtype=jnp.float32)[:, None] * inv_freq[None, :]
            return (jnp.cos(t), jnp.sin(t))

        def apply_rope(x, cos, sin):
            x1, x2 = jnp.split(x, 2, axis=-1)
            c = cos[None, :, None, :]
            s = sin[None, :, None, :]
            return jnp.concatenate([x1 * c - x2 * s, x1 * s + x2 * c], axis=-1)

        def layernorm(x, scale, bias, eps=LN_EPS):
            m = jnp.mean(x, axis=-1, keepdims=True)
            v = jnp.var(x, axis=-1, keepdims=True)
            return (x - m) * jax.lax.rsqrt(v + eps) * scale + bias

        def polynomial_attention(q, k, v, degree, is_causal):
            a = jnp.einsum('bhnd,bhmd->bhnm', q, k) ** degree
            if is_causal:
                a = jnp.tril(a)
            denom = jnp.sum(a, axis=-1, keepdims=True)
            return jnp.einsum('bhnm,bhmd->bhnd', a / denom, v)
        key = jax.random.key(seed)
        k0, k1, k2 = jax.random.split(key, 3)
        x = jax.random.normal(k0, (B, N, E), dtype=jnp.float32)
        w_qkv = jax.random.normal(k1, (E, 3 * E), dtype=jnp.float32) * (1.0 / np.sqrt(E))
        w_out = jax.random.normal(k2, (E, E), dtype=jnp.float32) * (1.0 / np.sqrt(E))
        ln_scale = jnp.ones((D,), dtype=jnp.float32)
        ln_bias = jnp.zeros((D,), dtype=jnp.float32)
        return {'x': x, 'w_qkv': w_qkv, 'w_out': w_out, 'ln_scale': ln_scale, 'ln_bias': ln_bias}
    _L0_attn_in = _L0_attn_setup()

    def _L0_ffn_setup():
        import jax, jax.numpy as jnp
        import numpy as np
        BLOCK_SIZE = 32
        HIDDEN_SIZE = 256
        MLP_DIM = 2048
        NVFP4_LUT = jnp.array([0.0, 0.5, 1.0, 1.5, 2.0, 3.0, 4.0, 6.0, 0.0, -0.5, -1.0, -1.5, -2.0, -3.0, -4.0, -6.0], dtype=jnp.float32)

        def dequant_nvfp4(W_packed, scales, block=BLOCK_SIZE):
            N = W_packed.shape[0]
            low = W_packed & 15
            high = W_packed >> 4 & 15
            idx = jnp.stack([low, high], axis=-1).reshape(N, -1)
            vals = NVFP4_LUT[idx]
            K = vals.shape[1]
            vals = vals.reshape(N, K // block, block) * scales[:, :, None]
            return vals.reshape(N, K)
        key = jax.random.key(seed)
        ks = jax.random.split(key, 7)
        x = jax.random.normal(ks[0], (4, 32, HIDDEN_SIZE), dtype=jnp.float32)
        gate_W_packed = jax.random.randint(ks[1], (MLP_DIM, HIDDEN_SIZE // 2), 0, 32, dtype=jnp.int32)
        gate_scales = jax.random.uniform(ks[2], (MLP_DIM, HIDDEN_SIZE // BLOCK_SIZE), dtype=jnp.float32) * 0.1 + 0.001
        up_W_packed = jax.random.randint(ks[3], (MLP_DIM, HIDDEN_SIZE // 2), 0, 32, dtype=jnp.int32)
        up_scales = jax.random.uniform(ks[4], (MLP_DIM, HIDDEN_SIZE // BLOCK_SIZE), dtype=jnp.float32) * 0.1 + 0.001
        down_W_packed = jax.random.randint(ks[5], (HIDDEN_SIZE, MLP_DIM // 2), 0, 32, dtype=jnp.int32)
        down_scales = jax.random.uniform(ks[6], (HIDDEN_SIZE, MLP_DIM // BLOCK_SIZE), dtype=jnp.float32) * 0.1 + 0.001
        return {'x': x, 'gate_W_packed': gate_W_packed, 'gate_scales': gate_scales, 'up_W_packed': up_W_packed, 'up_scales': up_scales, 'down_W_packed': down_W_packed, 'down_scales': down_scales}
    _L0_ffn_in = _L0_ffn_setup()

    def _L1_attn_setup():
        import jax, jax.numpy as jnp
        import numpy as np
        import math
        B, T, D = (2, 256, 256)
        H, G, DQ, DV = (16, 4, 128, 128)
        REP = H // G
        ROPE_THETA = 10000.0

        def _rope(x):
            t = x.shape[2]
            inv_freq = 1.0 / ROPE_THETA ** (jnp.arange(0, DQ, 2, dtype=jnp.float32) / DQ)
            freqs = jnp.arange(t, dtype=jnp.float32)[:, None] * inv_freq[None, :]
            freqs = jnp.repeat(freqs, 2, axis=-1)
            cos, sin = (jnp.cos(freqs), jnp.sin(freqs))
            x2 = x.reshape(*x.shape[:-1], DQ // 2, 2)
            rot = jnp.stack([-x2[..., 1], x2[..., 0]], axis=-1).reshape(x.shape)
            return x * cos + rot * sin

        def _alibi(t):
            slopes = 2.0 ** (-jnp.arange(1, H + 1, dtype=jnp.float32) * 8.0 / H)
            pos = jnp.arange(t, dtype=jnp.float32)
            diff = jnp.abs(pos[:, None] - pos[None, :])
            return -diff[None, :, :] * slopes[:, None, None]
        key = jax.random.key(seed)
        ks = jax.random.split(key, 5)
        s = 0.02
        return {'hidden_states': jax.random.normal(ks[0], (B, T, D), jnp.float32), 'Wq': jax.random.normal(ks[1], (D, H * DQ), jnp.float32) * s, 'Wk': jax.random.normal(ks[2], (D, G * DQ), jnp.float32) * s, 'Wv': jax.random.normal(ks[3], (D, G * DV), jnp.float32) * s, 'Wo': jax.random.normal(ks[4], (H * DV, D), jnp.float32) * s, 'bo': jnp.zeros((D,), jnp.float32)}
    _L1_attn_in = _L1_attn_setup()

    def _L1_ffn_setup():
        import jax, jax.numpy as jnp
        import numpy as np
        B, S, D = (2, 256, 256)
        I = 128
        E = 32
        K = 4
        NS = 1
        ALPHA = 7.0

        def _clamped_swiglu(x, wg, wu, wd):
            g = jnp.clip(x @ wg.T, -ALPHA, ALPHA)
            u = jnp.clip(x @ wu.T, -ALPHA, ALPHA)
            return jax.nn.silu(g) * u @ wd.T
        key = jax.random.key(seed)
        ks = jax.random.split(key, 9)
        s = 0.02
        return {'hidden': jax.random.normal(ks[0], (B, S, D), jnp.float32), 'router_w': jax.random.normal(ks[1], (E, D), jnp.float32) * s, 'expert_bias': jax.random.normal(ks[2], (E,), jnp.float32) * s, 'gate_w': jax.random.normal(ks[3], (E, I, D), jnp.float32) * s, 'up_w': jax.random.normal(ks[4], (E, I, D), jnp.float32) * s, 'down_w': jax.random.normal(ks[5], (E, D, I), jnp.float32) * s, 'shared_gate_w': jax.random.normal(ks[6], (NS * I, D), jnp.float32) * s, 'shared_up_w': jax.random.normal(ks[7], (NS * I, D), jnp.float32) * s, 'shared_down_w': jax.random.normal(ks[8], (D, NS * I), jnp.float32) * s}
    _L1_ffn_in = _L1_ffn_setup()
    _d = {'L0_attn_x': _L0_attn_in['x'], 'L0_attn_w_qkv': _L0_attn_in['w_qkv'], 'L0_attn_w_out': _L0_attn_in['w_out'], 'L0_attn_ln_scale': _L0_attn_in['ln_scale'], 'L0_attn_ln_bias': _L0_attn_in['ln_bias'], 'L0_ffn_gate_W_packed': _L0_ffn_in['gate_W_packed'], 'L0_ffn_gate_scales': _L0_ffn_in['gate_scales'], 'L0_ffn_up_W_packed': _L0_ffn_in['up_W_packed'], 'L0_ffn_up_scales': _L0_ffn_in['up_scales'], 'L0_ffn_down_W_packed': _L0_ffn_in['down_W_packed'], 'L0_ffn_down_scales': _L0_ffn_in['down_scales'], 'L1_attn_Wq': _L1_attn_in['Wq'], 'L1_attn_Wk': _L1_attn_in['Wk'], 'L1_attn_Wv': _L1_attn_in['Wv'], 'L1_attn_Wo': _L1_attn_in['Wo'], 'L1_attn_bo': _L1_attn_in['bo'], 'L1_ffn_router_w': _L1_ffn_in['router_w'], 'L1_ffn_expert_bias': _L1_ffn_in['expert_bias'], 'L1_ffn_gate_w': _L1_ffn_in['gate_w'], 'L1_ffn_up_w': _L1_ffn_in['up_w'], 'L1_ffn_down_w': _L1_ffn_in['down_w'], 'L1_ffn_shared_gate_w': _L1_ffn_in['shared_gate_w'], 'L1_ffn_shared_up_w': _L1_ffn_in['shared_up_w'], 'L1_ffn_shared_down_w': _L1_ffn_in['shared_down_w']}
    _x0 = _d['L0_attn_x']
    _d['L0_attn_x'] = jax.random.normal(jax.random.fold_in(jax.random.key(seed), 1), (1, 1024, 256), dtype=_x0.dtype)
    del _x0
    return _d

def reference(L0_attn_x, L0_attn_w_qkv, L0_attn_w_out, L0_attn_ln_scale, L0_attn_ln_bias, L0_ffn_gate_W_packed, L0_ffn_gate_scales, L0_ffn_up_W_packed, L0_ffn_up_scales, L0_ffn_down_W_packed, L0_ffn_down_scales, L1_attn_Wq, L1_attn_Wk, L1_attn_Wv, L1_attn_Wo, L1_attn_bo, L1_ffn_router_w, L1_ffn_expert_bias, L1_ffn_gate_w, L1_ffn_up_w, L1_ffn_down_w, L1_ffn_shared_gate_w, L1_ffn_shared_up_w, L1_ffn_shared_down_w):

    def _L0_attn_ref(x, w_qkv, w_out, ln_scale, ln_bias):
        import jax, jax.numpy as jnp
        import numpy as np
        B, N, E, H = (1, 512, 256, 16)
        D = E // H
        DEGREE = 4
        LN_EPS = 1e-05
        ROPE_BASE = 10000.0

        def rope_cos_sin(n, d):
            inv_freq = 1.0 / ROPE_BASE ** (jnp.arange(0, d, 2, dtype=jnp.float32) / d)
            t = jnp.arange(n, dtype=jnp.float32)[:, None] * inv_freq[None, :]
            return (jnp.cos(t), jnp.sin(t))

        def apply_rope(x, cos, sin):
            x1, x2 = jnp.split(x, 2, axis=-1)
            c = cos[None, :, None, :]
            s = sin[None, :, None, :]
            return jnp.concatenate([x1 * c - x2 * s, x1 * s + x2 * c], axis=-1)

        def layernorm(x, scale, bias, eps=LN_EPS):
            m = jnp.mean(x, axis=-1, keepdims=True)
            v = jnp.var(x, axis=-1, keepdims=True)
            return (x - m) * jax.lax.rsqrt(v + eps) * scale + bias

        def polynomial_attention(q, k, v, degree, is_causal):
            a = jnp.einsum('bhnd,bhmd->bhnm', q, k) ** degree
            if is_causal:
                a = jnp.tril(a)
            denom = jnp.sum(a, axis=-1, keepdims=True)
            return jnp.einsum('bhnm,bhmd->bhnd', a / denom, v)
        b, n, e = x.shape
        proj = x @ w_qkv
        q, k, v = jnp.split(proj, 3, axis=-1)
        q = q.reshape(b, n, H, D)
        k = k.reshape(b, n, H, D)
        v = v.reshape(b, n, H, D)
        cos, sin = rope_cos_sin(n, D)
        q = apply_rope(q, cos, sin)
        k = apply_rope(k, cos, sin)
        q = q.transpose(0, 2, 1, 3)
        k = k.transpose(0, 2, 1, 3)
        v = v.transpose(0, 2, 1, 3)
        q = layernorm(q, ln_scale, ln_bias)
        k = layernorm(k, ln_scale, ln_bias)
        out = polynomial_attention(q, k, v, DEGREE, True)
        out = out.transpose(0, 2, 1, 3).reshape(b, n, e)
        out = out @ w_out
        return out

    def _L0_ffn_ref(x, gate_W_packed, gate_scales, up_W_packed, up_scales, down_W_packed, down_scales):
        import jax, jax.numpy as jnp
        import numpy as np
        BLOCK_SIZE = 32
        HIDDEN_SIZE = 256
        MLP_DIM = 2048
        NVFP4_LUT = jnp.array([0.0, 0.5, 1.0, 1.5, 2.0, 3.0, 4.0, 6.0, 0.0, -0.5, -1.0, -1.5, -2.0, -3.0, -4.0, -6.0], dtype=jnp.float32)

        def dequant_nvfp4(W_packed, scales, block=BLOCK_SIZE):
            N = W_packed.shape[0]
            low = W_packed & 15
            high = W_packed >> 4 & 15
            idx = jnp.stack([low, high], axis=-1).reshape(N, -1)
            vals = NVFP4_LUT[idx]
            K = vals.shape[1]
            vals = vals.reshape(N, K // block, block) * scales[:, :, None]
            return vals.reshape(N, K)
        B, S, H = x.shape
        xt = x.reshape(B * S, H)
        Wg = dequant_nvfp4(gate_W_packed, gate_scales)
        Wu = dequant_nvfp4(up_W_packed, up_scales)
        Wd = dequant_nvfp4(down_W_packed, down_scales)
        gate = jnp.einsum('th,nh->tn', xt, Wg)
        up = jnp.einsum('th,nh->tn', xt, Wu)
        gelu = jnp.tanh(0.7978845608028654 * (gate + 0.044715 * gate ** 3)) * gate * 0.5 + gate * 0.5
        inter = gelu * up
        out = jnp.einsum('tn,hn->th', inter, Wd)
        return out.reshape(B, S, H)

    def _L1_attn_ref(hidden_states, Wq, Wk, Wv, Wo, bo):
        import jax, jax.numpy as jnp
        import numpy as np
        import math
        B, T, D = (2, 256, 256)
        H, G, DQ, DV = (16, 4, 128, 128)
        REP = H // G
        ROPE_THETA = 10000.0

        def _rope(x):
            t = x.shape[2]
            inv_freq = 1.0 / ROPE_THETA ** (jnp.arange(0, DQ, 2, dtype=jnp.float32) / DQ)
            freqs = jnp.arange(t, dtype=jnp.float32)[:, None] * inv_freq[None, :]
            freqs = jnp.repeat(freqs, 2, axis=-1)
            cos, sin = (jnp.cos(freqs), jnp.sin(freqs))
            x2 = x.reshape(*x.shape[:-1], DQ // 2, 2)
            rot = jnp.stack([-x2[..., 1], x2[..., 0]], axis=-1).reshape(x.shape)
            return x * cos + rot * sin

        def _alibi(t):
            slopes = 2.0 ** (-jnp.arange(1, H + 1, dtype=jnp.float32) * 8.0 / H)
            pos = jnp.arange(t, dtype=jnp.float32)
            diff = jnp.abs(pos[:, None] - pos[None, :])
            return -diff[None, :, :] * slopes[:, None, None]
        N, t, _ = hidden_states.shape
        q = (hidden_states @ Wq).reshape(N, t, H, DQ).transpose(0, 2, 1, 3)
        k = (hidden_states @ Wk).reshape(N, t, G, DQ).transpose(0, 2, 1, 3)
        v = (hidden_states @ Wv).reshape(N, t, G, DV).transpose(0, 2, 1, 3)
        q = _rope(q)
        k = _rope(k)
        k = jnp.repeat(k, REP, axis=1)
        v = jnp.repeat(v, REP, axis=1)
        scores = jnp.einsum('bhtd,bhsd->bhts', q, k)
        scores = scores + _alibi(t)[None]
        scores = scores / math.sqrt(DQ)
        scores = 30.0 * jnp.tanh(scores / 30.0)
        causal = jnp.tril(jnp.ones((t, t), bool))
        scores = jnp.where(causal[None, None], scores, -jnp.inf)
        probs = jax.nn.softmax(scores, axis=-1)
        ctx = jnp.einsum('bhts,bhsd->bhtd', probs, v)
        ctx = ctx.transpose(0, 2, 1, 3).reshape(N, t, H * DV)
        return ctx @ Wo + bo

    def _L1_ffn_ref(hidden, router_w, expert_bias, gate_w, up_w, down_w, shared_gate_w, shared_up_w, shared_down_w):
        import jax, jax.numpy as jnp
        import numpy as np
        B, S, D = (2, 256, 256)
        I = 128
        E = 32
        K = 4
        NS = 1
        ALPHA = 7.0

        def _clamped_swiglu(x, wg, wu, wd):
            g = jnp.clip(x @ wg.T, -ALPHA, ALPHA)
            u = jnp.clip(x @ wu.T, -ALPHA, ALPHA)
            return jax.nn.silu(g) * u @ wd.T
        Bb, Ss, Dd = hidden.shape
        flat = hidden.reshape(-1, Dd)
        T = flat.shape[0]
        logits = flat @ router_w.T
        scores = jnp.sqrt(jax.nn.softplus(logits))
        _, idx = jax.lax.top_k(scores + expert_bias, K)
        topv = jnp.take_along_axis(scores, idx, axis=1)
        topv = topv / (topv.sum(axis=-1, keepdims=True) + 1e-20)
        probs = jnp.zeros((T, E), flat.dtype).at[jnp.arange(T)[:, None], idx].set(topv)

        def body(acc, xs):
            wg, wu, wd, p = xs
            return (acc + p[:, None] * _clamped_swiglu(flat, wg, wu, wd), None)
        out, _ = jax.lax.scan(body, jnp.zeros_like(flat), (gate_w, up_w, down_w, probs.T))
        out = out + _clamped_swiglu(flat, shared_gate_w, shared_up_w, shared_down_w)
        return out.reshape(Bb, Ss, Dd)
    x = L0_attn_x
    xn = _layernorm(x, axis=-1)
    s = _L0_attn_ref(xn, L0_attn_w_qkv, L0_attn_w_out, L0_attn_ln_scale, L0_attn_ln_bias)
    g = _silu(_L0_ffn_ref(xn, L0_ffn_gate_W_packed, L0_ffn_gate_scales, L0_ffn_up_W_packed, L0_ffn_up_scales, L0_ffn_down_W_packed, L0_ffn_down_scales))
    x = x + s * g
    xn = _layernorm(x, axis=-1)
    s = _L1_attn_ref(xn, L1_attn_Wq, L1_attn_Wk, L1_attn_Wv, L1_attn_Wo, L1_attn_bo)
    g = _silu(_L1_ffn_ref(xn, L1_ffn_router_w, L1_ffn_expert_bias, L1_ffn_gate_w, L1_ffn_up_w, L1_ffn_down_w, L1_ffn_shared_gate_w, L1_ffn_shared_up_w, L1_ffn_shared_down_w))
    x = x + s * g
    return x

_drawn_inputs = setup_inputs


def setup_inputs(seed=0):
    import zlib

    import numpy as np

    out = dict(_drawn_inputs(seed))
    spreads = {'L0_attn_ln_scale': (1.0, 0.2), 'L0_attn_ln_bias': (0.0, 0.1), 'L1_attn_bo': (0.0, 0.8)}
    factors = {'L1_attn_Wq': 8.0,
     'L1_attn_Wk': 8.0,
     'L1_attn_Wv': 8.0,
     'L1_attn_Wo': 8.0,
     'L1_ffn_router_w': 8.0,
     'L1_ffn_expert_bias': 8.0,
     'L1_ffn_gate_w': 8.0,
     'L1_ffn_up_w': 8.0,
     'L1_ffn_down_w': 8.0,
     'L1_ffn_shared_gate_w': 8.0,
     'L1_ffn_shared_up_w': 8.0,
     'L1_ffn_shared_down_w': 8.0}
    for name, (base, spread) in spreads.items():
        noise = np.random.default_rng([zlib.crc32(name.encode()), seed]).standard_normal(out[name].shape)
        drawn = base * np.exp(spread * noise) if base else spread * noise
        out[name] = jnp.asarray(drawn.astype(out[name].dtype))
    for name, factor in factors.items():
        out[name] = (out[name] * factor).astype(out[name].dtype)
    return out
```

```python
from contextlib import ExitStack

import numpy as np

import concourse.bass as bass
from concourse import mybir

ALU = mybir.AluOpType
ACT = mybir.ActivationFunctionType
F32 = mybir.dt.float32
F32R = mybir.dt.float32r
BF16 = mybir.dt.bfloat16
I32 = mybir.dt.int32
U32 = mybir.dt.uint32
AX_X = mybir.AxisListType.X

P = 128
TOK = 1024
NT = TOK // P
D = 256
NC = D // P
HALF = 512
NHALF = TOK // HALF
LN_EPS = 1e-5

H0, D0 = 16, 16
STK = 4 * D0
MLP = 2048
NJ = MLP // (2 * P)
U0 = MLP // P
BLK = 32
GELU_C, GELU_K = 0.7978845608028654, 0.044715
H1, G1, D1 = 16, 4, 128
REP = H1 // G1
CAP = 30.0
PAIR = 2
NE, TOPK, ALPHA = 32, 4, 7.0
U1 = NE + 1

OFF = [sum((NT - i) * P for i in range(j)) for j in range(NT + 1)]
TRI = OFF[NT]


def spans(width):
    return [(a, min(a + HALF, width)) for a in range(0, width, HALF)]


def build_program(nc, x_in, wqkv_in, wout_in, lns_in, lnb_in, gp_in, gs_in, up_in, us_in, dp_in, ds_in,
                  wq_in, wk_in, wv_in, wo_in, bo_in, rw_in, eb_in, eg_in, eu_in, ed_in,
                  ident_in, rope0_in, cos1_in, sin1_in, dist_in, iota_in, out, dbg=None):
    gates_dram = nc.dram_tensor("gates_scratch", (NE, TOK), F32, kind="Internal").ap()

    with ExitStack() as ctx:
        def sem(name):
            return ctx.enter_context(nc.semaphore(name))

        def alloc(scope):
            return lambda name, shape, dt=F32: scope.enter_context(nc.sbuf_tensor(name, shape, dt))

        sb = alloc(ctx)
        ident = sb("ident", [P, P])
        x_tok = sb("x_tok", [P, NT, D])
        xn_tok = sb("xn_tok", [P, NT, D])
        xT_hi = sb("xT_hi", [P, NC, TOK], F32R)
        xT_lo = sb("xT_lo", [P, NC, TOK], F32R)
        s_tok = sb("s_tok", [P, NT, D])
        ln_stats = sb("ln_stats", [P, 6])
        ln_mv = sb("ln_mv", [P, NT, 2])
        ln_var = sb("ln_var", [P, NT])
        ln_sd = sb("ln_sd", [P, NT])
        ln_r = sb("ln_r", [P, NT])
        ln_t = sb("ln_t", [P, NT])
        consts = sb("consts", [P, 4])

        l0 = ExitStack()
        sb = alloc(l0)
        QT = sb("QT", [P, H0 // 2, TOK], F32R)
        KT = sb("KT", [P, H0 // 2, TOK], F32R)
        V0 = sb("V0", [P, NT, H0, D0 + 1])
        A0 = sb("A0", [P, 2, TRI])
        wqkv_hi = sb("wqkv_hi", [P, NC, 3 * D], F32R)
        wqkv_lo = sb("wqkv_lo", [P, NC, 3 * D], F32R)
        stack = sb("stack", [P, 2, 2, H0, 4, D0])
        rope_a = sb("rope_a", [P, 2 * D])
        rope_b = sb("rope_b", [P, 2 * D])
        rope0 = sb("rope0", [P, NT, 2, D0])
        hv = sb("hv", [P, NT, 2 * H0])
        hsd = sb("hsd", [P, NT, 2 * H0])
        hr = sb("hr", [P, NT, 2 * H0])
        ht = sb("ht", [P, NT, 2 * H0])
        hm = sb("hm", [P, 2, 2 * H0])
        lns = sb("lns", [P, 2, D0])
        o_rden = sb("o_rden", [P, NT, 1])
        wqkv = A0[:, 0, 0:NC * 3 * D].rearrange("p (c n) -> p c n", c=NC)
        qk_tok = A0[:, 1, 0:NT * 2 * D].rearrange("p (t n) -> p t n", t=NT)
        qk_sq = rope_a
        o_tok = xn_tok
        l0.close()

        l0b = ExitStack()
        sb = alloc(l0b)
        oT_hi = sb("oT_hi", [P, NC, TOK], F32R)
        oT_lo = sb("oT_lo", [P, NC, TOK], F32R)
        wout = sb("wout", [P, NC, D])
        wout_hi = sb("wout_hi", [P, NC, D], F32R)
        wout_lo = sb("wout_lo", [P, NC, D], F32R)
        f0T = sb("f0T", [P, NC, TOK])
        pk = sb("pk", [P, 2, 3, 2 * P], I32)
        pks = sb("pks", [P, 2, 3, 2 * P])
        mag = sb("mag", [P, 3, 2, 2 * P], I32)
        sgn = sb("sgn", [P, 3, 2, 2 * P], I32)
        dq_a = sb("dq_a", [P, 3, 2, 2 * P], BF16)
        dq_b = sb("dq_b", [P, 3, 2, 2 * P], BF16)
        dq_m = sb("dq_m", [P, 3, 2, 2 * P], BF16)
        dq_s = sb("dq_s", [P, 3, 2, 2 * P], BF16)
        w0 = sb("w0", [P, 2, 3, 2, 2 * P])
        w0_hi = sb("w0_hi", [P, 2, 2, 2, 2 * P], F32R)
        w0_lo = sb("w0_lo", [P, 2, 2, 2, 2 * P], F32R)
        e0_a = sb("e0_a", [P, 2, HALF])
        e0_b = sb("e0_b", [P, 2, HALF])
        h0 = sb("h0", [P, 2, HALF])
        l0b.close()

        l1 = ExitStack()
        sb = alloc(l1)
        cos1 = sb("cos1", [P, TOK])
        sin1 = sb("sin1", [P, TOK])
        dist = sb("dist", [P, TOK])
        wqk = sb("wqk", [P, 2, NC, D1])
        wqk_hi = sb("wqk_hi", [P, 2, NC, D1], F32R)
        wqk_lo = sb("wqk_lo", [P, 2, NC, D1], F32R)
        q_hi = sb("q_hi", [P, 2, TOK], F32R)
        q_lo = sb("q_lo", [P, 2, TOK], F32R)
        k_hi = sb("k_hi", [P, 2, TOK], F32R)
        k_lo = sb("k_lo", [P, 2, TOK], F32R)
        V1 = sb("V1", [P, NT, G1, D1 + 1])
        P1 = sb("P1", [P, 2, TRI])
        cap = sb("cap", [P, 2, TOK])
        swap = sb("swap", [P, HALF])
        rot = sb("rot", [P, HALF])
        rot2 = sb("rot2", [P, HALF])
        c_rden = sb("c_rden", [P, 3, 1])
        ctx_tok = sb("ctx_tok", [P, 2, NT, D1])
        cT_hi = sb("cT_hi", [P, PAIR, TOK], F32R)
        cT_lo = sb("cT_lo", [P, PAIR, TOK], F32R)
        wo = sb("wo", [P, 2, PAIR, D])
        wo_hi = sb("wo_hi", [P, PAIR, D], F32R)
        wo_lo = sb("wo_lo", [P, PAIR, D], F32R)
        bo = sb("bo", [P, D])
        wv = P1[:, 0, 0:NC * G1 * D1].rearrange("p (c n) -> p c n", c=NC)
        wv_hi = sb("wv_hi", [P, NC, G1 * D1], F32R)
        wv_lo = sb("wv_lo", [P, NC, G1 * D1], F32R)
        l1.close()

        l1b = ExitStack()
        sb = alloc(l1b)
        rw = sb("rw", [P, NC, NE])
        rw_hi = sb("rw_hi", [P, NC, NE], F32R)
        rw_lo = sb("rw_lo", [P, NC, NE], F32R)
        ebias = sb("ebias", [P, NE])
        iota = sb("iota", [P, NE])
        lg = sb("lg", [P, NT, NE])
        r_a = sb("r_a", [P, NT, NE])
        r_b = sb("r_b", [P, NT, NE])
        r_c = sb("r_c", [P, NT, NE])
        r_d = sb("r_d", [P, NT, NE])
        top = sb("top", [P, NT, 8])
        topi = sb("topi", [P, NT, 8], U32)
        topf = sb("topf", [P, NT, 8])
        r_sum = sb("r_sum", [P, NT, 1])
        r_inv = sb("r_inv", [P, NT, 1])
        gT = sb("gT", [NE, TOK])
        pb = sb("pb", [P, 2, TOK])
        ew = sb("ew", [P, 2, 2, NC, P])
        ed = sb("ed", [P, 3, D])
        ew_hi = sb("ew_hi", [P, 2, 2, NC, P], F32R)
        ew_lo = sb("ew_lo", [P, 2, 2, NC, P], F32R)
        gu = sb("gu", [P, 2, 2, HALF])
        e1_a = sb("e1_a", [P, 2, HALF])
        e1_b = sb("e1_b", [P, 2, HALF])
        h1 = sb("h1", [P, 2, HALF])
        f1T = sb("f1T", [P, NC, TOK])
        l1b.close()

        mix_a = ctx.enter_context(nc.sbuf_tensor("mix_a", [P, 2, D], F32, side="right"))
        mix_b = ctx.enter_context(nc.sbuf_tensor("mix_b", [P, 2, D], F32, side="right"))

        ps = ctx.enter_context(nc.psum_tensor("ps", [P, 8, HALF], F32))
        psf = ps[:, :, :].rearrange("p b n -> p (b n)")

        in_x, in_const, in_wqkv, in_l0c = sem("in_x"), sem("in_const"), sem("in_wqkv"), sem("in_l0c")
        in_wout, in_pk, in_l1c = sem("in_wout"), [sem("in_pk0"), sem("in_pk1")], sem("in_l1c")
        in_wqk, in_wo, in_wv = [sem("in_wqk0"), sem("in_wqk1")], [sem("in_wo0"), sem("in_wo1")], sem("in_wv")
        in_router = sem("in_router")
        in_ew = [sem("in_ew0"), sem("in_ew1")]
        in_pb = [sem("in_pb0"), sem("in_pb1")]
        vec = sem("vec")
        pool_step = sem("pool_step")
        act_step = sem("act_step")
        consts_ready = sem("consts_ready")
        var_ready, sd_ready, xn_ready = sem("var_ready"), sem("sd_ready"), sem("xn_ready")
        xT_ps, xT_hi_ready, xT_ready = sem("xT_ps"), sem("xT_hi_ready"), sem("xT_ready")
        wqkv_hi_ready, wqkv_ready = sem("wqkv_hi_ready"), sem("wqkv_ready")
        qkv_ps, qkv_read = sem("qkv_ps"), sem("qkv_read")
        hvar_ready, hsd_ready = sem("hvar_ready"), sem("hsd_ready")
        qk_ready, stk_hi, stk_ready, stk_ps, stk_read = (sem("qk_ready"), sem("stk_hi"), sem("stk_ready"),
                                                        sem("stk_ps"), sem("stk_read"))
        s0_ps, s0_sq, s0_four, s0_mask = sem("s0_ps"), sem("s0_sq"), sem("s0_four"), sem("s0_mask")
        o0_ps, o0_ready = sem("o0_ps"), sem("o0_ready")
        wout_hi_ready, wout_ready = sem("wout_hi_ready"), sem("wout_ready")
        oT_ps, oT_hi_ready, oT_ready = sem("oT_ps"), sem("oT_hi_ready"), sem("oT_ready")
        so_ps, so_read = sem("so_ps"), sem("so_read")
        nib_ready, relu_ready, w0_ready, w0_hi_ready, w0_lo_ready = (
            sem("nib_ready"), sem("relu_ready"), sem("w0_ready"), sem("w0_hi_ready"), sem("w0_lo_ready"))
        gu0_ps, g2_ready, inner_ready, th0_ready, h0_ready, dn0_ps = (
            sem("gu0_ps"), sem("g2_ready"), sem("inner_ready"), sem("th0_ready"), sem("h0_ready"), sem("dn0_ps"))
        fT_ready, f_ps, fth_ready, x_ready = sem("fT_ready"), sem("f_ps"), sem("fth_ready"), sem("x_ready")
        wv_hi_ready, wv_ready, v_ps, v_read = sem("wv_hi_ready"), sem("wv_ready"), sem("v_ps"), sem("v_read")
        wqk_hi_ready, wqk_ready = sem("wqk_hi_ready"), sem("wqk_ready")
        pj_ps, pj_swap, pj_rot, pj_hi, pj_ready = (sem("pj_ps"), sem("pj_swap"), sem("pj_rot"), sem("pj_hi"),
                                                  sem("pj_ready"))
        s1_ps, s1_bias, s1_exp, s1_mask = sem("s1_ps"), sem("s1_bias"), sem("s1_exp"), sem("s1_mask")
        c_ps, c_ready = sem("c_ps"), sem("c_ready")
        cT_ps, cT_hi_ready, cT_ready = sem("cT_ps"), sem("cT_hi_ready"), sem("cT_ready")
        wo_hi_ready, wo_ready = sem("wo_hi_ready"), sem("wo_ready")
        s_ps, s_added = sem("s_ps"), sem("s_added")
        rw_ready, lg_ps, lg_read, sp_a, sp_b, gates_ready = (sem("rw_ready"), sem("lg_ps"), sem("lg_read"),
                                                            sem("sp_a"), sem("sp_b"), sem("gates_ready"))
        gT_ps, gT_ready, gates_out = sem("gT_ps"), sem("gT_ready"), sem("gates_out")
        ew_hi_ready, ew_ready = sem("ew_hi_ready"), sem("ew_ready")
        gu1_ps, clip_ready, th1_ready, up_ready, h1_ready, dn1_ps = (
            sem("gu1_ps"), sem("clip_ready"), sem("th1_ready"), sem("up_ready"), sem("h1_ready"), sem("dn1_ps"))
        out_sent = sem("out_sent")

        block = ctx.enter_context(nc.Block())

        def expert_source(u):
            return eg_in[u], eu_in[u], ed_in[u]

        @block.sync
        def _(sp):
            sp.dma_start(x_tok[:], x_in.rearrange("(t p) d -> p t d", p=P)).then_inc(in_x, 16)
            sp.dma_start(ident[:], ident_in).then_inc(in_const, 16)
            sp.dma_start(wqkv, wqkv_in.rearrange("(p c) n -> p c n", c=NC)).then_inc(in_wqkv, 16)
            sp.dma_start(rope0[:], rope0_in).then_inc(in_l0c, 16)
            sp.dma_start(lns[:, 0, :], lns_in.rearrange("(a n) -> a n", a=1).to_broadcast((P, D0))).then_inc(in_l0c, 16)
            sp.dma_start(lns[:, 1, :], lnb_in.rearrange("(a n) -> a n", a=1).to_broadcast((P, D0))).then_inc(in_l0c, 16)
            sp.wait_ge(o0_ready, H0)
            sp.dma_start(wout[:], wout_in.rearrange("(c p) n -> p c n", p=P)).then_inc(in_wout, 16)
            for J in range(NJ):
                if J >= 2:
                    sp.wait_ge(w0_ready, J - 1)
                b = J % 2
                sp.dma_start(pk[:, b, 0, :], gp_in[:, J, :]).then_inc(in_pk[b], 16)
                sp.dma_start(pk[:, b, 1, :], up_in[:, J, :]).then_inc(in_pk[b], 16)
                sp.dma_start(pk[:, b, 2, :], dp_in[J]).then_inc(in_pk[b], 16)
                per = P // (D // BLK)
                for q in range(D // BLK):
                    rows = slice(q * per, (q + 1) * per)
                    sp.dma_start(pks[rows, b, 0, :], gs_in[q:q + 1, J, :].to_broadcast((per, 2 * P))).then_inc(in_pk[b], 16)
                    sp.dma_start(pks[rows, b, 1, :], us_in[q:q + 1, J, :].to_broadcast((per, 2 * P))).then_inc(in_pk[b], 16)
                    sp.dma_start(pks[rows, b, 2, :], ds_in[J, q:q + 1, :].to_broadcast((per, D))).then_inc(in_pk[b], 16)
            sp.wait_ge(x_ready, NT)
            sp.dma_start(wv, wv_in.rearrange("(p c) n -> p c n", c=NC)).then_inc(in_wv, 16)
            sp.dma_start(cos1[:], cos1_in).then_inc(in_l1c, 16)
            sp.dma_start(sin1[:], sin1_in).then_inc(in_l1c, 16)
            sp.dma_start(dist[:], dist_in).then_inc(in_l1c, 16)
            sp.dma_start(bo[:], bo_in.rearrange("(a n) -> a n", a=1).to_broadcast((P, D))).then_inc(in_l1c, 16)
            for n, (kind, i) in enumerate(PROJ):
                if n >= 2:
                    sp.wait_ge(wqk_ready, n - 1)
                src = (wq_in if kind == "q" else wk_in)[:, i * D1:(i + 1) * D1]
                sp.dma_start(wqk[:, n % 2], src.rearrange("(p c) n -> p c n", c=NC)).then_inc(in_wqk[n % 2], 16)
                if kind == "q" and i % PAIR == 0:
                    m = i // PAIR
                    if m >= 2:
                        sp.wait_ge(wo_ready, m - 1)
                    sp.dma_start(wo[:, m % 2], wo_in[i * D1:(i + PAIR) * D1, :].rearrange("(h p) n -> p h n", p=P))\
                        .then_inc(in_wo[m % 2], 16)
            sp.wait_ge(s_added, (H1 // PAIR) * NT)
            sp.dma_start(rw[:], rw_in).then_inc(in_router, 16)
            sp.dma_start(ebias[:], eb_in.rearrange("(a n) -> a n", a=1).to_broadcast((P, NE))).then_inc(in_router, 16)
            sp.dma_start(iota[:], iota_in).then_inc(in_router, 16)
            for u in range(U1):
                if u >= 2:
                    sp.wait_ge(ew_ready, u - 1)
                if u >= 3:
                    sp.wait_ge(dn1_ps, 2 * (u - 2))
                g, up, dn = expert_source(u)
                sp.dma_start(ew[:, u % 2, 0], g.rearrange("(p c) n -> p c n", c=NC)).then_inc(in_ew[u % 2], 16)
                sp.dma_start(ew[:, u % 2, 1], up.rearrange("(p c) n -> p c n", c=NC)).then_inc(in_ew[u % 2], 16)
                sp.dma_start(ed[:, u % 3], dn).then_inc(in_ew[u % 2], 16)
                if u == 0:
                    sp.wait_ge(gT_ready, 1)
                    sp.dma_start(gates_dram, gT[:]).then_inc(gates_out, 16)
                    sp.wait_ge(gates_out, 16)
                if u < NE:
                    if u >= 2:
                        sp.wait_ge(up_ready, 2 * (u - 1))
                    sp.dma_start(pb[:, u % 2], gates_dram[u:u + 1, :].to_broadcast((P, TOK))).then_inc(in_pb[u % 2], 16)
            for t in range(NT):
                sp.wait_ge(x_ready, NT + t + 1)
                sp.dma_start(out[0, t * P:(t + 1) * P, :], x_tok[:, t, :]).then_inc(out_sent, 16)
            sp.wait_ge(out_sent, 16 * NT)


        @block.tensor
        def _(pe):
            def mm3(o, l_hi, l_lo, r_hi, r_lo, start, stop):
                pe.matmul(o, l_hi, r_hi, start=start, stop=False)
                pe.matmul(o, l_lo, r_hi, start=False, stop=False)
                return pe.matmul(o, l_hi, r_lo, start=False, stop=stop)

            def transpose_x(layer):
                for k in range(2 * NHALF):
                    half, c = k // NC, k % NC
                    pe.wait_ge(xn_ready, NT * layer + 4 * (half + 1))
                    for i in range(4):
                        t = 4 * half + i
                        last = pe.transpose(ps[:, k, i * P:(i + 1) * P], xn_tok[:, t, c::NC], ident[:])
                    last.then_inc(xT_ps, 1)

            def qkv0():
                pe.wait_ge(wqkv_ready, 1)
                for t in range(NT):
                    pe.wait_ge(xT_ready, 2 * (t // 4 + 1))
                    if t >= 2:
                        pe.wait_ge(qkv_read, t - 1)
                    b = 4 + 2 * (t % 2)
                    tk = slice(t * P, (t + 1) * P)
                    for o, cols in ((ps[:, b, :], slice(0, 2 * D)), (ps[:, b + 1, 0:D], slice(2 * D, 3 * D))):
                        for c in range(NC):
                            last = mm3(o, xT_hi[:, c, tk], xT_lo[:, c, tk], wqkv_hi[:, c, cols], wqkv_lo[:, c, cols],
                                       c == 0, c == NC - 1)
                    last.then_inc(qkv_ps, 1)
                pe.wait_ge(xT_ready, 2 * NC)
                for t in range(NT):
                    pe.wait_ge(stk_ready, t + 1)
                    for q in range(4):
                        n = 4 * t + q
                        if n >= 4:
                            pe.wait_ge(stk_read, n - 3)
                        for i in range(4):
                            h = 2 * (4 * (q % 2) + i)
                            src = stack[:, t % 2, q // 2, h:h + 2].rearrange("p h a d -> p (h a d)")
                            last = pe.transpose(ps[:, q, i * P:(i + 1) * P], src, ident[:])
                        last.then_inc(stk_ps, 1)

            def scores0(h, j):
                n = h * NT + j
                if n == 0:
                    pe.wait_ge(stk_read, 4 * NT)
                if n >= 3:
                    pe.wait_ge(s0_sq, n - 2)
                rows = slice(64 * (h % 2), 64 * (h % 2) + STK)
                o = 1024 * (n % 3)
                for a, e in spans((NT - j) * P):
                    last = pe.matmul(psf[:, o + a:o + e], KT[rows, h // 2, j * P:(j + 1) * P],
                                     QT[rows, h // 2, j * P + a:j * P + e], start=True, stop=True)
                last.then_inc(s0_ps, 1)

            def out0(h, t):
                if t == 0 and h >= 2:
                    pe.wait_ge(o0_ready, h - 1)
                pe.wait_ge(s0_mask, h * NT + t + 1)
                for j in range(t + 1):
                    a = OFF[j] + (t - j) * P
                    last = pe.matmul(ps[:, 6 + h % 2, 32 * t:32 * t + D0 + 1], A0[:, h % 2, a:a + P],
                                     V0[:, j, h, :], start=(j == 0), stop=(j == t))
                if t == NT - 1:
                    last.then_inc(o0_ps, 1)

            def project_out0():
                pe.wait_ge(o0_ready, H0)
                for k in range(2 * NHALF):
                    half, c = k // NC, k % NC
                    for i in range(4):
                        last = pe.transpose(ps[:, k, i * P:(i + 1) * P], o_tok[:, 4 * half + i, c * P:(c + 1) * P],
                                            ident[:])
                    last.then_inc(oT_ps, 1)
                pe.wait_ge(oT_ready, 2 * NC)
                pe.wait_ge(wout_ready, 1)
                for t in range(NT):
                    if t >= 2:
                        pe.wait_ge(so_read, t - 1)
                    tk = slice(t * P, (t + 1) * P)
                    for c in range(NC):
                        last = mm3(ps[:, 4 + t % 2, 0:D], oT_hi[:, c, tk], oT_lo[:, c, tk], wout_hi[:, c], wout_lo[:, c],
                                   c == 0, c == NC - 1)
                    last.then_inc(so_ps, 1)

            def unit(s, n_units, w_hi, w_lo, w_dn, ready, used, gu_done, h_ready, h, dn_done):
                if s < 2 * n_units:
                    u, half = s // 2, s % 2
                    ready(u)
                    used(s)
                    tk = slice(half * HALF, (half + 1) * HALF)
                    for m in range(2):
                        for c in range(NC):
                            last = mm3(ps[:, 2 * (s % 2) + m, :], w_hi(u, m, c), w_lo(u, m, c), xT_hi[:, c, tk],
                                       xT_lo[:, c, tk], c == 0, c == NC - 1)
                    last.then_inc(gu_done, 1)
                if s >= 1:
                    s -= 1
                    u, half = s // 2, s % 2
                    pe.wait_ge(h_ready, s + 1)
                    for c in range(NC):
                        last = pe.matmul(ps[:, 4 + 2 * c + half, :], w_dn(u, c), h[:, s % 2, :], start=(u == 0),
                                         stop=(u == n_units - 1))
                    last.then_inc(dn_done, 1)

            def turn_f(layer, fT):
                pe.wait_ge(fT_ready, 2 * NC * (layer + 1))
                for t in range(NT):
                    if t >= 2:
                        pe.wait_ge(x_ready, NT * layer + t - 1)
                    for c in range(NC):
                        last = pe.transpose(ps[:, t % 2, c * P:(c + 1) * P], fT[:, c, t * P:(t + 1) * P], ident[:])
                    last.then_inc(f_ps, 1)

            pe.wait_ge(in_const, 16)
            transpose_x(0)
            qkv0()
            for h in range(H0 + 1):
                for j in range(NT):
                    if h < H0:
                        scores0(h, j)
                    if h >= 1:
                        out0(h - 1, j)
            project_out0()

            def ready0(u):
                pe.wait_ge(w0_lo_ready, u // 2 + 1)

            def used0(s):
                if s == 0:
                    pe.wait_ge(so_read, NT)
                if s >= 2:
                    pe.wait_ge(h0_ready, s - 1)

            for s in range(2 * U0 + 1):
                unit(s, U0, lambda u, m, c: w0_hi[:, (u // 2) % 2, m, c, (u % 2) * P:(u % 2 + 1) * P],
                     lambda u, m, c: w0_lo[:, (u // 2) % 2, m, c, (u % 2) * P:(u % 2 + 1) * P],
                     lambda u, c: w0[:, (u // 2) % 2, 2, u % 2, c * P:(c + 1) * P],
                     ready0, used0, gu0_ps, h0_ready, h0, dn0_ps)
            turn_f(0, f0T)

            pe.wait_ge(x_ready, NT)
            transpose_x(1)
            pe.wait_ge(xT_ready, 4 * NC)
            pe.wait_ge(wv_ready, 1)
            for t in range(NT):
                if t >= 2:
                    pe.wait_ge(v_read, t - 1)
                tk = slice(t * P, (t + 1) * P)
                for c in range(NC):
                    last = mm3(ps[:, 4 + t % 2, :], xT_hi[:, c, tk], xT_lo[:, c, tk], wv_hi[:, c], wv_lo[:, c],
                               c == 0, c == NC - 1)
                last.then_inc(v_ps, 1)
            pe.wait_ge(v_read, NT)

            def side_slot():
                n = side[0]
                side[0] += 1
                if n >= 2:
                    name, count = side_read(SIDE[n - 2])
                    pe.wait_ge({"pj_rot": pj_rot, "cT_ready": cT_ready, "s_added": s_added}[name], count)
                return ps[:, 6 + n % 2, :]
            side = [0]

            def project(n, half):
                pe.wait_ge(wqk_ready, n + 1)
                o = side_slot()
                tk = slice(half * HALF, (half + 1) * HALF)
                for c in range(NC):
                    last = mm3(o, wqk_hi[:, n % 2, c], wqk_lo[:, n % 2, c], xT_hi[:, c, tk], xT_lo[:, c, tk],
                               c == 0, c == NC - 1)
                last.then_inc(pj_ps, 1)

            def scores1(h, j):
                n = h * NT + j
                if j == 0:
                    pe.wait_ge(pj_ready, 2 * (PROJ.index(("q", h)) + 1))
                if n >= 2:
                    pe.wait_ge(s1_bias, n - 1)
                g = h // REP
                o = 1024 * (n % 2)
                kk = slice(j * P, (j + 1) * P)
                for a, e in spans((NT - j) * P):
                    qq = slice(j * P + a, j * P + e)
                    last = mm3(psf[:, o + a:o + e], k_hi[:, g % 2, kk], k_lo[:, g % 2, kk], q_hi[:, h % 2, qq],
                               q_lo[:, h % 2, qq], True, True)
                last.then_inc(s1_ps, 1)

            def context(h, t):
                r = 3 * h + t // 3
                if t % 3 == 0 and r >= 2:
                    pe.wait_ge(c_ready, r - 1)
                pe.wait_ge(s1_mask, h * NT + t + 1)
                o = (D1 + 1) * (t % 3)
                for j in range(t + 1):
                    a = OFF[j] + (t - j) * P
                    last = pe.matmul(ps[:, 4 + r % 2, o:o + D1 + 1], P1[:, h % 2, a:a + P], V1[:, j, h // REP, :],
                                     start=(j == 0), stop=(j == t))
                if t % 3 == 2 or t == NT - 1:
                    last.then_inc(c_ps, 1)

            def turn_context(h, half):
                pe.wait_ge(c_ready, 3 * h + (2 if half == 0 else 3))
                o = side_slot()
                for i in range(4):
                    last = pe.transpose(o[:, i * P:(i + 1) * P], ctx_tok[:, h % 2, 4 * half + i, :], ident[:])
                last.then_inc(cT_ps, 1)

            def project_out1(m, t):
                if t == 0:
                    pe.wait_ge(cT_ready, 2 * PAIR * (m + 1))
                    pe.wait_ge(wo_ready, m + 1)
                o = side_slot()
                tk = slice(t * P, (t + 1) * P)
                for i in range(PAIR):
                    last = mm3(o[:, 0:D], cT_hi[:, i, tk], cT_lo[:, i, tk], wo_hi[:, i], wo_lo[:, i], i == 0, i == PAIR - 1)
                last.then_inc(s_ps, 1)

            for step in STEPS1:
                {"project": project, "scores": scores1, "context": context, "turn": turn_context,
                 "out": project_out1}[step[0]](*step[1:])

            pe.wait_ge(s_added, (H1 // PAIR) * NT)
            pe.wait_ge(rw_ready, 1)
            for t in range(NT):
                tk = slice(t * P, (t + 1) * P)
                for c in range(NC):
                    last = mm3(ps[:, 0, t * NE:(t + 1) * NE], xT_hi[:, c, tk], xT_lo[:, c, tk], rw_hi[:, c], rw_lo[:, c],
                               c == 0, c == NC - 1)
            last.then_inc(lg_ps, 1)
            pe.wait_ge(gates_ready, 1)
            for t in range(NT):
                last = pe.transpose(ps[0:NE, 1 + t // 4, (t % 4) * P:(t % 4 + 1) * P], r_d[:, t, :], ident[:])
            last.then_inc(gT_ps, 1)

            def ready1(u):
                pe.wait_ge(ew_ready, u + 1)

            def used1(s):
                if s == 0:
                    pe.wait_ge(gT_ready, 1)
                if s >= 2:
                    pe.wait_ge(clip_ready, s - 1)

            for s in range(2 * U1 + 1):
                unit(s, U1, lambda u, m, c: ew_hi[:, u % 2, m, c], lambda u, m, c: ew_lo[:, u % 2, m, c],
                     lambda u, c: ed[:, u % 3, c * P:(c + 1) * P], ready1, used1, gu1_ps, h1_ready, h1, dn1_ps)
            turn_f(1, f1T)

        @block.scalar
        def _(act):
            def layernorm(layer):
                act.wait_ge(var_ready, layer + 1)
                act.activation(ln_sd[:], ln_var[:], ACT.Sqrt).then_inc(sd_ready, 1)
                for k in range(2 * NHALF):
                    half, c = k // NC, k % NC
                    act.wait_ge(xT_ps, 4 * layer + k + 1)
                    act.activation(xT_hi[:, c, half * HALF:(half + 1) * HALF], ps[:, k, :], ACT.Copy)\
                        .then_inc(xT_hi_ready, 1)

            def turn_f(layer, n_dn, dn_done, fT):
                act.wait_ge(dn_done, n_dn)
                for c in range(NC):
                    for half in range(NHALF):
                        act.activation(fT[:, c, half * HALF:(half + 1) * HALF], ps[:, 4 + 2 * c + half, :], ACT.Copy)\
                            .then_inc(fT_ready, 1)
                for t in range(NT):
                    act.wait_ge(f_ps, NT * layer + t + 1)
                    if t >= 2:
                        act.wait_ge(x_ready, NT * layer + t - 1)
                    act.activation(mix_a[:, t % 2, :], ps[:, t % 2, 0:D], ACT.Tanh, scale=0.5).then_inc(fth_ready, 1)

            act.wait_ge(in_wqkv, 16)
            act.activation(wqkv_hi[:], wqkv, ACT.Copy).then_inc(wqkv_hi_ready, 1)
            layernorm(0)
            act.wait_ge(hvar_ready, 1)
            act.activation(hsd[:], hv[:], ACT.Sqrt).then_inc(hsd_ready, 1)

            def evacuate_stack(n):
                t, q = n // 4, n % 4
                act.wait_ge(stk_ps, n + 1)
                dst = (QT, KT)[q // 2][:, 4 * (q % 2):4 * (q % 2) + 4, t * P:(t + 1) * P]
                act.activation(dst, ps[:, q, :].rearrange("p (i n) -> p i n", i=4), ACT.Copy).then_inc(stk_read, 1)

            for t in range(NT + 1):
                if t < NT:
                    act.wait_ge(qk_ready, t + 1)
                    if t >= 2:
                        act.wait_ge(stk_ps, 4 * (t - 1))
                    for m, places in ((0, slice(0, 4, 2)), (1, slice(0, 2))):
                        src = qk_tok[:, t, m * D:(m + 1) * D].rearrange("p (h a d) -> p h a d", h=H0, a=1)
                        last = act.activation(stack[:, t % 2, m, :, places, :].bitcast(F32R),
                                              src.to_broadcast((P, H0, 2, D0)), ACT.Copy)
                        last.then_inc(stk_hi, 1)
                if t >= 1:
                    for q in range(4):
                        evacuate_stack(4 * (t - 1) + q)
            for h in range(H0):
                for j in range(NT):
                    n = h * NT + j
                    act.wait_ge(s0_ps, n + 1)
                    if j == 0 and h >= 2:
                        act.wait_ge(o0_ps, h - 1)
                    if n == 0:
                        act.wait_ge(stk_ready, NT)
                    w = (NT - j) * P
                    act.activation(A0[:, h % 2, OFF[j]:OFF[j] + w], psf[:, 1024 * (n % 3):1024 * (n % 3) + w],
                                   ACT.Square).then_inc(s0_sq, 1)
            for k in range(2 * NHALF):
                half, c = k // NC, k % NC
                act.wait_ge(oT_ps, k + 1)
                act.activation(oT_hi[:, c, half * HALF:(half + 1) * HALF], ps[:, k, :], ACT.Copy).then_inc(oT_hi_ready, 1)
            act.wait_ge(in_wout, 16)
            act.activation(wout_hi[:], wout[:], ACT.Copy).then_inc(wout_hi_ready, 1)
            for t in range(NT):
                act.wait_ge(so_ps, t + 1)
                act.activation(s_tok[:, t, :], ps[:, 4 + t % 2, 0:D], ACT.Copy).then_inc(so_read, 1)

            def relus(J):
                act.wait_ge(nib_ready, J + 1)
                if J >= 1:
                    act.wait_ge(w0_ready, J)
                act.activation(dq_a[:], mag[:], ACT.Relu, bias=consts[:, 0:1]).then_inc(relu_ready, 1)
                act.activation(dq_b[:], mag[:], ACT.Relu, bias=consts[:, 1:2], scale=2.0).then_inc(relu_ready, 1)
                act.activation(dq_m[:], mag[:], ACT.Copy).then_inc(relu_ready, 1)
                act.activation(dq_s[:], sgn[:], ACT.Identity, bias=consts[:, 2:3], scale=-0.125).then_inc(relu_ready, 1)

            def high0(J):
                act.wait_ge(w0_ready, J + 1)
                if J >= 2:
                    act.wait_ge(gu0_ps, 4 * (J - 1))
                act.activation(w0_hi[:, J % 2], w0[:, J % 2, 0:2], ACT.Copy).then_inc(w0_hi_ready, 1)

            act.wait_ge(consts_ready, 1)
            relus(0)
            high0(0)
            relus(1)
            high0(1)
            for s in range(2 * U0 + 1):
                if s < 2 * U0:
                    act.wait_ge(gu0_ps, s + 1)
                    if s >= 2:
                        act.wait_ge(inner_ready, s - 1)
                    act.activation(e0_a[:, s % 2, :], ps[:, 2 * (s % 2), :], ACT.Square).then_inc(g2_ready, 1)
                if s >= 1:
                    r = s - 1
                    act.wait_ge(inner_ready, r + 1)
                    act.activation(e0_b[:, r % 2, :], e0_b[:, r % 2, :], ACT.Tanh, scale=GELU_C * GELU_K)\
                        .then_inc(th0_ready, 1)
                if s % 4 == 2 and s // 4 + 2 < NJ:
                    relus(s // 4 + 2)
                if s % 4 == 1 and 2 <= s // 4 + 1 < NJ:
                    high0(s // 4 + 1)
            turn_f(0, 2 * U0, dn0_ps, f0T)

            layernorm(1)
            act.wait_ge(in_wv, 16)
            act.activation(wv_hi[:], wv, ACT.Copy).then_inc(wv_hi_ready, 1)

            def split_wqk(n):
                act.wait_ge(in_wqk[n % 2], 16 * (n // 2 + 1))
                if n >= 2:
                    act.wait_ge(pj_ps, 2 * (n - 1))
                act.activation(wqk_hi[:, n % 2], wqk[:, n % 2], ACT.Copy).then_inc(wqk_hi_ready, 1)

            def split_wo(m):
                act.wait_ge(in_wo[m % 2], 16 * (m // 2 + 1))
                if m >= 1:
                    act.wait_ge(s_ps, NT * m)
                act.activation(wo_hi[:], wo[:, m % 2], ACT.Copy).then_inc(wo_hi_ready, 1)

            def project(n, half):
                i = 2 * n + half
                act.wait_ge(pj_ps, i + 1)
                if i >= 1:
                    act.wait_ge(pj_rot, i)
                b = ps[:, 6 + side_of["project", n, half] % 2, :]
                act.activation(swap[0:64, :], b[64:128, :], ACT.Copy).then_inc(pj_swap, 1)
                act.activation(swap[64:128, :], b[0:64, :], ACT.Copy).then_inc(pj_swap, 1)
                act.wait_ge(pj_rot, i + 1)
                kind, hd = PROJ[n]
                if kind == "q" and hd >= 2:
                    act.wait_ge(s1_ps, NT * (hd - 1))
                if kind == "k" and hd >= 2:
                    act.wait_ge(s1_ps, NT * REP * (hd - 1))
                dst = (q_hi if kind == "q" else k_hi)[:, hd % 2, half * HALF:(half + 1) * HALF]
                act.activation(dst, rot[:], ACT.Copy).then_inc(pj_hi, 1)

            def scores(h, j):
                n = h * NT + j
                w = (NT - j) * P
                act.wait_ge(s1_bias, n + 1)
                act.activation(cap[:, n % 2, 0:w], cap[:, n % 2, 0:w], ACT.Tanh, scale=1.0 / (CAP * float(D1) ** 0.5))\
                    .then_inc(act_step, 1)
                act.wait_ge(act_step, n + 1)
                if j == 0 and h >= 2:
                    act.wait_ge(c_ps, 3 * (h - 1))
                act.activation(P1[:, h % 2, OFF[j]:OFF[j] + w], cap[:, n % 2, 0:w], ACT.Exp, scale=CAP)\
                    .then_inc(s1_exp, 1)

            def turn(h, half):
                act.wait_ge(cT_ps, 2 * h + half + 1)
                if h >= PAIR:
                    act.wait_ge(s_ps, NT * (h // PAIR))
                act.activation(cT_hi[:, h % PAIR, half * HALF:(half + 1) * HALF],
                               ps[:, 6 + side_of["turn", h, half] % 2, :], ACT.Copy).then_inc(cT_hi_ready, 1)

            act.wait_ge(in_l1c, 64)
            for step in ACT_STEPS1:
                {"project": project, "scores": scores, "turn": turn, "split_wqk": split_wqk,
                 "split_wo": split_wo}[step[0]](*step[1:])

            act.wait_ge(in_router, 48)
            act.activation(rw_hi[:], rw[:], ACT.Copy).then_inc(act_step, 1)
            act.wait_ge(lg_read, 1)
            act.activation(r_b[:], r_a[:], ACT.Exp, scale=-1.0).then_inc(sp_a, 1)
            act.wait_ge(sp_b, 1)
            act.activation(r_d[:], r_c[:], ACT.Ln).then_inc(sp_a, 1)
            act.wait_ge(sp_b, 2)
            act.activation(r_b[:], r_a[:], ACT.Sqrt).then_inc(sp_a, 1)

            def split_ew(u):
                act.wait_ge(in_ew[u % 2], 48 * (u // 2 + 1))
                if u >= 2:
                    act.wait_ge(gu1_ps, 2 * (u - 1))
                act.activation(ew_hi[:, u % 2], ew[:, u % 2], ACT.Copy).then_inc(ew_hi_ready, 1)

            split_ew(0)
            split_ew(1)
            for s in range(2 * U1):
                act.wait_ge(clip_ready, s + 1)
                if s >= 2:
                    act.wait_ge(h1_ready, s - 1)
                act.activation(e1_a[:, s % 2, :], gu[:, s % 2, 0, :], ACT.Tanh, scale=0.5).then_inc(th1_ready, 1)
                if s % 2 == 1 and s // 2 + 2 < U1:
                    split_ew(s // 2 + 2)
            turn_f(1, 2 * U1, dn1_ps, f1T)

        @block.vector
        def _(dve):
            steps = [0]

            def link(ins):
                steps[0] += 1
                ins.then_inc(vec, 1)
                dve.wait_ge(vec, steps[0])

            def rsqrt(sd, var, r, t):
                link(dve.reciprocal(r, sd))
                link(dve.tensor_tensor(t, r, r, ALU.mult))
                link(dve.tensor_tensor(t, t, var, ALU.mult))
                link(dve.tensor_scalar(t, t, -0.5, 1.5, ALU.mult, ALU.add))
                link(dve.tensor_tensor(r, r, t, ALU.mult))

            def layernorm(layer):
                for t in range(NT):
                    link(dve.bn_stats(ln_stats[:], x_tok[:, t, :]))
                    link(dve.bn_aggr(ln_mv[:, t, :], ln_stats[:]))
                dve.tensor_scalar(ln_var[:], ln_mv[:, :, 1], LN_EPS, None, ALU.add).then_inc(var_ready, 1)
                dve.wait_ge(sd_ready, layer + 1)
                rsqrt(ln_sd[:], ln_var[:], ln_r[:], ln_t[:])
                for t in range(NT):
                    dve.tensor_scalar(xn_tok[:, t, :], x_tok[:, t, :], ln_mv[:, t, 0:1], ln_r[:, t:t + 1],
                                      ALU.subtract, ALU.mult).then_inc(xn_ready, 1)
                for k in range(2 * NHALF):
                    half, c = k // NC, k % NC
                    dve.wait_ge(xT_hi_ready, 4 * layer + k + 1)
                    tk = slice(half * HALF, (half + 1) * HALF)
                    dve.tensor_tensor(xT_lo[:, c, tk], ps[:, k, :], xT_hi[:, c, tk].bitcast(F32), ALU.subtract)\
                        .then_inc(xT_ready, 1)

            def combine(layer):
                for t in range(NT):
                    dve.wait_ge(fth_ready, NT * layer + t + 1)
                    b = t % 2
                    link(dve.scalar_tensor_tensor(out=mix_b[:, b, :], in0=mix_a[:, b, :], scalar=1.0,
                                                  in1=ps[:, b, 0:D], op0=ALU.add, op1=ALU.mult))
                    link(dve.scalar_tensor_tensor(out=mix_b[:, b, :], in0=mix_b[:, b, :], scalar=0.5,
                                                  in1=s_tok[:, t, :], op0=ALU.mult, op1=ALU.mult))
                    dve.tensor_tensor(x_tok[:, t, :], x_tok[:, t, :], mix_b[:, b, :], ALU.add).then_inc(x_ready, 1)

            for i, v in enumerate((-4.0, -12.0, 0.5, 0.0)):
                last = dve.memset(consts[:, i:i + 1], v)
            last.then_inc(consts_ready, 1)
            dve.memset(V0[:, :, :, D0:D0 + 1], 1.0)
            dve.wait_ge(wqkv_hi_ready, 1)
            dve.tensor_tensor(wqkv_lo[:], wqkv, wqkv_hi[:].bitcast(F32), ALU.subtract).then_inc(wqkv_ready, 1)
            dve.wait_ge(in_x, 16)
            layernorm(0)

            dve.wait_ge(in_l0c, 48)
            hd = dict(h=2 * H0)
            for t in range(NT):
                dve.wait_ge(qkv_ps, t + 1)
                b = 4 + 2 * (t % 2)
                pq = ps[:, b, :].rearrange("p (h d) -> p h d", **hd)
                ra = rope_a[:].rearrange("p (h d) -> p h d", **hd)
                rb = rope_b[:].rearrange("p (h d) -> p h d", **hd)
                qd = qk_tok[:, t, :].rearrange("p (h d) -> p h d", **hd)
                hf = D0 // 2
                cs = rope0[:, t, 0:1, :].to_broadcast((P, 2 * H0, D0))
                dve.tensor_tensor(ra, pq, cs, ALU.mult)
                dve.tensor_tensor(rb[:, :, 0:hf], pq[:, :, hf:], rope0[:, t, 1:2, 0:hf].to_broadcast((P, 2 * H0, hf)),
                                  ALU.mult)
                link(dve.tensor_tensor(rb[:, :, hf:], pq[:, :, 0:hf],
                                       rope0[:, t, 1:2, hf:].to_broadcast((P, 2 * H0, hf)), ALU.mult))
                dve.tensor_copy(V0[:, t, :, 0:D0], ps[:, b + 1, 0:D].rearrange("p (h d) -> p h d", h=H0))\
                    .then_inc(qkv_read, 1)
                link(dve.tensor_tensor(ra, ra, rb, ALU.add))
                link(dve.tensor_reduce(hm[:, 0, :], ra, AX_X, ALU.add))
                link(dve.tensor_scalar(hm[:, 1, :], hm[:, 0, :], 1.0 / D0, None, ALU.mult))
                mean = hm[:, 1, :].rearrange("p (h a) -> p h a", a=1).to_broadcast((P, 2 * H0, D0))
                link(dve.tensor_tensor(qd, ra, mean, ALU.subtract))
                link(dve.tensor_tensor(rb, qd, qd, ALU.mult))
                link(dve.tensor_reduce(hv[:, t, :], rb, AX_X, ALU.add))
            dve.tensor_scalar(hv[:], hv[:], 1.0 / D0, LN_EPS, ALU.mult, ALU.add).then_inc(hvar_ready, 1)
            dve.wait_ge(hsd_ready, 1)
            rsqrt(hsd[:], hv[:], hr[:], ht[:])
            for t in range(NT):
                qd = qk_tok[:, t, :].rearrange("p (h d) -> p h d", **hd)
                rs = hr[:, t, :].rearrange("p (h a) -> p h a", a=1).to_broadcast((P, 2 * H0, D0))
                link(dve.tensor_tensor(qd, qd, rs, ALU.mult))
                link(dve.tensor_tensor(qd, qd, lns[:, 0:1, :].to_broadcast((P, 2 * H0, D0)), ALU.mult))
                dve.tensor_tensor(qd, qd, lns[:, 1:2, :].to_broadcast((P, 2 * H0, D0)), ALU.add).then_inc(qk_ready, 1)
                dve.wait_ge(qk_ready, t + 1)
                for m, hi, lo in ((0, slice(0, 4, 2), slice(1, 4, 2)), (1, slice(0, 2), slice(2, 4))):
                    dve.wait_ge(stk_hi, 2 * t + m + 1)
                    src = qk_tok[:, t, m * D:(m + 1) * D].rearrange("p (h a d) -> p h a d", h=H0, a=1)
                    last = dve.tensor_tensor(stack[:, t % 2, m, :, lo, :].bitcast(F32R),
                                             src.to_broadcast((P, H0, 2, D0)), stack[:, t % 2, m, :, hi, :],
                                             ALU.subtract)
                last.then_inc(stk_ready, 1)

            def read_out0(h):
                dve.wait_ge(o0_ps, h + 1)
                o = ps[:, 6 + h % 2, 0:32 * NT].rearrange("p (t d) -> p t d", d=32)
                link(dve.reciprocal(o_rden[:], o[:, :, D0:D0 + 1]))
                dve.tensor_tensor(o_tok[:, :, h * D0:(h + 1) * D0], o[:, :, 0:D0], o_rden[:].to_broadcast((P, NT, D0)),
                                  ALU.mult).then_inc(o0_ready, 1)

            for h in range(H0):
                for j in range(NT):
                    n = h * NT + j
                    dve.wait_ge(s0_sq, n + 1)
                    a = A0[:, h % 2, OFF[j]:OFF[j + 1]]
                    dve.tensor_tensor(a, a, a, ALU.mult).then_inc(s0_four, 1)
                    if h >= 1 and j == 4:
                        read_out0(h - 1)
            read_out0(H0 - 1)
            for k in range(2 * NHALF):
                half, c = k // NC, k % NC
                tk = slice(half * HALF, (half + 1) * HALF)
                dve.wait_ge(oT_hi_ready, k + 1)
                dve.tensor_tensor(oT_lo[:, c, tk], ps[:, k, :], oT_hi[:, c, tk].bitcast(F32), ALU.subtract)\
                    .then_inc(oT_ready, 1)
            dve.wait_ge(wout_hi_ready, 1)
            dve.tensor_tensor(wout_lo[:], wout[:], wout_hi[:].bitcast(F32), ALU.subtract).then_inc(wout_ready, 1)

            def nibbles(J):
                dve.wait_ge(in_pk[J % 2], 16 * (3 + 3 * (D // BLK)) * (J // 2 + 1))
                if J >= 1:
                    dve.wait_ge(w0_ready, J)
                src = pk[:, J % 2]
                for i, sh in enumerate((0, 4)):
                    dve.tensor_scalar(mag[:, :, i, :], src, sh, 7, ALU.logical_shift_right, ALU.bitwise_and)
                    last = dve.tensor_scalar(sgn[:, :, i, :], src, sh, 8, ALU.logical_shift_right, ALU.bitwise_and)
                last.then_inc(nib_ready, 1)

            nibbles(0)
            nibbles(1)
            for s in range(2 * U0):
                b = s % 2
                g, up = ps[:, 2 * b, :], ps[:, 2 * b + 1, :]
                dve.wait_ge(g2_ready, s + 1)
                dve.scalar_tensor_tensor(out=e0_b[:, b, :], in0=e0_a[:, b, :], scalar=1.0 / GELU_K, in1=g,
                                         op0=ALU.add, op1=ALU.mult).then_inc(inner_ready, 1)
                dve.wait_ge(th0_ready, s + 1)
                link(dve.scalar_tensor_tensor(out=e0_b[:, b, :], in0=e0_b[:, b, :], scalar=1.0, in1=g,
                                              op0=ALU.add, op1=ALU.mult))
                if s >= 2:
                    dve.wait_ge(dn0_ps, s - 1)
                dve.scalar_tensor_tensor(out=h0[:, b, :], in0=e0_b[:, b, :], scalar=0.5, in1=up,
                                         op0=ALU.mult, op1=ALU.mult).then_inc(h0_ready, 1)
                if s % 4 == 1 and s // 4 + 2 < NJ:
                    nibbles(s // 4 + 2)
            combine(0)

            dve.wait_ge(x_ready, NT)
            layernorm(1)
            dve.memset(V1[:, :, :, D1:D1 + 1], 1.0)
            dve.wait_ge(wv_hi_ready, 1)
            dve.tensor_tensor(wv_lo[:], wv, wv_hi[:].bitcast(F32), ALU.subtract).then_inc(wv_ready, 1)
            for t in range(NT):
                dve.wait_ge(v_ps, t + 1)
                dve.tensor_copy(V1[:, t, :, 0:D1], ps[:, 4 + t % 2, :].rearrange("p (g d) -> p g d", g=G1))\
                    .then_inc(v_read, 1)
            dve.wait_ge(in_l1c, 64)

            def split_wqk(n):
                dve.wait_ge(wqk_hi_ready, n + 1)
                dve.tensor_tensor(wqk_lo[:, n % 2], wqk[:, n % 2], wqk_hi[:, n % 2].bitcast(F32), ALU.subtract)\
                    .then_inc(wqk_ready, 1)

            def split_wo(m):
                dve.wait_ge(wo_hi_ready, m + 1)
                dve.tensor_tensor(wo_lo[:], wo[:, m % 2], wo_hi[:].bitcast(F32), ALU.subtract).then_inc(wo_ready, 1)

            def project(n, half):
                i = 2 * n + half
                tk = slice(half * HALF, (half + 1) * HALF)
                b = ps[:, 6 + side_of["project", n, half] % 2, :]
                dve.wait_ge(pj_swap, 2 * i + 2)
                if i >= 1:
                    dve.wait_ge(pj_hi, i)
                    dve.wait_ge(pj_ready, i)
                link(dve.tensor_tensor(rot[:], b, cos1[:, tk], ALU.mult))
                link(dve.tensor_tensor(rot2[:], swap[:], sin1[:, tk], ALU.mult))
                dve.tensor_tensor(rot[:], rot[:], rot2[:], ALU.add).then_inc(pj_rot, 1)
                dve.wait_ge(pj_hi, i + 1)
                kind, hd = PROJ[n]
                hi, lo = ((q_hi, q_lo) if kind == "q" else (k_hi, k_lo))
                dve.tensor_tensor(lo[:, hd % 2, tk], rot[:], hi[:, hd % 2, tk].bitcast(F32), ALU.subtract)\
                    .then_inc(pj_ready, 1)

            def scores(h, j):
                n = h * NT + j
                w = (NT - j) * P
                dve.wait_ge(s1_ps, n + 1)
                if n >= 2:
                    dve.wait_ge(s1_exp, n - 1)
                slope = float(np.float32(2.0) ** np.float32(-(h + 1) * 8.0 / H1))
                dve.scalar_tensor_tensor(out=cap[:, n % 2, 0:w], in0=dist[:, 0:w], scalar=slope,
                                         in1=psf[:, 1024 * (n % 2):1024 * (n % 2) + w], op0=ALU.mult, op1=ALU.add)\
                    .then_inc(s1_bias, 1)

            def context(h, r):
                k = 3 * h + r
                tiles = min(3, NT - 3 * r)
                dve.wait_ge(c_ps, k + 1)
                if k >= 1:
                    dve.wait_ge(c_ready, k)
                if h >= 2 and r == 0:
                    dve.wait_ge(cT_ps, 2 * (h - 1))
                o = ps[:, 4 + k % 2, 0:tiles * (D1 + 1)].rearrange("p (t d) -> p t d", t=tiles)
                link(dve.reciprocal(c_rden[:, 0:tiles], o[:, :, D1:D1 + 1]))
                dve.tensor_tensor(ctx_tok[:, h % 2, 3 * r:3 * r + tiles, :], o[:, :, 0:D1],
                                  c_rden[:, 0:tiles].to_broadcast((P, tiles, D1)), ALU.mult).then_inc(c_ready, 1)

            def turn(h, half):
                tk = slice(half * HALF, (half + 1) * HALF)
                dve.wait_ge(cT_hi_ready, 2 * h + half + 1)
                dve.tensor_tensor(cT_lo[:, h % PAIR, tk], ps[:, 6 + side_of["turn", h, half] % 2, :],
                                  cT_hi[:, h % PAIR, tk].bitcast(F32), ALU.subtract).then_inc(cT_ready, 1)

            def add_out(m, t):
                dve.wait_ge(s_ps, NT * m + t + 1)
                if m >= 1 and t == 0:
                    dve.wait_ge(s_added, NT * m)
                dve.tensor_tensor(s_tok[:, t, :], ps[:, 6 + side_of["out", m, t] % 2, 0:D],
                                  bo[:] if m == 0 else s_tok[:, t, :], ALU.add).then_inc(s_added, 1)

            for step in DVE_STEPS1:
                {"project": project, "scores": scores, "turn": turn, "context": context, "out": add_out,
                 "split_wqk": split_wqk, "split_wo": split_wo}[step[0]](*step[1:])

            dve.wait_ge(s_added, (H1 // PAIR) * NT)
            dve.wait_ge(act_step, H1 * NT + 1)
            dve.tensor_tensor(rw_lo[:], rw[:], rw_hi[:].bitcast(F32), ALU.subtract).then_inc(rw_ready, 1)
            dve.wait_ge(lg_ps, 1)
            link(dve.tensor_copy(lg[:], ps[:, 0, 0:NT * NE].rearrange("p (t e) -> p t e", t=NT)))
            link(dve.tensor_scalar(r_a[:], lg[:], -1.0, None, ALU.mult))
            dve.tensor_tensor(r_a[:], r_a[:], lg[:], ALU.max).then_inc(lg_read, 1)
            dve.wait_ge(sp_a, 1)
            dve.tensor_scalar(r_c[:], r_b[:], 1.0, None, ALU.add).then_inc(sp_b, 1)
            dve.wait_ge(sp_b, 1)
            link(dve.tensor_scalar(r_a[:], r_c[:], 1.0, None, ALU.is_equal))
            dve.wait_ge(sp_a, 2)
            link(dve.tensor_scalar(r_c[:], r_c[:], -1.0, None, ALU.add))
            link(dve.tensor_tensor(r_c[:], r_c[:], r_a[:], ALU.add))
            link(dve.tensor_tensor(r_d[:], r_d[:], r_a[:], ALU.add))
            link(dve.reciprocal(r_a[:], r_c[:]))
            link(dve.tensor_tensor(r_d[:], r_d[:], r_b[:], ALU.mult))
            link(dve.tensor_tensor(r_d[:], r_d[:], r_a[:], ALU.mult))
            link(dve.tensor_scalar(r_c[:], lg[:], 0.0, None, ALU.max))
            dve.tensor_tensor(r_a[:], r_d[:], r_c[:], ALU.add).then_inc(sp_b, 1)
            dve.wait_ge(sp_b, 2)
            dve.wait_ge(sp_a, 3)
            eb = ebias[:].rearrange("p (t e) -> p t e", t=1).to_broadcast((P, NT, NE))
            link(dve.tensor_scalar(r_c[:], r_b[:], 1e-30, None, ALU.max))
            link(dve.reciprocal(r_d[:], r_c[:]))
            link(dve.tensor_tensor(r_d[:], r_d[:], r_a[:], ALU.mult))
            link(dve.tensor_tensor(r_d[:], r_d[:], r_b[:], ALU.add))
            link(dve.tensor_scalar(r_b[:], r_d[:], 0.5, None, ALU.mult))
            link(dve.tensor_tensor(r_a[:], r_b[:], eb, ALU.add))
            for t in range(NT):
                link(dve.max(top[:, t, :], r_a[:, t, :]))
                link(dve.max_index(topi[:, t, :], top[:, t, :], r_a[:, t, :]))
            link(dve.tensor_copy(topf[:], topi[:]))
            it = iota[:].rearrange("p (t e) -> p t e", t=1).to_broadcast((P, NT, NE))
            for k in range(TOPK):
                dst = r_d if k == 0 else r_c
                link(dve.tensor_tensor(dst[:], it, topf[:, :, k:k + 1].to_broadcast((P, NT, NE)), ALU.is_equal))
                if k:
                    link(dve.tensor_tensor(r_d[:], r_d[:], r_c[:], ALU.add))
            link(dve.tensor_tensor(r_d[:], r_d[:], r_b[:], ALU.mult))
            link(dve.tensor_reduce(r_sum[:], r_d[:], AX_X, ALU.add))
            link(dve.tensor_scalar(r_sum[:], r_sum[:], 1e-20, None, ALU.add))
            link(dve.reciprocal(r_inv[:], r_sum[:]))
            link(dve.tensor_scalar(r_inv[:], r_inv[:], 0.5, None, ALU.mult))
            dve.tensor_tensor(r_d[:], r_d[:], r_inv[:].to_broadcast((P, NT, NE)), ALU.mult).then_inc(gates_ready, 1)
            dve.wait_ge(gT_ps, 1)
            dve.tensor_copy(gT[:], psf[0:NE, HALF:HALF + TOK]).then_inc(gT_ready, 1)

            for s in range(2 * U1):
                b = s % 2
                dve.wait_ge(gu1_ps, s + 1)
                if s >= 2:
                    dve.wait_ge(th1_ready, s - 1)
                    dve.wait_ge(up_ready, s - 1)
                dve.tensor_scalar(gu[:, b].rearrange("p m n -> p (m n)"), psf[:, 1024 * b:1024 * b + 1024], ALPHA, -ALPHA,
                                  ALU.min, ALU.max).then_inc(clip_ready, 1)
                dve.wait_ge(th1_ready, s + 1)
                link(dve.scalar_tensor_tensor(out=e1_a[:, b, :], in0=e1_a[:, b, :], scalar=1.0, in1=gu[:, b, 0, :],
                                              op0=ALU.add, op1=ALU.mult))
                dve.wait_ge(up_ready, s + 1)
                if s >= 2:
                    dve.wait_ge(dn1_ps, s - 1)
                dve.tensor_tensor(h1[:, b, :], e1_a[:, b, :], e1_b[:, b, :], ALU.mult).then_inc(h1_ready, 1)
            combine(1)

        @block.gpsimd
        def _(pool):
            steps = [0]

            def link(ins):
                steps[0] += 1
                ins.then_inc(pool_step, 1)
                pool.wait_ge(pool_step, steps[0])

            def causal(block_ap, ready, n, done):
                pool.wait_ge(ready, n + 1)
                pool.affine_select(out=block_ap, in_=block_ap, compare_op=ALU.is_ge, fill=0.0, base=0,
                                   pattern=[[1, P]], channel_multiplier=-1).then_inc(done, 1)

            for h in range(H0):
                for j in range(NT):
                    causal(A0[:, h % 2, OFF[j]:OFF[j] + P], s0_four, h * NT + j, s0_mask)
            for J in range(NJ):
                b = J % 2
                pool.wait_ge(relu_ready, 4 * J + 4)
                link(pool.tensor_tensor(dq_a[:], dq_a[:], dq_b[:], ALU.add))
                link(pool.tensor_tensor(dq_a[:], dq_a[:], dq_m[:], ALU.add))
                link(pool.tensor_tensor(dq_a[:], dq_a[:], dq_s[:], ALU.mult))
                if J >= 2:
                    pool.wait_ge(dn0_ps, 4 * (J - 1))
                    pool.wait_ge(w0_hi_ready, J - 1)
                for m in range(3):
                    sc = pks[:, b, m:m + 1, :].to_broadcast((P, 2, 2 * P))
                    last = pool.tensor_tensor(w0[:, b, m], dq_a[:, m], sc, ALU.mult)
                last.then_inc(w0_ready, 1)
                pool.wait_ge(w0_hi_ready, J + 1)
                pool.tensor_tensor(w0_lo[:, b], w0[:, b, 0:2], w0_hi[:, b].bitcast(F32), ALU.subtract)\
                    .then_inc(w0_lo_ready, 1)
            for h in range(H1):
                for j in range(NT):
                    causal(P1[:, h % 2, OFF[j]:OFF[j] + P], s1_exp, h * NT + j, s1_mask)

            def low(u):
                pool.wait_ge(ew_hi_ready, u + 1)
                pool.tensor_tensor(ew_lo[:, u % 2], ew[:, u % 2], ew_hi[:, u % 2].bitcast(F32), ALU.subtract)\
                    .then_inc(ew_ready, 1)

            low(0)
            low(1)
            for s in range(2 * U1):
                b, u, half = s % 2, s // 2, s % 2
                pool.wait_ge(clip_ready, s + 1)
                if s >= 2:
                    pool.wait_ge(h1_ready, s - 1)
                if u < NE:
                    pool.wait_ge(in_pb[u % 2], 16 * (u // 2 + 1))
                    pool.tensor_tensor(e1_b[:, b, :], gu[:, b, 1, :], pb[:, u % 2, half * HALF:(half + 1) * HALF],
                                       ALU.mult).then_inc(up_ready, 1)
                else:
                    pool.tensor_scalar(e1_b[:, b, :], gu[:, b, 1, :], 0.5, None, ALU.mult).then_inc(up_ready, 1)
                if s % 2 == 1 and u + 2 < U1:
                    low(u + 2)


PROJ = [p for g in range(G1) for p in [("k", g)] + [("q", g * REP + i) for i in range(REP)]]


def schedule():
    steps = []
    first = [i for i, p in enumerate(PROJ) if p == ("q", 0)][0]
    for n in range(first + 1):
        steps += [("project", n, 0), ("project", n, 1)]
    for h in range(H1 + 1):
        todo = []
        if h + 1 < H1:
            at = PROJ.index(("q", h + 1))
            if (h + 1) % REP == 0:
                todo += [("project", at - 1, 0), ("project", at - 1, 1)]
            todo += [("project", at, 0), ("project", at, 1)]
        for j in range(NT):
            if h < H1:
                steps.append(("scores", h, j))
            if h >= 1:
                steps.append(("context", h - 1, j))
            if j % 2 == 1 and todo:
                steps.append(todo.pop(0))
            if j == 2 and h >= 2:
                steps += [("turn", h - 2, 0), ("turn", h - 2, 1)]
            if j >= 4 and h >= 2 and (h - 2) % PAIR == PAIR - 1:
                m = (h - 2) // PAIR
                steps += [("out", m, 2 * (j - 4)), ("out", m, 2 * (j - 4) + 1)]
    steps += [("turn", H1 - 1, 0), ("turn", H1 - 1, 1)]
    steps += [("out", H1 // PAIR - 1, t) for t in range(NT)]
    return steps


STEPS1 = schedule()
SIDE = [s for s in STEPS1 if s[0] in ("project", "turn", "out")]
side_of = {s: n for n, s in enumerate(SIDE)}


def side_read(step):
    if step[0] == "project":
        return "pj_rot", 2 * step[1] + step[2] + 1
    if step[0] == "turn":
        return "cT_ready", 2 * step[1] + step[2] + 1
    return "s_added", NT * step[1] + step[2] + 1


def follow(engine):
    out = [("split_wqk", 0), ("split_wqk", 1), ("split_wo", 0)]
    for s in STEPS1:
        if s[0] == "context":
            if engine == "dve" and (s[2] % 3 == 2 or s[2] == NT - 1):
                out.append(("context", s[1], s[2] // 3))
            continue
        if s[0] == "out":
            if engine == "dve":
                out.append(s)
            if s[2] == NT - 1 and s[1] + 1 < H1 // PAIR:
                out.append(("split_wo", s[1] + 1))
            continue
        out.append(s)
        if s[0] == "project" and s[2] == 1 and s[1] + 2 < len(PROJ):
            out.append(("split_wqk", s[1] + 2))
    return out


ACT_STEPS1 = follow("act")
DVE_STEPS1 = follow("dve")


def kernel(**inputs):
    import numpy as _np
    import concourse.bacc as _bacc
    from concourse import mybir as _mybir
    from concourse.bass_utils import run_bass_kernel_spmd as _run

    a = {k: _np.asarray(v) for k, v in inputs.items()}
    half0 = D0 // 2
    inv0 = (_np.float32(1.0) / _np.power(_np.float32(10000.0), _np.arange(0, D0, 2, dtype=_np.float32) / _np.float32(D0))).astype(_np.float32)
    ang0 = _np.arange(TOK, dtype=_np.float32)[:, None] * inv0[None, :]
    c0, s0 = _np.cos(ang0), _np.sin(ang0)
    rope0 = _np.stack([_np.concatenate([c0, c0], 1), _np.concatenate([-s0, s0], 1)], 1).astype(_np.float32)
    rope0 = rope0.reshape(NT, P, 2, D0).transpose(1, 0, 2, 3)
    inv1 = (_np.float32(1.0) / _np.power(_np.float32(10000.0), _np.arange(0, D1, 2, dtype=_np.float32) / _np.float32(D1))).astype(_np.float32)
    ang1 = (_np.arange(TOK, dtype=_np.float32)[:, None] * inv1[None, :]).T
    c1, s1 = _np.cos(ang1), _np.sin(ang1)
    consts = {
        "ident": _np.eye(P, dtype=_np.float32),
        "rope0": rope0,
        "cos1": _np.concatenate([c1, c1], 0),
        "sin1": _np.concatenate([-s1, s1], 0),
        "dist": (_np.arange(P)[:, None] - _np.arange(TOK)[None, :]).astype(_np.float32),
        "iota": _np.tile(_np.arange(NE, dtype=_np.float32), (P, 1)),
    }

    def blocks(w):
        return w.T.reshape(w.shape[1], NJ, P, 2).transpose(0, 1, 3, 2).reshape(w.shape[1], NJ, 2 * P)

    def halves(w, heads):
        return w.reshape(D, heads, D1 // 2, 2).transpose(0, 1, 3, 2).reshape(D, heads * D1)

    def with_shared(e, s):
        return _np.concatenate([e, s[None]], 0).transpose(0, 2, 1)

    feeds = {
        "x": a["L0_attn_x"].reshape(TOK, D), "wqkv": a["L0_attn_w_qkv"], "wout": a["L0_attn_w_out"],
        "lns": a["L0_attn_ln_scale"], "lnb": a["L0_attn_ln_bias"],
        "gp": blocks(a["L0_ffn_gate_W_packed"]), "gs": blocks(a["L0_ffn_gate_scales"]),
        "up": blocks(a["L0_ffn_up_W_packed"]), "us": blocks(a["L0_ffn_up_scales"]),
        "dp": a["L0_ffn_down_W_packed"].T.reshape(NJ, P, D), "ds": a["L0_ffn_down_scales"].T.reshape(NJ, D // BLK, D),
        "wq": halves(a["L1_attn_Wq"], H1), "wk": halves(a["L1_attn_Wk"], G1), "wv": a["L1_attn_Wv"],
        "wo": a["L1_attn_Wo"], "bo": a["L1_attn_bo"],
        "rw": a["L1_ffn_router_w"].T.reshape(P, NC, NE), "eb": a["L1_ffn_expert_bias"],
        "eg": with_shared(a["L1_ffn_gate_w"], a["L1_ffn_shared_gate_w"]),
        "eu": with_shared(a["L1_ffn_up_w"], a["L1_ffn_shared_up_w"]),
        "ed": with_shared(a["L1_ffn_down_w"], a["L1_ffn_shared_down_w"]),
        **consts,
    }
    nc = _bacc.Bacc("TRN2", target_bir_lowering=False, num_devices=1)
    arrays, args = {}, []
    for name, v in feeds.items():
        v = _np.ascontiguousarray(v)
        arrays[f"in_{name}"] = v
        args.append(nc.dram_tensor(f"in_{name}", v.shape, _mybir.dt.from_np(v.dtype), kind="ExternalInput").ap())
    out = nc.dram_tensor("out", (1, TOK, D), F32, kind="ExternalOutput").ap()
    build_program(nc, *args, out)
    r = _run(nc, [arrays], core_ids=[0])
    return r.results[0]["out"]
```

```python
from contextlib import ExitStack

import numpy as np

import concourse.bass as bass
from concourse import mybir

ALU = mybir.AluOpType
ACT = mybir.ActivationFunctionType
F32 = mybir.dt.float32
F32R = mybir.dt.float32r
BF16 = mybir.dt.bfloat16
I32 = mybir.dt.int32
U32 = mybir.dt.uint32
AX_X = mybir.AxisListType.X

P = 128
TOK = 1024
NT = TOK // P
D = 256
NC = D // P
HALF = 512
NHALF = TOK // HALF
LN_EPS = 1e-5

H0, D0 = 16, 16
STK = 4 * D0
QUAD = 4
MLP = 2048
NJ = MLP // (2 * P)
U0 = MLP // P
BLK = 32
GELU_C, GELU_K = 0.7978845608028654, 0.044715
H1, G1, D1 = 16, 4, 128
REP = H1 // G1
CAP = 30.0
PAIR = 2
NE, TOPK, ALPHA = 32, 4, 7.0
U1 = NE + 1

OFF = [sum((NT - i) * P for i in range(j)) for j in range(NT + 1)]
TRI = OFF[NT]


def spans(width):
    return [(a, min(a + HALF, width)) for a in range(0, width, HALF)]


def build_program(nc, x_in, wqkv_in, wout_in, lns_in, lnb_in, packed_in, scales_in,
                  wqk_in, wv_in, wo_in, bo_in, rw_in, eb_in, experts_in,
                  ident_in, rope0_in, cos1_in, sin1_in, dist_in, iota_in, out):
    gates_dram = nc.dram_tensor("gates_scratch", (NE, TOK), F32, kind="Internal").ap()

    with ExitStack() as ctx:
        def sem(name):
            return ctx.enter_context(nc.semaphore(name))

        def alloc(scope):
            return lambda name, shape, dt=F32: scope.enter_context(nc.sbuf_tensor(name, shape, dt))

        sb = alloc(ctx)
        ident = sb("ident", [P, P])
        x_tok = sb("x_tok", [P, NT, D])
        xn_tok = sb("xn_tok", [P, NT, D])
        xT_hi = sb("xT_hi", [P, NC, TOK], F32R)
        xT_lo = sb("xT_lo", [P, NC, TOK], F32R)
        s_tok = sb("s_tok", [P, NT, D])
        ln_stats = sb("ln_stats", [P, 6])
        ln_mv = sb("ln_mv", [P, NT, 2])
        ln_var = sb("ln_var", [P, NT])
        ln_sd = sb("ln_sd", [P, NT])
        ln_r = sb("ln_r", [P, NT])
        ln_t = sb("ln_t", [P, NT])
        consts = sb("consts", [P, 4])

        l0 = ExitStack()
        sb = alloc(l0)
        V0 = sb("V0", [P, NT, H0, D0 + 1])
        qk_tok = sb("qk_tok", [P, NT, 2 * D])
        wout = sb("wout", [P, NC, D])
        wout_hi = sb("wout_hi", [P, NC, D], F32R)
        wout_lo = sb("wout_lo", [P, NC, D], F32R)
        rope0 = sb("rope0", [P, NT, 2, D0])
        rope_a = sb("rope_a", [P, 2 * D])
        rope_b = sb("rope_b", [P, 2 * D])
        hv = sb("hv", [P, NT, 2 * H0])
        hsd = sb("hsd", [P, NT, 2 * H0])
        hr = sb("hr", [P, NT, 2 * H0])
        ht = sb("ht", [P, NT, 2 * H0])
        hm = sb("hm", [P, 2, 2 * H0])
        lns = sb("lns", [P, 2, D0])
        o_raw = sb("o_raw", [P, TOK])
        o_rden = sb("o_rden", [P, NT, QUAD, 1])
        mix0_a = sb("mix0_a", [P, 2, D])
        mix0_b = sb("mix0_b", [P, 2, D])
        g0_tok = s_tok
        o_tok = xn_tok
        oT_hi, oT_lo = xT_hi, xT_lo

        l0m = ExitStack()
        sb = alloc(l0m)
        pk = sb("pk", [P, 2, 3, 2 * P], I32)
        pks = sb("pks", [P, 2, 3, 2 * P])
        mag = sb("mag", [P, 3, 2, 2 * P], I32)
        sgn = sb("sgn", [P, 3, 2, 2 * P], I32)
        dq_a = sb("dq_a", [P, 3, 2, 2 * P], BF16)
        dq_b = sb("dq_b", [P, 3, 2, 2 * P], BF16)
        dq_m = sb("dq_m", [P, 3, 2, 2 * P], BF16)
        dq_s = sb("dq_s", [P, 3, 2, 2 * P], BF16)
        w0 = sb("w0", [P, 2, 2, 2 * P])
        w0_hi = sb("w0_hi", [P, 3, 2, 2, 2 * P], F32R)
        w0_lo = sb("w0_lo", [P, 3, 2, 2, 2 * P], F32R)
        w0_dn = sb("w0_dn", [P, 3, 2, 2 * P])
        l0w = ExitStack()
        sb = alloc(l0w)
        wqkv = sb("wqkv", [P, NC, 3 * D])
        wqkv_hi = sb("wqkv_hi", [P, NC, 3 * D], F32R)
        wqkv_lo = sb("wqkv_lo", [P, NC, 3 * D], F32R)
        l0w.close()
        l0w = ExitStack()
        sb = alloc(l0w)
        e0_gu = sb("e0_gu", [P, 3, 2, HALF])
        e0_a = sb("e0_a", [P, 2, HALF])
        e0_b = sb("e0_b", [P, 3, HALF])
        h0 = sb("h0", [P, 3, HALF])
        f0T = sb("f0T", [P, NC, TOK])
        l0w.close()
        l0m.close()

        l0a = ExitStack()
        sb = alloc(l0a)
        stack = sb("stack", [P, 2, 2, H0, 4, D0])
        QT = sb("QT", [P, H0 // 2, TOK], F32R)
        KT = sb("KT", [P, H0 // 2, TOK], F32R)
        A0 = sb("A0", [P, 2, TRI])
        l0a.close()
        l0.close()

        l1 = ExitStack()
        sb = alloc(l1)
        eraw = sb("eraw", [P, 3, 3, D])
        l1a = ExitStack()
        sb = alloc(l1a)
        cos1 = sb("cos1", [P, TOK])
        sin1 = sb("sin1", [P, TOK])
        dist = sb("dist", [P, TOK])
        wqk = sb("wqk", [P, 2, NC, D1])
        wqk_hi = sb("wqk_hi", [P, 2, NC, D1], F32R)
        wqk_lo = sb("wqk_lo", [P, 2, NC, D1], F32R)
        q_hi = sb("q_hi", [P, 2, TOK], F32R)
        q_lo = sb("q_lo", [P, 2, TOK], F32R)
        k_hi = sb("k_hi", [P, 2, TOK], F32R)
        k_lo = sb("k_lo", [P, 2, TOK], F32R)
        V1 = sb("V1", [P, NT, G1, D1 + 1])
        P1 = sb("P1", [P, 2, TRI])
        cap = sb("cap", [P, 2, TOK])
        swap = sb("swap", [P, 2, HALF])
        rot = sb("rot", [P, 3, HALF])
        c_rden = sb("c_rden", [P, 3, 1])
        ctx_tok = sb("ctx_tok", [P, 2, NT, D1])
        cT_hi = sb("cT_hi", [P, PAIR, TOK], F32R)
        cT_lo = sb("cT_lo", [P, PAIR, TOK], F32R)
        wo = sb("wo", [P, 2, PAIR, D])
        wo_hi = sb("wo_hi", [P, PAIR, D], F32R)
        wo_lo = sb("wo_lo", [P, PAIR, D], F32R)
        bo = sb("bo", [P, D])
        wv = P1[:, 0, 0:NC * G1 * D1].rearrange("p (c n) -> p c n", c=NC)
        wv_hi = q_hi[:, 1, :].rearrange("p (c n) -> p c n", c=NC)
        wv_lo = q_lo[:, 1, :].rearrange("p (c n) -> p c n", c=NC)
        rw = sb("rw", [P, NC, NE])
        rw_hi = sb("rw_hi", [P, NC, NE], F32R)
        rw_lo = sb("rw_lo", [P, NC, NE], F32R)
        ebias = sb("ebias", [P, NE])
        iota = sb("iota", [P, NE])
        lg, r_a, r_b, r_c, r_d = (xn_tok[:, i, :].rearrange("p (t e) -> p t e", t=NT) for i in range(5))
        gT = xn_tok[0:NE, 0:4, :].rearrange("e t n -> e (t n)")
        top = sb("top", [P, NT, 8])
        topi = sb("topi", [P, NT, 8], U32)
        topf = sb("topf", [P, NT, 8])
        r_sum = sb("r_sum", [P, NT, 1])
        r_inv = sb("r_inv", [P, NT, 1])
        l1a.close()

        l1b = ExitStack()
        sb = alloc(l1b)
        pb = sb("pb", [P, 2, TOK])
        e_hi = sb("e_hi", [P, 3, 3, D], F32R)
        e_lo = sb("e_lo", [P, 3, 3, D], F32R)
        gu = sb("gu", [P, 2, 2, HALF])
        e1_a = sb("e1_a", [P, 2, HALF])
        e1_b = sb("e1_b", [P, 2, HALF])
        h1 = sb("h1", [P, 2, HALF])
        h1_hi = sb("h1_hi", [P, 3, HALF], F32R)
        h1_lo = sb("h1_lo", [P, 3, HALF], F32R)
        f1T = sb("f1T", [P, NC, TOK])
        mix1_a = sb("mix1_a", [P, 2, D])
        mix1_b = sb("mix1_b", [P, 2, D])
        l1b.close()
        l1.close()

        ps = ctx.enter_context(nc.psum_tensor("ps", [P, 8, HALF], F32))
        psf = ps[:, :, :].rearrange("p b n -> p (b n)")

        in_x, in_const, in_wqkv, in_l0c = sem("in_x"), sem("in_const"), sem("in_wqkv"), sem("in_l0c")
        in_wout, in_pk, in_l1c = sem("in_wout"), [sem("in_pk0"), sem("in_pk1")], sem("in_l1c")
        in_wqk, in_wo, in_wv = [sem("in_wqk0"), sem("in_wqk1")], [sem("in_wo0"), sem("in_wo1")], sem("in_wv")
        in_router = sem("in_router")
        in_ew = [sem("in_ew0"), sem("in_ew1"), sem("in_ew2")]
        in_pb = [sem("in_pb0"), sem("in_pb1")]
        vec = sem("vec")
        pool_step = sem("pool_step")
        act_step = sem("act_step")
        consts_ready = sem("consts_ready")
        var_ready, sd_ready, xn_ready = sem("var_ready"), sem("sd_ready"), sem("xn_ready")
        xT_ps, xT_hi_ready, xT_ready = sem("xT_ps"), sem("xT_hi_ready"), sem("xT_ready")
        wqkv_hi_ready, wqkv_ready = sem("wqkv_hi_ready"), sem("wqkv_ready")
        qkv_ps, qkv_read = sem("qkv_ps"), sem("qkv_read")
        hvar_ready, hsd_ready = sem("hvar_ready"), sem("hsd_ready")
        qk_ready, stk_hi, stk_ready, stk_ps, stk_read = (sem("qk_ready"), sem("stk_hi"), sem("stk_ready"),
                                                        sem("stk_ps"), sem("stk_read"))
        s0_ps, s0_sq, s0_four, s0_mask = sem("s0_ps"), sem("s0_sq"), sem("s0_four"), sem("s0_mask")
        o0_ps, o0_copied, o0_turned, o0_ready = sem("o0_ps"), sem("o0_copied"), sem("o0_turned"), sem("o0_ready")
        wout_hi_ready, wout_ready = sem("wout_hi_ready"), sem("wout_ready")
        oT_ps, oT_hi_ready, oT_ready = sem("oT_ps"), sem("oT_hi_ready"), sem("oT_ready")
        so_ps, so_read = sem("so_ps"), sem("so_read")
        nib_ready, relu_ready, w0_ready, w0_hi_ready, w0_lo_ready = (
            sem("nib_ready"), sem("relu_ready"), sem("w0_ready"), sem("w0_hi_ready"), sem("w0_lo_ready"))
        gu0_copied, square_ready, g0_ready = sem("gu0_copied"), sem("square_ready"), sem("g0_ready")
        stk_read_act, stk_read_dve = sem("stk_read_act"), sem("stk_read_dve")
        qk_copied, v0_copied = sem("qk_copied"), sem("v0_copied")
        gu0_ps, g2_ready, inner_ready, th0_ready, h0_ready, dn0_ps = (
            sem("gu0_ps"), sem("g2_ready"), sem("inner_ready"), sem("th0_ready"), sem("h0_ready"), sem("dn0_ps"))
        fT_ready, f_ps, fth_ready, x_ready = sem("fT_ready"), sem("f_ps"), sem("fth_ready"), sem("x_ready")
        wv_hi_ready, wv_ready, v_ps, v_read = sem("wv_hi_ready"), sem("wv_ready"), sem("v_ps"), sem("v_read")
        wqk_hi_ready, wqk_ready = sem("wqk_hi_ready"), sem("wqk_ready")
        pj_ps, pj_swap, pj_cos, pj_rot = sem("pj_ps"), sem("pj_swap"), sem("pj_cos"), sem("pj_rot")
        parts_hi, parts_ready = sem("parts_hi"), sem("parts_ready")
        s1_ps, s1_bias, s1_exp, s1_mask = sem("s1_ps"), sem("s1_bias"), sem("s1_exp"), sem("s1_mask")
        c_ps, c_ready = sem("c_ps"), sem("c_ready")
        cT_ps, cT_read = sem("cT_ps"), sem("cT_read")
        wo_hi_ready, wo_ready = sem("wo_hi_ready"), sem("wo_ready")
        s_ps, s_added = sem("s_ps"), sem("s_added")
        rw_hi_ready, rw_ready, lg_ps, lg_read, sp_a, sp_b, gates_ready = (sem("rw_hi_ready"), sem("rw_ready"), sem("lg_ps"), sem("lg_read"),
                                                            sem("sp_a"), sem("sp_b"), sem("gates_ready"))
        gT_ps, gT_ready, gates_out = sem("gT_ps"), sem("gT_ready"), sem("gates_out")
        e_hi_ready, e_ready, h1_hi_ready, h1_parts_ready = (sem("e_hi_ready"), sem("e_ready"), sem("h1_hi_ready"),
                                                            sem("h1_parts_ready"))
        gu1_ps, clip_ready, th1_ready, up_ready, h1_ready, dn1_ps = (
            sem("gu1_ps"), sem("clip_ready"), sem("th1_ready"), sem("up_ready"), sem("h1_ready"), sem("dn1_ps"))
        out_sent = sem("out_sent")

        block = ctx.enter_context(nc.Block())

        @block.sync
        def _(sp):
            def to_all(v, n):
                return v.rearrange("(a n) -> a n", a=1).to_broadcast((P, n))

            sp.dma_start(x_tok[:], x_in.rearrange("(t p) d -> p t d", p=P)).then_inc(in_x, 16)
            sp.dma_start(ident[:], ident_in).then_inc(in_const, 16)
            sp.dma_start(wqkv[:], wqkv_in.rearrange("(p c) n -> p c n", c=NC)).then_inc(in_wqkv, 16)
            for J in range(NJ):
                if J >= 2:
                    sp.wait_ge(w0_ready, J - 1)
                b = J % 2
                sp.dma_start(pk[:, b], packed_in[J]).then_inc(in_pk[b], 16)
                sp.dma_start(pks[:, b], scales_in[J]).then_inc(in_pk[b], 16)
                if J == 1:
                    sp.dma_start(rope0[:], rope0_in).then_inc(in_l0c, 16)
                    sp.dma_start(lns[:, 0, :], to_all(lns_in, D0)).then_inc(in_l0c, 16)
                    sp.dma_start(lns[:, 1, :], to_all(lnb_in, D0)).then_inc(in_l0c, 16)
                    sp.dma_start(wout[:], wout_in.rearrange("(c p) n -> p c n", p=P)).then_inc(in_wout, 16)
            sp.wait_ge(x_ready, NT)
            sp.dma_start(rw[:], rw_in).then_inc(in_router, 16)
            sp.dma_start(ebias[:], to_all(eb_in, NE)).then_inc(in_router, 16)
            sp.dma_start(iota[:], iota_in).then_inc(in_router, 16)
            sp.dma_start(wv, wv_in.rearrange("(p c) n -> p c n", c=NC)).then_inc(in_wv, 16)
            sp.dma_start(cos1[:], cos1_in).then_inc(in_l1c, 16)
            sp.dma_start(sin1[:], sin1_in).then_inc(in_l1c, 16)
            sp.dma_start(dist[:], dist_in).then_inc(in_l1c, 16)
            sp.dma_start(bo[:], to_all(bo_in, D)).then_inc(in_l1c, 16)
            for u in range(3):
                sp.dma_start(eraw[:, u], experts_in[u]).then_inc(in_ew[u], 16)

            def load_wo(m):
                if m >= 2:
                    sp.wait_ge(wo_ready, m - 1)
                sp.dma_start(wo[:, m % 2], wo_in[m * PAIR * D1:(m + 1) * PAIR * D1, :].rearrange("(h p) n -> p h n", p=P))\
                    .then_inc(in_wo[m % 2], 16)

            for n, (kind, i) in enumerate(PROJ):
                if n >= 2:
                    sp.wait_ge(wqk_ready, n - 1)
                sp.dma_start(wqk[:, n % 2], wqk_in[n]).then_inc(in_wqk[n % 2], 16)
                if kind == "q" and i % PAIR == 0 and i >= PAIR:
                    load_wo(i // PAIR - 1)
            load_wo(H1 // PAIR - 1)
            sp.wait_ge(gT_ready, 2)
            sp.dma_start(gates_dram, gT).then_inc(gates_out, 16)
            sp.wait_ge(gates_out, 16)
            sp.wait_ge(s_added, (H1 // PAIR) * NT)
            for u in range(U1):
                if u < NE:
                    if u >= 2:
                        sp.wait_ge(up_ready, 2 * (u - 1))
                    sp.dma_start(pb[:, u % 2], gates_dram[u:u + 1, :].to_broadcast((P, TOK))).then_inc(in_pb[u % 2], 16)
                if u + 3 < U1:
                    sp.wait_ge(e_ready, u + 1)
                    sp.dma_start(eraw[:, u % 3], experts_in[u + 3]).then_inc(in_ew[u % 3], 16)
            for t in range(NT):
                sp.wait_ge(x_ready, NT + t + 1)
                sp.dma_start(out[0, t * P:(t + 1) * P, :], x_tok[:, t, :]).then_inc(out_sent, 16)
            sp.wait_ge(out_sent, 16 * NT)

        @block.tensor
        def _(pe):
            def mm3(o, l_hi, l_lo, r_hi, r_lo, start, stop):
                pe.matmul(o, l_hi, r_hi, start=start, stop=False)
                pe.matmul(o, l_lo, r_hi, start=False, stop=False)
                return pe.matmul(o, l_hi, r_lo, start=False, stop=stop)

            def transpose_x(layer):
                for k in range(2 * NHALF):
                    half, c = k // NC, k % NC
                    pe.wait_ge(xn_ready, NT * layer + 4 * (half + 1))
                    for i in range(4):
                        t = 4 * half + i
                        last = pe.transpose(ps[:, k, i * P:(i + 1) * P], xn_tok[:, t, c::NC], ident[:])
                    last.then_inc(xT_ps, 1)

            def qkv0():
                pe.wait_ge(wqkv_ready, 1)
                for t in range(NT):
                    pe.wait_ge(xT_ready, 2 * (t // 4 + 1))
                    if t >= 2:
                        pe.wait_ge(qk_copied, t - 1)
                        pe.wait_ge(v0_copied, t - 1)
                    b = 4 + 2 * (t % 2)
                    tk = slice(t * P, (t + 1) * P)
                    for o, cols in ((ps[:, b, :], slice(0, 2 * D)), (ps[:, b + 1, 0:D], slice(2 * D, 3 * D))):
                        for c in range(NC):
                            last = mm3(o, xT_hi[:, c, tk], xT_lo[:, c, tk], wqkv_hi[:, c, cols], wqkv_lo[:, c, cols],
                                       c == 0, c == NC - 1)
                    last.then_inc(qkv_ps, 1)

            def turn_stack(t):
                pe.wait_ge(stk_ready, t + 1)
                for q in range(4):
                    if t >= 1:
                        pe.wait_ge(stk_read_act if q % 2 == 0 else stk_read_dve, 2 * (t - 1) + q // 2 + 1)
                    for i in range(4):
                        h = 2 * (4 * (q % 2) + i)
                        src = stack[:, t % 2, q // 2, h:h + 2].rearrange("p h a d -> p (h a d)")
                        last = pe.transpose(ps[:, q, i * P:(i + 1) * P], src, ident[:])
                    last.then_inc(stk_ps, 1)

            def turn_f0(t):
                if t >= 2:
                    pe.wait_ge(g0_ready, t - 1)
                for c in range(NC):
                    last = pe.transpose(ps[:, 6 + t % 2, c * P:(c + 1) * P], f0T[:, c, t * P:(t + 1) * P], ident[:])
                last.then_inc(f_ps, 1)

            def scores0(h, j):
                n = h * NT + j
                if n == 0:
                    pe.wait_ge(stk_read_act, 2 * NT)
                    pe.wait_ge(stk_read_dve, 2 * NT)
                if n >= 2:
                    pe.wait_ge(s0_sq, n - 1)
                rows = slice(64 * (h % 2), 64 * (h % 2) + STK)
                o = 1024 * (n % 2)
                for a, e in spans((NT - j) * P):
                    last = pe.matmul(psf[:, o + a:o + e], KT[rows, h // 2, j * P:(j + 1) * P],
                                     QT[rows, h // 2, j * P + a:j * P + e], start=True, stop=True)
                last.then_inc(s0_ps, 1)

            def out0(h, j):
                if j == 0:
                    if h == 0:
                        pe.wait_ge(g0_ready, NT)
                    if h >= 2:
                        pe.wait_ge(o0_copied, h - 1)
                    if h % QUAD == 1 and h >= QUAD:
                        pe.wait_ge(o0_ready, h // QUAD)
                pe.wait_ge(s0_mask, h * NT + j + 1)
                for half in range(NHALF):
                    a, e = max(j * P, half * HALF), (half + 1) * HALF
                    if a < e:
                        last = pe.matmul(ps[0:D0 + 1, 4 + 2 * (h % 2) + half, a - half * HALF:HALF], V0[:, j, h, :],
                                         A0[:, h % 2, OFF[j] + a - j * P:OFF[j] + e - j * P],
                                         start=(j == 0), stop=(j == 4 * half + 3))
                if j == NT - 1:
                    last.then_inc(o0_ps, 1)

            def turn_out0(g):
                pe.wait_ge(o0_copied, QUAD * (g + 1))
                for t in range(NT):
                    last = pe.transpose(psf[:, 3072 + t * P:3072 + (t + 1) * P], o_raw[:, t * P:(t + 1) * P], ident[:])
                last.then_inc(o0_turned, 1)

            def project_out0():
                pe.wait_ge(o0_ready, H0 // QUAD)
                for k in range(2 * NHALF):
                    half, c = k // NC, k % NC
                    for i in range(4):
                        last = pe.transpose(ps[:, k, i * P:(i + 1) * P], o_tok[:, 4 * half + i, c * P:(c + 1) * P],
                                            ident[:])
                    last.then_inc(oT_ps, 1)
                pe.wait_ge(oT_ready, 2 * NC)
                pe.wait_ge(wout_ready, 1)
                for t in range(NT):
                    if t >= 2:
                        pe.wait_ge(x_ready, t - 1)
                    tk = slice(t * P, (t + 1) * P)
                    for c in range(NC):
                        last = mm3(ps[:, 4 + t % 2, 0:D], oT_hi[:, c, tk], oT_lo[:, c, tk], wout_hi[:, c], wout_lo[:, c],
                                   c == 0, c == NC - 1)
                    last.then_inc(so_ps, 1)

            def gate_up(s, w_hi, w_lo, done):
                half = s % 2
                tk = slice(half * HALF, (half + 1) * HALF)
                for m in range(2):
                    for c in range(NC):
                        last = mm3(ps[:, 2 * (s % 2) + m, :], w_hi(m, c), w_lo(m, c), xT_hi[:, c, tk],
                                   xT_lo[:, c, tk], c == 0, c == NC - 1)
                last.then_inc(done, 1)

            pe.wait_ge(in_const, 16)
            transpose_x(0)
            qkv0()
            for s in range(2 * U0 + 2):
                if s < 2 * U0:
                    J, col = s // 4, (s // 2) % 2 * P
                    if s % 4 == 0:
                        pe.wait_ge(w0_lo_ready, J + 1)
                    if s == 0:
                        pe.wait_ge(qk_copied, NT)
                        pe.wait_ge(v0_copied, NT)
                    if s >= 2:
                        pe.wait_ge(gu0_copied, s - 1)
                    gate_up(s, lambda m, c: w0_hi[:, J % 3, m, c, col:col + P],
                            lambda m, c: w0_lo[:, J % 3, m, c, col:col + P], gu0_ps)
                if s >= 2:
                    r = s - 2
                    u, half = r // 2, r % 2
                    pe.wait_ge(h0_ready, r + 1)
                    for c in range(NC):
                        last = pe.matmul(ps[:, 4 + 2 * c + half, :], w0_dn[:, (u // 2) % 3, u % 2, c * P:(c + 1) * P],
                                         h0[:, r % 3, :], start=(u == 0), stop=(u == U0 - 1))
                    last.then_inc(dn0_ps, 1)
            pe.wait_ge(fT_ready, 2 * NC)
            for t in range(NT):
                turn_stack(t)
                turn_f0(t)
            for h in range(H0 + 1):
                for j in range(NT):
                    if h < H0:
                        scores0(h, j)
                    if h >= 1:
                        out0(h - 1, j)
                    if h >= QUAD and h % QUAD == 1 and j == 3:
                        turn_out0(h // QUAD - 1)
            turn_out0(H0 // QUAD - 1)
            project_out0()

            pe.wait_ge(x_ready, NT)
            transpose_x(1)
            pe.wait_ge(xT_ready, 4 * NC)
            pe.wait_ge(rw_ready, 1)
            for t in range(NT):
                tk = slice(t * P, (t + 1) * P)
                for c in range(NC):
                    last = mm3(ps[:, 6, t * NE:(t + 1) * NE], xT_hi[:, c, tk], xT_lo[:, c, tk], rw_hi[:, c], rw_lo[:, c],
                               c == 0, c == NC - 1)
            last.then_inc(lg_ps, 1)
            pe.wait_ge(wv_ready, 1)
            for t in range(NT):
                if t >= 2:
                    pe.wait_ge(v_read, t - 1)
                tk = slice(t * P, (t + 1) * P)
                for c in range(NC):
                    last = mm3(ps[:, 4 + t % 2, :], xT_hi[:, c, tk], xT_lo[:, c, tk], wv_hi[:, c], wv_lo[:, c],
                               c == 0, c == NC - 1)
                last.then_inc(v_ps, 1)
            pe.wait_ge(v_read, NT)
            pe.wait_ge(lg_read, 1)

            def side_slot():
                n = side[0]
                side[0] += 1
                if n >= 2:
                    name, a, b = SIDE[n - 2]
                    if name == "project":
                        pe.wait_ge(pj_swap, 2 * (2 * a + b + 1))
                    elif name == "turn":
                        pe.wait_ge(cT_read, 2 * a + b + 1)
                    elif name == "out":
                        pe.wait_ge(s_added, NT * a + b + 1)
                    else:
                        pe.wait_ge(gT_ready, b + 1)
                return ps[:, 6 + n % 2, :]
            side = [0]

            def project(n, half):
                pe.wait_ge(wqk_ready, n + 1)
                o = side_slot()
                tk = slice(half * HALF, (half + 1) * HALF)
                for c in range(NC):
                    last = mm3(o, wqk_hi[:, n % 2, c], wqk_lo[:, n % 2, c], xT_hi[:, c, tk], xT_lo[:, c, tk],
                               c == 0, c == NC - 1)
                last.then_inc(pj_ps, 1)

            def scores1(h, j):
                n = h * NT + j
                if j == 0:
                    pe.wait_ge(parts_ready, part_of["project", PROJ.index(("q", h)), 1] + 1)
                if n >= 2:
                    pe.wait_ge(s1_bias, n - 1)
                g = h // REP
                o = 1024 * (n % 2)
                kk = slice(j * P, (j + 1) * P)
                for a, e in spans((NT - j) * P):
                    qq = slice(j * P + a, j * P + e)
                    last = mm3(psf[:, o + a:o + e], k_hi[:, g % 2, kk], k_lo[:, g % 2, kk], q_hi[:, h % 2, qq],
                               q_lo[:, h % 2, qq], True, True)
                last.then_inc(s1_ps, 1)

            def context(h, t):
                r = 3 * h + t // 3
                if t % 3 == 0 and r >= 2:
                    pe.wait_ge(c_ready, r - 1)
                pe.wait_ge(s1_mask, h * NT + t + 1)
                o = (D1 + 1) * (t % 3)
                for j in range(t + 1):
                    a = OFF[j] + (t - j) * P
                    last = pe.matmul(ps[:, 4 + r % 2, o:o + D1 + 1], P1[:, h % 2, a:a + P], V1[:, j, h // REP, :],
                                     start=(j == 0), stop=(j == t))
                if t % 3 == 2 or t == NT - 1:
                    last.then_inc(c_ps, 1)

            def turn_context(h, half):
                pe.wait_ge(c_ready, 3 * h + (2 if half == 0 else 3))
                o = side_slot()
                for i in range(4):
                    last = pe.transpose(o[:, i * P:(i + 1) * P], ctx_tok[:, h % 2, 4 * half + i, :], ident[:])
                last.then_inc(cT_ps, 1)

            def project_out1(m, t):
                if t == 0:
                    pe.wait_ge(parts_ready, part_of["turn", PAIR * m + PAIR - 1, 1] + 1)
                    pe.wait_ge(wo_ready, m + 1)
                o = side_slot()
                tk = slice(t * P, (t + 1) * P)
                for i in range(PAIR):
                    last = mm3(o[:, 0:D], cT_hi[:, i, tk], cT_lo[:, i, tk], wo_hi[:, i], wo_lo[:, i], i == 0, i == PAIR - 1)
                last.then_inc(s_ps, 1)

            def turn_gates(_, half):
                pe.wait_ge(gates_ready, 1)
                o = side_slot()
                for i in range(4):
                    last = pe.transpose(o[0:NE, i * P:(i + 1) * P], r_d[:, 4 * half + i, :], ident[:])
                last.then_inc(gT_ps, 1)

            for step in STEPS1:
                {"project": project, "scores": scores1, "context": context, "turn": turn_context,
                 "out": project_out1, "gates": turn_gates}[step[0]](*step[1:])

            pe.wait_ge(s_added, (H1 // PAIR) * NT)
            for s in range(2 * U1 + 2):
                if s < 2 * U1:
                    u = s // 2
                    pe.wait_ge(e_ready, u + 1)
                    if s >= 2:
                        pe.wait_ge(clip_ready, s - 1)
                    gate_up(s, lambda m, c: e_hi[:, u % 3, m, c * P:(c + 1) * P],
                            lambda m, c: e_lo[:, u % 3, m, c * P:(c + 1) * P], gu1_ps)
                if s >= 2:
                    r = s - 2
                    u, half = r // 2, r % 2
                    pe.wait_ge(h1_parts_ready, r + 1)
                    for c in range(NC):
                        cc = slice(c * P, (c + 1) * P)
                        last = mm3(ps[:, 4 + 2 * c + half, :], e_hi[:, u % 3, 2, cc], e_lo[:, u % 3, 2, cc],
                                   h1_hi[:, r % 3, :], h1_lo[:, r % 3, :], u == 0, u == U1 - 1)
                    last.then_inc(dn1_ps, 1)
            pe.wait_ge(fT_ready, 4 * NC)
            for t in range(NT):
                if t >= 2:
                    pe.wait_ge(x_ready, NT + t - 1)
                for c in range(NC):
                    last = pe.transpose(ps[:, t % 2, c * P:(c + 1) * P], f1T[:, c, t * P:(t + 1) * P], ident[:])
                last.then_inc(f_ps, 1)

        @block.scalar
        def _(act):
            def layernorm_sd(layer):
                act.wait_ge(var_ready, layer + 1)
                act.activation(ln_sd[:], ln_var[:], ACT.Sqrt).then_inc(sd_ready, 1)

            def layernorm_hi(layer):
                for k in range(2 * NHALF):
                    half, c = k // NC, k % NC
                    act.wait_ge(xT_ps, 4 * layer + k + 1)
                    act.activation(xT_hi[:, c, half * HALF:(half + 1) * HALF], ps[:, k, :], ACT.Copy)\
                        .then_inc(xT_hi_ready, 1)

            def collect_f(n_dn, dn_done, fT):
                act.wait_ge(dn_done, n_dn)
                for c in range(NC):
                    for half in range(NHALF):
                        act.activation(fT[:, c, half * HALF:(half + 1) * HALF], ps[:, 4 + 2 * c + half, :], ACT.Copy)\
                            .then_inc(fT_ready, 1)

            def bend(J):
                act.wait_ge(nib_ready, J + 1)
                if J >= 1:
                    act.wait_ge(w0_ready, J)
                act.activation(dq_a[:], mag[:], ACT.Relu, bias=consts[:, 0:1]).then_inc(relu_ready, 1)
                act.activation(dq_b[:], mag[:], ACT.Relu, bias=consts[:, 1:2], scale=2.0).then_inc(relu_ready, 1)
                act.activation(dq_m[:], mag[:], ACT.Copy).then_inc(relu_ready, 1)
                act.activation(dq_s[:], sgn[:], ACT.Identity, bias=consts[:, 2:3], scale=-0.125).then_inc(relu_ready, 1)

            def high0(J):
                act.wait_ge(w0_ready, J + 1)
                if J >= 3:
                    act.wait_ge(gu0_ps, 4 * (J - 2))
                act.activation(w0_hi[:, J % 3], w0[:], ACT.Copy).then_inc(w0_hi_ready, 1)

            act.wait_ge(in_wqkv, 16)
            act.activation(wqkv_hi[:], wqkv[:], ACT.Copy).then_inc(wqkv_hi_ready, 1)
            act.wait_ge(consts_ready, 1)
            layernorm_sd(0)
            bend(0)
            layernorm_hi(0)
            for t in range(NT):
                act.wait_ge(qkv_ps, t + 1)
                act.activation(qk_tok[:, t, :], ps[:, 4 + 2 * (t % 2), :], ACT.Copy).then_inc(qk_copied, 1)
                if t == 3:
                    high0(0)
                    bend(1)

            high0(1)
            for s in range(2 * U0 + 1):
                if s < 2 * U0:
                    act.wait_ge(gu0_ps, s + 1)
                    if s >= 3:
                        act.wait_ge(h0_ready, s - 2)
                    act.activation(e0_gu[:, s % 3].rearrange("p m n -> p (m n)"),
                                   psf[:, 1024 * (s % 2):1024 * (s % 2) + 1024], ACT.Copy).then_inc(gu0_copied, 1)
                if s >= 1:
                    r = s - 1
                    act.wait_ge(inner_ready, r + 1)
                    act.activation(e0_b[:, r % 3, :], e0_b[:, r % 3, :], ACT.Tanh, scale=GELU_C * GELU_K)\
                        .then_inc(th0_ready, 1)
                if s % 4 == 1 and s // 4 + 2 < NJ:
                    bend(s // 4 + 2)
                if s % 4 == 3 and s // 4 + 2 < NJ:
                    high0(s // 4 + 2)
                if s == ROPE_STEPS:
                    act.wait_ge(hvar_ready, 1)
                    act.activation(hsd[:], hv[:], ACT.Sqrt).then_inc(hsd_ready, 1)
            collect_f(2 * U0, dn0_ps, f0T)
            for t in range(NT + 1):
                if t < NT:
                    act.wait_ge(qk_ready, t + 1)
                    if t >= 2:
                        act.wait_ge(stk_ps, 4 * (t - 1))
                    for m, places in ((0, slice(0, 4, 2)), (1, slice(0, 2))):
                        src = qk_tok[:, t, m * D:(m + 1) * D].rearrange("p (h a d) -> p h a d", h=H0, a=1)
                        act.activation(stack[:, t % 2, m, :, places, :].bitcast(F32R),
                                       src.to_broadcast((P, H0, 2, D0)), ACT.Copy).then_inc(stk_hi, 1)
                if t >= 1:
                    r = t - 1
                    for q in (0, 2):
                        act.wait_ge(stk_ps, 4 * r + q + 1)
                        act.activation((QT, KT)[q // 2][:, 0:4, r * P:(r + 1) * P],
                                       ps[:, q, :].rearrange("p (i n) -> p i n", i=4), ACT.Copy).then_inc(stk_read_act, 1)
                    act.wait_ge(f_ps, t)
                    if r >= 2:
                        act.wait_ge(g0_ready, r - 1)
                    act.activation(mix0_a[:, r % 2, :], ps[:, 6 + r % 2, 0:D], ACT.Tanh, scale=0.5).then_inc(fth_ready, 1)
            def copy_out0(h):
                act.wait_ge(o0_ps, h + 1)
                if h >= QUAD and h % QUAD == 0:
                    act.wait_ge(o0_turned, h // QUAD)
                act.activation(o_raw[32 * (h % QUAD):32 * (h % QUAD) + D0 + 1, :],
                               psf[0:D0 + 1, 2048 + 1024 * (h % 2):3072 + 1024 * (h % 2)], ACT.Copy).then_inc(o0_copied, 1)

            for h in range(H0):
                for j in range(NT):
                    n = h * NT + j
                    act.wait_ge(s0_ps, n + 1)
                    if j == 0 and h >= 2:
                        act.wait_ge(o0_ps, h - 1)
                    w = (NT - j) * P
                    act.activation(A0[:, h % 2, OFF[j]:OFF[j] + w], psf[:, 1024 * (n % 2):1024 * (n % 2) + w],
                                   ACT.Square).then_inc(s0_sq, 1)
                    if h >= 2 and j == 1:
                        copy_out0(h - 2)
                if h == 0:
                    act.wait_ge(in_wout, 16)
                    act.activation(wout_hi[:], wout[:], ACT.Copy).then_inc(wout_hi_ready, 1)
            copy_out0(H0 - 2)
            copy_out0(H0 - 1)
            for k in range(2 * NHALF):
                half, c = k // NC, k % NC
                act.wait_ge(oT_ps, k + 1)
                act.activation(oT_hi[:, c, half * HALF:(half + 1) * HALF], ps[:, k, :], ACT.Copy).then_inc(oT_hi_ready, 1)

            layernorm_sd(1)
            act.wait_ge(in_router, 48)
            act.activation(rw_hi[:], rw[:], ACT.Copy).then_inc(rw_hi_ready, 1)
            act.wait_ge(in_wv, 16)
            act.activation(wv_hi, wv, ACT.Copy).then_inc(wv_hi_ready, 1)
            layernorm_hi(1)

            def split_wqk(n):
                act.wait_ge(in_wqk[n % 2], 16 * (n // 2 + 1))
                if n >= 2:
                    act.wait_ge(pj_ps, 2 * (n - 1))
                act.activation(wqk_hi[:, n % 2], wqk[:, n % 2], ACT.Copy).then_inc(wqk_hi_ready, 1)

            def split_wo(m):
                act.wait_ge(in_wo[m % 2], 16 * (m // 2 + 1))
                if m >= 1:
                    act.wait_ge(s_ps, NT * m)
                act.activation(wo_hi[:], wo[:, m % 2], ACT.Copy).then_inc(wo_hi_ready, 1)

            def project(n, half):
                i = 2 * n + half
                act.wait_ge(pj_cos, i + 1)
                if i >= 2:
                    act.wait_ge(pj_rot, i - 1)
                b = ps[:, 6 + side_of["project", n, half] % 2, :]
                act.activation(swap[0:64, i % 2, :], b[64:128, :], ACT.Copy).then_inc(pj_swap, 1)
                act.activation(swap[64:128, i % 2, :], b[0:64, :], ACT.Copy).then_inc(pj_swap, 1)

            def project_part(n, half):
                act.wait_ge(pj_rot, 2 * n + half + 1)
                kind, hd = PROJ[n]
                if kind == "q" and hd >= 2:
                    act.wait_ge(s1_ps, NT * (hd - 1))
                if kind == "k" and hd >= 2:
                    act.wait_ge(s1_ps, NT * REP * (hd - 1))
                dst = (q_hi if kind == "q" else k_hi)[:, hd % 2, half * HALF:(half + 1) * HALF]
                act.activation(dst, rot[:, part_of["project", n, half] % 3], ACT.Copy).then_inc(parts_hi, 1)

            def scores(h, j):
                n = h * NT + j
                w = (NT - j) * P
                act.wait_ge(s1_bias, n + 1)
                act.activation(cap[:, n % 2, 0:w], cap[:, n % 2, 0:w], ACT.Tanh, scale=1.0 / (CAP * float(D1) ** 0.5))\
                    .then_inc(act_step, 1)
                act.wait_ge(act_step, n + 1)
                if j == 0 and h >= 2:
                    act.wait_ge(c_ps, 3 * (h - 1))
                act.activation(P1[:, h % 2, OFF[j]:OFF[j] + w], cap[:, n % 2, 0:w], ACT.Exp, scale=CAP)\
                    .then_inc(s1_exp, 1)

            def turn_part(h, half):
                act.wait_ge(cT_read, 2 * h + half + 1)
                if h >= PAIR:
                    act.wait_ge(s_ps, NT * (h // PAIR))
                act.activation(cT_hi[:, h % PAIR, half * HALF:(half + 1) * HALF],
                               rot[:, part_of["turn", h, half] % 3], ACT.Copy).then_inc(parts_hi, 1)

            def router(part):
                if part == 0:
                    act.wait_ge(lg_read, 1)
                    act.activation(r_b[:], r_a[:], ACT.Exp, scale=-1.0).then_inc(sp_a, 1)
                elif part == 1:
                    act.wait_ge(sp_b, 1)
                    act.activation(r_d[:], r_c[:], ACT.Ln).then_inc(sp_a, 1)
                elif part == 2:
                    act.wait_ge(sp_b, 2)
                    act.activation(r_b[:], r_a[:], ACT.Sqrt).then_inc(sp_a, 1)

            for step in ACT_STEPS1:
                {"project": project, "project_part": project_part, "scores": scores, "turn_part": turn_part,
                 "split_wqk": split_wqk, "split_wo": split_wo, "router": router}[step[0]](*step[1:])

            def split_expert(u):
                act.wait_ge(in_ew[u % 3], 16 * (u // 3 + 1))
                if u >= 3:
                    act.wait_ge(dn1_ps, 2 * (u - 2))
                act.activation(e_hi[:, u % 3], eraw[:, u % 3], ACT.Copy).then_inc(e_hi_ready, 1)

            act.wait_ge(s_added, (H1 // PAIR) * NT)
            split_expert(0)
            split_expert(1)
            for s in range(2 * U1 + 1):
                if s < 2 * U1:
                    act.wait_ge(clip_ready, s + 1)
                    if s >= 2:
                        act.wait_ge(h1_ready, s - 1)
                    act.activation(e1_a[:, s % 2, :], gu[:, s % 2, 0, :], ACT.Tanh, scale=0.5).then_inc(th1_ready, 1)
                if s >= 1:
                    r = s - 1
                    act.wait_ge(h1_ready, r + 1)
                    if r >= 3:
                        act.wait_ge(dn1_ps, r - 2)
                    act.activation(h1_hi[:, r % 3, :], h1[:, r % 2, :], ACT.Copy).then_inc(h1_hi_ready, 1)
                if s % 2 == 1 and s // 2 + 2 < U1:
                    split_expert(s // 2 + 2)
            collect_f(2 * U1, dn1_ps, f1T)
            for t in range(NT):
                act.wait_ge(f_ps, NT + t + 1)
                if t >= 2:
                    act.wait_ge(x_ready, NT + t - 1)
                act.activation(mix1_a[:, t % 2, :], ps[:, t % 2, 0:D], ACT.Tanh, scale=0.5).then_inc(fth_ready, 1)

        @block.vector
        def _(dve):
            steps = [0]

            def link(ins):
                steps[0] += 1
                ins.then_inc(vec, 1)
                dve.wait_ge(vec, steps[0])

            def rsqrt(sd, var, r, t):
                link(dve.reciprocal(r, sd))
                link(dve.tensor_tensor(t, r, r, ALU.mult))
                link(dve.tensor_tensor(t, t, var, ALU.mult))
                link(dve.tensor_scalar(t, t, -0.5, 1.5, ALU.mult, ALU.add))
                link(dve.tensor_tensor(r, r, t, ALU.mult))

            def layernorm_stats(layer):
                for t in range(NT):
                    link(dve.bn_stats(ln_stats[:], x_tok[:, t, :]))
                    link(dve.bn_aggr(ln_mv[:, t, :], ln_stats[:]))
                dve.tensor_scalar(ln_var[:], ln_mv[:, :, 1], LN_EPS, None, ALU.add).then_inc(var_ready, 1)

            def layernorm_norm(layer):
                dve.wait_ge(sd_ready, layer + 1)
                rsqrt(ln_sd[:], ln_var[:], ln_r[:], ln_t[:])
                for t in range(NT):
                    dve.tensor_scalar(xn_tok[:, t, :], x_tok[:, t, :], ln_mv[:, t, 0:1], ln_r[:, t:t + 1],
                                      ALU.subtract, ALU.mult).then_inc(xn_ready, 1)

            def layernorm_lo(layer):
                for k in range(2 * NHALF):
                    half, c = k // NC, k % NC
                    dve.wait_ge(xT_hi_ready, 4 * layer + k + 1)
                    tk = slice(half * HALF, (half + 1) * HALF)
                    dve.tensor_tensor(xT_lo[:, c, tk], ps[:, k, :], xT_hi[:, c, tk].bitcast(F32), ALU.subtract)\
                        .then_inc(xT_ready, 1)

            dve.memset(o_raw[:], 0.0)
            for i, v in enumerate((-4.0, -12.0, 0.5, 0.0)):
                last = dve.memset(consts[:, i:i + 1], v)
            last.then_inc(consts_ready, 1)
            dve.memset(V0[:, :, :, D0:D0 + 1], 1.0)

            def nibbles(J):
                dve.wait_ge(in_pk[J % 2], 32 * (J // 2 + 1))
                if J >= 1:
                    dve.wait_ge(relu_ready, 4 * J)
                src = pk[:, J % 2]
                for i, sh in enumerate((0, 4)):
                    dve.tensor_scalar(mag[:, :, i, :], src, sh, 7, ALU.logical_shift_right, ALU.bitwise_and)
                    last = dve.tensor_scalar(sgn[:, :, i, :], src, sh, 8, ALU.logical_shift_right, ALU.bitwise_and)
                last.then_inc(nib_ready, 1)

            dve.wait_ge(in_x, 16)
            layernorm_stats(0)
            nibbles(0)
            layernorm_norm(0)
            dve.wait_ge(wqkv_hi_ready, 1)
            dve.tensor_tensor(wqkv_lo[:], wqkv[:], wqkv_hi[:].bitcast(F32), ALU.subtract).then_inc(wqkv_ready, 1)
            layernorm_lo(0)
            nibbles(1)
            for t in range(NT):
                dve.wait_ge(qkv_ps, t + 1)
                dve.tensor_copy(V0[:, t, :, 0:D0], ps[:, 5 + 2 * (t % 2), 0:D].rearrange("p (h d) -> p h d", h=H0))\
                    .then_inc(v0_copied, 1)

            hd = dict(h=2 * H0)
            ra = rope_a[:].rearrange("p (h d) -> p h d", **hd)
            rb = rope_b[:].rearrange("p (h d) -> p h d", **hd)

            def rope_tile(t):
                dve.wait_ge(qk_copied, t + 1)
                qd = qk_tok[:, t, :].rearrange("p (h d) -> p h d", **hd)
                hf = D0 // 2
                cs = rope0[:, t, 0:1, :].to_broadcast((P, 2 * H0, D0))
                dve.tensor_tensor(ra, qd, cs, ALU.mult)
                dve.tensor_tensor(rb[:, :, 0:hf], qd[:, :, hf:], rope0[:, t, 1:2, 0:hf].to_broadcast((P, 2 * H0, hf)),
                                  ALU.mult)
                link(dve.tensor_tensor(rb[:, :, hf:], qd[:, :, 0:hf],
                                       rope0[:, t, 1:2, hf:].to_broadcast((P, 2 * H0, hf)), ALU.mult))
                link(dve.tensor_tensor(ra, ra, rb, ALU.add))
                link(dve.tensor_reduce(hm[:, 0, :], ra, AX_X, ALU.add))
                link(dve.tensor_scalar(hm[:, 1, :], hm[:, 0, :], 1.0 / D0, None, ALU.mult))
                mean = hm[:, 1, :].rearrange("p (h a) -> p h a", a=1).to_broadcast((P, 2 * H0, D0))
                link(dve.tensor_tensor(qd, ra, mean, ALU.subtract))
                link(dve.tensor_tensor(rb, qd, qd, ALU.mult))
                link(dve.tensor_reduce(hv[:, t, :], rb, AX_X, ALU.add))

            def norm_tile(t):
                qd = qk_tok[:, t, :].rearrange("p (h d) -> p h d", **hd)
                rs = hr[:, t, :].rearrange("p (h a) -> p h a", a=1).to_broadcast((P, 2 * H0, D0))
                link(dve.tensor_tensor(qd, qd, rs, ALU.mult))
                link(dve.tensor_tensor(qd, qd, lns[:, 0:1, :].to_broadcast((P, 2 * H0, D0)), ALU.mult))
                dve.tensor_tensor(qd, qd, lns[:, 1:2, :].to_broadcast((P, 2 * H0, D0)), ALU.add).then_inc(qk_ready, 1)

            dve.wait_ge(in_l0c, 48)
            for s in range(2 * U0 + 1):
                if s < 2 * U0:
                    dve.wait_ge(square_ready, s + 1)
                    if s >= 3:
                        dve.wait_ge(h0_ready, s - 2)
                    dve.scalar_tensor_tensor(out=e0_b[:, s % 3, :], in0=e0_a[:, s % 2, :], scalar=1.0 / GELU_K,
                                             in1=e0_gu[:, s % 3, 0, :], op0=ALU.add, op1=ALU.mult).then_inc(inner_ready, 1)
                if s >= 1:
                    r = s - 1
                    dve.wait_ge(th0_ready, r + 1)
                    link(dve.scalar_tensor_tensor(out=e0_b[:, r % 3, :], in0=e0_b[:, r % 3, :], scalar=1.0,
                                                  in1=e0_gu[:, r % 3, 0, :], op0=ALU.add, op1=ALU.mult))
                    if r >= 3:
                        dve.wait_ge(dn0_ps, r - 2)
                    dve.scalar_tensor_tensor(out=h0[:, r % 3, :], in0=e0_b[:, r % 3, :], scalar=0.5,
                                             in1=e0_gu[:, r % 3, 1, :], op0=ALU.mult, op1=ALU.mult).then_inc(h0_ready, 1)
                if s % 4 == 0 and s // 4 + 2 < NJ:
                    nibbles(s // 4 + 2)
                if s % 2 == 1 and s < ROPE_STEPS:
                    rope_tile(s // 2)
                if s == ROPE_STEPS:
                    dve.tensor_scalar(hv[:], hv[:], 1.0 / D0, LN_EPS, ALU.mult, ALU.add).then_inc(hvar_ready, 1)
                if s == ROPE_STEPS + 2:
                    dve.wait_ge(hsd_ready, 1)
                    rsqrt(hsd[:], hv[:], hr[:], ht[:])
                if s > ROPE_STEPS + 2 and s - ROPE_STEPS - 3 < NT:
                    norm_tile(s - ROPE_STEPS - 3)

            for t in range(NT + 1):
                if t < NT:
                    dve.wait_ge(qk_ready, t + 1)
                    for m, hi, lo in ((0, slice(0, 4, 2), slice(1, 4, 2)), (1, slice(0, 2), slice(2, 4))):
                        dve.wait_ge(stk_hi, 2 * t + m + 1)
                        src = qk_tok[:, t, m * D:(m + 1) * D].rearrange("p (h a d) -> p h a d", h=H0, a=1)
                        last = dve.tensor_tensor(stack[:, t % 2, m, :, lo, :].bitcast(F32R),
                                                 src.to_broadcast((P, H0, 2, D0)), stack[:, t % 2, m, :, hi, :],
                                                 ALU.subtract)
                    last.then_inc(stk_ready, 1)
                if t >= 1:
                    r = t - 1
                    for q in (1, 3):
                        dve.wait_ge(stk_ps, 4 * r + q + 1)
                        dve.tensor_copy((QT, KT)[q // 2][:, 4:8, r * P:(r + 1) * P],
                                        ps[:, q, :].rearrange("p (i n) -> p i n", i=4)).then_inc(stk_read_dve, 1)
                    dve.wait_ge(fth_ready, t)
                    dve.scalar_tensor_tensor(out=g0_tok[:, r, :], in0=mix0_a[:, r % 2, :], scalar=1.0,
                                             in1=ps[:, 6 + r % 2, 0:D], op0=ALU.add, op1=ALU.mult).then_inc(g0_ready, 1)

            def read_out0(g):
                dve.wait_ge(o0_turned, g + 1)
                if g >= 1:
                    dve.wait_ge(o0_ready, g)
                o = psf[:, 3072:4096].rearrange("p (t h d) -> p t h d", t=NT, h=QUAD)
                link(dve.reciprocal(o_rden[:], o[:, :, :, D0:D0 + 1]))
                dst = o_tok[:, :, g * QUAD * D0:(g + 1) * QUAD * D0].rearrange("p t (h d) -> p t h d", h=QUAD)
                dve.tensor_tensor(dst, o[:, :, :, 0:D0], o_rden[:].to_broadcast((P, NT, QUAD, D0)), ALU.mult)\
                    .then_inc(o0_ready, 1)

            for h in range(H0):
                for j in range(NT):
                    n = h * NT + j
                    dve.wait_ge(s0_sq, n + 1)
                    a = A0[:, h % 2, OFF[j]:OFF[j + 1]]
                    dve.tensor_tensor(a, a, a, ALU.mult).then_inc(s0_four, 1)
                    if h >= QUAD and h % QUAD == 1 and j == 5:
                        read_out0(h // QUAD - 1)
                if h == 0:
                    dve.wait_ge(wout_hi_ready, 1)
                    dve.tensor_tensor(wout_lo[:], wout[:], wout_hi[:].bitcast(F32), ALU.subtract).then_inc(wout_ready, 1)
            read_out0(H0 // QUAD - 1)
            for k in range(2 * NHALF):
                half, c = k // NC, k % NC
                tk = slice(half * HALF, (half + 1) * HALF)
                dve.wait_ge(oT_hi_ready, k + 1)
                dve.tensor_tensor(oT_lo[:, c, tk], ps[:, k, :], oT_hi[:, c, tk].bitcast(F32), ALU.subtract)\
                    .then_inc(oT_ready, 1)
            for t in range(NT):
                dve.wait_ge(so_ps, t + 1)
                link(dve.scalar_tensor_tensor(out=mix0_b[:, t % 2, :], in0=ps[:, 4 + t % 2, 0:D], scalar=0.5,
                                              in1=g0_tok[:, t, :], op0=ALU.mult, op1=ALU.mult))
                dve.tensor_tensor(x_tok[:, t, :], x_tok[:, t, :], mix0_b[:, t % 2, :], ALU.add).then_inc(x_ready, 1)

            dve.wait_ge(x_ready, NT)
            layernorm_stats(1)
            layernorm_norm(1)
            dve.wait_ge(rw_hi_ready, 1)
            dve.tensor_tensor(rw_lo[:], rw[:], rw_hi[:].bitcast(F32), ALU.subtract).then_inc(rw_ready, 1)
            dve.memset(V1[:, :, :, D1:D1 + 1], 1.0)
            dve.wait_ge(wv_hi_ready, 1)
            dve.tensor_tensor(wv_lo, wv, wv_hi.bitcast(F32), ALU.subtract).then_inc(wv_ready, 1)
            layernorm_lo(1)
            dve.wait_ge(lg_ps, 1)
            link(dve.tensor_copy(lg[:], ps[:, 6, 0:NT * NE].rearrange("p (t e) -> p t e", t=NT)))
            link(dve.tensor_scalar(r_a[:], lg[:], -1.0, None, ALU.mult))
            dve.tensor_tensor(r_a[:], r_a[:], lg[:], ALU.max).then_inc(lg_read, 1)
            for t in range(NT):
                dve.wait_ge(v_ps, t + 1)
                dve.tensor_copy(V1[:, t, :, 0:D1], ps[:, 4 + t % 2, :].rearrange("p (g d) -> p g d", g=G1))\
                    .then_inc(v_read, 1)
            dve.wait_ge(in_l1c, 64)

            def project(n, half):
                i = 2 * n + half
                tk = slice(half * HALF, (half + 1) * HALF)
                b = ps[:, 6 + side_of["project", n, half] % 2, :]
                dve.wait_ge(pj_ps, i + 1)
                k = part_of["project", n, half]
                if k >= 3:
                    dve.wait_ge(parts_ready, k - 2)
                dve.tensor_tensor(rot[:, k % 3], b, cos1[:, tk], ALU.mult).then_inc(pj_cos, 1)

            def scores(h, j):
                n = h * NT + j
                w = (NT - j) * P
                dve.wait_ge(s1_ps, n + 1)
                if n >= 2:
                    dve.wait_ge(s1_exp, n - 1)
                slope = float(np.float32(2.0) ** np.float32(-(h + 1) * 8.0 / H1))
                dve.scalar_tensor_tensor(out=cap[:, n % 2, 0:w], in0=dist[:, 0:w], scalar=slope,
                                         in1=psf[:, 1024 * (n % 2):1024 * (n % 2) + w], op0=ALU.mult, op1=ALU.add)\
                    .then_inc(s1_bias, 1)

            def context(h, r):
                k = 3 * h + r
                tiles = min(3, NT - 3 * r)
                dve.wait_ge(c_ps, k + 1)
                if k >= 1:
                    dve.wait_ge(c_ready, k)
                if h >= 2 and r == 0:
                    dve.wait_ge(cT_ps, 2 * (h - 1))
                o = ps[:, 4 + k % 2, 0:tiles * (D1 + 1)].rearrange("p (t d) -> p t d", t=tiles)
                link(dve.reciprocal(c_rden[:, 0:tiles], o[:, :, D1:D1 + 1]))
                dve.tensor_tensor(ctx_tok[:, h % 2, 3 * r:3 * r + tiles, :], o[:, :, 0:D1],
                                  c_rden[:, 0:tiles].to_broadcast((P, tiles, D1)), ALU.mult).then_inc(c_ready, 1)

            def turn(h, half):
                k = part_of["turn", h, half]
                dve.wait_ge(cT_ps, 2 * h + half + 1)
                if k >= 3:
                    dve.wait_ge(parts_ready, k - 2)
                dve.tensor_copy(rot[:, k % 3], ps[:, 6 + side_of["turn", h, half] % 2, :]).then_inc(cT_read, 1)

            def add_out(m, t):
                dve.wait_ge(s_ps, NT * m + t + 1)
                if m >= 1 and t == 0:
                    dve.wait_ge(s_added, NT * m)
                dve.tensor_tensor(s_tok[:, t, :], ps[:, 6 + side_of["out", m, t] % 2, 0:D],
                                  bo[:] if m == 0 else s_tok[:, t, :], ALU.add).then_inc(s_added, 1)

            def router(part):
                if part == 0:
                    dve.wait_ge(sp_a, 1)
                    dve.tensor_scalar(r_c[:], r_b[:], 1.0, None, ALU.add).then_inc(sp_b, 1)
                    dve.wait_ge(sp_b, 1)
                    link(dve.tensor_scalar(r_a[:], r_c[:], 1.0, None, ALU.is_equal))
                elif part == 1:
                    dve.wait_ge(sp_a, 2)
                    link(dve.tensor_scalar(r_c[:], r_c[:], -1.0, None, ALU.add))
                    link(dve.tensor_tensor(r_c[:], r_c[:], r_a[:], ALU.add))
                    link(dve.tensor_tensor(r_d[:], r_d[:], r_a[:], ALU.add))
                    link(dve.reciprocal(r_a[:], r_c[:]))
                    link(dve.tensor_tensor(r_d[:], r_d[:], r_b[:], ALU.mult))
                elif part == 2:
                    link(dve.tensor_tensor(r_d[:], r_d[:], r_a[:], ALU.mult))
                    link(dve.tensor_scalar(r_c[:], lg[:], 0.0, None, ALU.max))
                    dve.tensor_tensor(r_a[:], r_d[:], r_c[:], ALU.add).then_inc(sp_b, 1)
                elif part == 3:
                    dve.wait_ge(sp_b, 2)
                    dve.wait_ge(sp_a, 3)
                    link(dve.tensor_scalar(r_c[:], r_b[:], 1e-30, None, ALU.max))
                    link(dve.reciprocal(r_d[:], r_c[:]))
                    link(dve.tensor_tensor(r_d[:], r_d[:], r_a[:], ALU.mult))
                    link(dve.tensor_tensor(r_d[:], r_d[:], r_b[:], ALU.add))
                    link(dve.tensor_scalar(r_b[:], r_d[:], 0.5, None, ALU.mult))
                    eb = ebias[:].rearrange("p (t e) -> p t e", t=1).to_broadcast((P, NT, NE))
                    link(dve.tensor_tensor(r_a[:], r_b[:], eb, ALU.add))
                elif part < 8:
                    for t in (2 * (part - 4), 2 * (part - 4) + 1):
                        link(dve.max(top[:, t, :], r_a[:, t, :]))
                        link(dve.max_index(topi[:, t, :], top[:, t, :], r_a[:, t, :]))
                elif part == 8:
                    link(dve.tensor_copy(topf[:], topi[:]))
                elif part < 9 + TOPK:
                    k = part - 9
                    it = iota[:].rearrange("p (t e) -> p t e", t=1).to_broadcast((P, NT, NE))
                    dst = r_d if k == 0 else r_c
                    link(dve.tensor_tensor(dst[:], it, topf[:, :, k:k + 1].to_broadcast((P, NT, NE)), ALU.is_equal))
                    if k:
                        link(dve.tensor_tensor(r_d[:], r_d[:], r_c[:], ALU.add))
                else:
                    link(dve.tensor_tensor(r_d[:], r_d[:], r_b[:], ALU.mult))
                    link(dve.tensor_reduce(r_sum[:], r_d[:], AX_X, ALU.add))
                    link(dve.tensor_scalar(r_sum[:], r_sum[:], 1e-20, None, ALU.add))
                    link(dve.reciprocal(r_inv[:], r_sum[:]))
                    link(dve.tensor_scalar(r_inv[:], r_inv[:], 0.5, None, ALU.mult))
                    dve.tensor_tensor(r_d[:], r_d[:], r_inv[:].to_broadcast((P, NT, NE)), ALU.mult)\
                        .then_inc(gates_ready, 1)

            def gates(_, half):
                dve.wait_ge(gT_ps, half + 1)
                dve.tensor_copy(gT[:, half * HALF:(half + 1) * HALF], ps[0:NE, 6 + side_of["gates", 0, half] % 2, :])\
                    .then_inc(gT_ready, 1)

            for step in DVE_STEPS1:
                {"project": project, "scores": scores, "turn": turn, "context": context, "out": add_out,
                 "router": router, "gates": gates}[step[0]](*step[1:])

            for s in range(2 * U1):
                b = s % 2
                dve.wait_ge(gu1_ps, s + 1)
                if s >= 2:
                    dve.wait_ge(th1_ready, s - 1)
                    dve.wait_ge(up_ready, s - 1)
                dve.tensor_scalar(gu[:, b].rearrange("p m n -> p (m n)"), psf[:, 1024 * b:1024 * b + 1024], ALPHA, -ALPHA,
                                  ALU.min, ALU.max).then_inc(clip_ready, 1)
                dve.wait_ge(th1_ready, s + 1)
                link(dve.scalar_tensor_tensor(out=e1_a[:, b, :], in0=e1_a[:, b, :], scalar=1.0, in1=gu[:, b, 0, :],
                                              op0=ALU.add, op1=ALU.mult))
                dve.wait_ge(up_ready, s + 1)
                if s >= 2:
                    dve.wait_ge(h1_parts_ready, s - 1)
                dve.tensor_tensor(h1[:, b, :], e1_a[:, b, :], e1_b[:, b, :], ALU.mult).then_inc(h1_ready, 1)
            for t in range(NT):
                dve.wait_ge(fth_ready, NT + t + 1)
                b = t % 2
                link(dve.scalar_tensor_tensor(out=mix1_b[:, b, :], in0=mix1_a[:, b, :], scalar=1.0,
                                              in1=ps[:, b, 0:D], op0=ALU.add, op1=ALU.mult))
                link(dve.scalar_tensor_tensor(out=mix1_b[:, b, :], in0=mix1_b[:, b, :], scalar=0.5,
                                              in1=s_tok[:, t, :], op0=ALU.mult, op1=ALU.mult))
                dve.tensor_tensor(x_tok[:, t, :], x_tok[:, t, :], mix1_b[:, b, :], ALU.add).then_inc(x_ready, 1)

        @block.gpsimd
        def _(pool):
            steps = [0]

            def link(ins):
                steps[0] += 1
                ins.then_inc(pool_step, 1)
                pool.wait_ge(pool_step, steps[0])

            def causal(block_ap, ready, n, done):
                pool.wait_ge(ready, n + 1)
                pool.affine_select(out=block_ap, in_=block_ap, compare_op=ALU.is_ge, fill=0.0, base=0,
                                   pattern=[[1, P]], channel_multiplier=-1).then_inc(done, 1)

            def values0(J, part):
                if part == 0:
                    pool.wait_ge(relu_ready, 4 * J + 4)
                    link(pool.tensor_tensor(dq_a[:], dq_a[:], dq_b[:], ALU.add))
                if part == 1:
                    link(pool.tensor_tensor(dq_a[:], dq_a[:], dq_m[:], ALU.add))
                    link(pool.tensor_tensor(dq_a[:], dq_a[:], dq_s[:], ALU.mult))
                if part == 2:
                    if J >= 1:
                        pool.wait_ge(w0_lo_ready, J)
                    if J >= 3:
                        pool.wait_ge(dn0_ps, 4 * (J - 2))
                    for m in range(3):
                        sc = pks[:, J % 2, m:m + 1, :].to_broadcast((P, 2, 2 * P))
                        dst = w0[:, m] if m < 2 else w0_dn[:, J % 3]
                        last = pool.tensor_tensor(dst, dq_a[:, m], sc, ALU.mult)
                    last.then_inc(w0_ready, 1)
                if part == 3:
                    pool.wait_ge(w0_hi_ready, J + 1)
                    pool.tensor_tensor(w0_lo[:, J % 3], w0[:], w0_hi[:, J % 3].bitcast(F32), ALU.subtract)\
                        .then_inc(w0_lo_ready, 1)

            for J in range(2):
                for part in range(4):
                    values0(J, part)
            for s in range(2 * U0):
                pool.wait_ge(gu0_copied, s + 1)
                if s >= 2:
                    pool.wait_ge(inner_ready, s - 1)
                g = e0_gu[:, s % 3, 0, :]
                pool.tensor_tensor(e0_a[:, s % 2, :], g, g, ALU.mult).then_inc(square_ready, 1)
                J, part = (s - 1) // 4 + 2, (s - 1) % 4
                if s >= 1 and J < NJ:
                    values0(J, part)

            for h in range(H0):
                for j in range(NT):
                    causal(A0[:, h % 2, OFF[j]:OFF[j] + P], s0_four, h * NT + j, s0_mask)

            def scores(h, j):
                causal(P1[:, h % 2, OFF[j]:OFF[j] + P], s1_exp, h * NT + j, s1_mask)

            def split_wqk(n):
                pool.wait_ge(wqk_hi_ready, n + 1)
                pool.tensor_tensor(wqk_lo[:, n % 2], wqk[:, n % 2], wqk_hi[:, n % 2].bitcast(F32), ALU.subtract)\
                    .then_inc(wqk_ready, 1)

            def split_wo(m):
                pool.wait_ge(wo_hi_ready, m + 1)
                pool.tensor_tensor(wo_lo[:], wo[:, m % 2], wo_hi[:].bitcast(F32), ALU.subtract).then_inc(wo_ready, 1)

            def project(n, half):
                i = 2 * n + half
                r = rot[:, part_of["project", n, half] % 3]
                pool.wait_ge(pj_swap, 2 * i + 2)
                if i == 0:
                    pool.wait_ge(in_l1c, 64)
                link(pool.tensor_tensor(swap[:, i % 2, :], swap[:, i % 2, :], sin1[:, half * HALF:(half + 1) * HALF],
                                        ALU.mult))
                pool.wait_ge(pj_cos, i + 1)
                pool.tensor_tensor(r, r, swap[:, i % 2, :], ALU.add).then_inc(pj_rot, 1)

            def low_part(step, hi, lo):
                pool.wait_ge(parts_hi, part_of[step] + 1)
                pool.tensor_tensor(lo, rot[:, part_of[step] % 3], hi.bitcast(F32), ALU.subtract).then_inc(parts_ready, 1)

            def project_part(n, half):
                kind, hd = PROJ[n]
                hi, lo = ((q_hi, q_lo) if kind == "q" else (k_hi, k_lo))
                tk = slice(half * HALF, (half + 1) * HALF)
                low_part(("project", n, half), hi[:, hd % 2, tk], lo[:, hd % 2, tk])

            def turn_part(h, half):
                tk = slice(half * HALF, (half + 1) * HALF)
                low_part(("turn", h, half), cT_hi[:, h % PAIR, tk], cT_lo[:, h % PAIR, tk])

            for step in POOL_STEPS1:
                {"project": project, "project_part": project_part, "scores": scores, "turn_part": turn_part,
                 "split_wqk": split_wqk, "split_wo": split_wo}[step[0]](*step[1:])

            def low(u):
                pool.wait_ge(e_hi_ready, u + 1)
                pool.tensor_tensor(e_lo[:, u % 3], eraw[:, u % 3], e_hi[:, u % 3].bitcast(F32), ALU.subtract)\
                    .then_inc(e_ready, 1)

            def low_h(r):
                pool.wait_ge(h1_hi_ready, r + 1)
                pool.tensor_tensor(h1_lo[:, r % 3, :], h1[:, r % 2, :], h1_hi[:, r % 3, :].bitcast(F32), ALU.subtract)\
                    .then_inc(h1_parts_ready, 1)

            low(0)
            low(1)
            for s in range(2 * U1 + 1):
                if s < 2 * U1:
                    b, u, half = s % 2, s // 2, s % 2
                    pool.wait_ge(clip_ready, s + 1)
                    if s >= 2:
                        pool.wait_ge(h1_ready, s - 1)
                    if u < NE:
                        pool.wait_ge(in_pb[u % 2], 16 * (u // 2 + 1))
                        pool.tensor_tensor(e1_b[:, b, :], gu[:, b, 1, :], pb[:, u % 2, half * HALF:(half + 1) * HALF],
                                           ALU.mult).then_inc(up_ready, 1)
                    else:
                        pool.tensor_scalar(e1_b[:, b, :], gu[:, b, 1, :], 0.5, None, ALU.mult).then_inc(up_ready, 1)
                if s >= 1:
                    low_h(s - 1)
                if s % 2 == 1 and s // 2 + 2 < U1:
                    low(s // 2 + 2)


ROPE_STEPS = 2 * NT
ROUTER = {"act": [0, 4, 10], "dve": [2, 6, 8, 12] + [14 + 2 * i for i in range(10)]}
GATES_AT = 6
PROJ = [p for g in range(G1) for p in [("k", g)] + [("q", g * REP + i) for i in range(REP)]]


def schedule():
    steps = []
    first = PROJ.index(("q", 0))
    for n in range(first + 1):
        steps += [("project", n, 0), ("project", n, 1)]
    for h in range(H1 + 1):
        todo = []
        if h + 1 < H1:
            at = PROJ.index(("q", h + 1))
            if (h + 1) % REP == 0:
                todo += [("project", at - 1, 0), ("project", at - 1, 1)]
            todo += [("project", at, 0), ("project", at, 1)]
        for j in range(NT):
            if h < H1:
                steps.append(("scores", h, j))
            if h >= 1:
                steps.append(("context", h - 1, j))
            if todo:
                steps.append(todo.pop(0))
            if h >= 2 and j in (4, 5):
                steps.append(("turn", h - 2, j - 4))
            if h >= PAIR + 1 and (h - 2) % PAIR == PAIR - 1 and j >= 6:
                steps += [("out", (h - 2) // PAIR, 2 * (j - 6)), ("out", (h - 2) // PAIR, 2 * (j - 6) + 1)]
            if h >= PAIR + 2 and (h - 2) % PAIR == 0 and j < 4:
                steps.append(("out", (h - 2) // PAIR - 1, 4 + j))
            if h == GATES_AT and j in (6, 7):
                steps.append(("gates", 0, j - 6))
    steps += [("turn", H1 - 1, 0), ("turn", H1 - 1, 1)]
    steps += [("out", H1 // PAIR - 1, t) for t in range(NT)]
    return steps


STEPS1 = schedule()
SIDE = [s for s in STEPS1 if s[0] in ("project", "turn", "out", "gates")]
side_of = {s: n for n, s in enumerate(SIDE)}
part_of = {s: n for n, s in enumerate([s for s in STEPS1 if s[0] in ("project", "turn")])}


def follow(engine):
    out, later = [], []
    if engine != "dve":
        out += [("split_wqk", 0), ("split_wqk", 1)]
    for n, s in enumerate(STEPS1):
        name = s[0]
        if name == "scores" and s[2] == 0:
            out += later
            later = []
        if name == "scores":
            out.append(s)
            if engine in ROUTER and NT * s[1] + s[2] in ROUTER[engine]:
                out.append(("router", ROUTER[engine].index(NT * s[1] + s[2])))
        elif name == "context":
            if engine == "dve" and (s[2] % 3 == 2 or s[2] == NT - 1):
                out.append(("context", s[1], s[2] // 3))
        elif name in ("project", "turn"):
            if engine == "dve" or name == "project":
                out.append(s)
            if engine != "dve":
                later.append((name + "_part", *s[1:]))
                if name == "project" and s[2] == 1 and s[1] + 2 < len(PROJ):
                    later.append(("split_wqk", s[1] + 2))
                if s == ("turn", 0, 0):
                    later.append(("split_wo", 0))
        elif name in ("out", "gates"):
            if engine == "dve":
                out.append(s)
            elif name == "out" and s[2] == NT - 1 and s[1] + 1 < H1 // PAIR:
                later.append(("split_wo", s[1] + 1))
        if name == "scores" or not any(x[0] == "scores" for x in STEPS1[:n]) or \
                not any(x[0] == "scores" for x in STEPS1[n:]):
            out += later
            later = []
    return out


ACT_STEPS1 = follow("act")
DVE_STEPS1 = follow("dve")
POOL_STEPS1 = follow("pool")


def kernel(**inputs):
    import numpy as _np
    import concourse.bacc as _bacc
    from concourse import mybir as _mybir
    from concourse.bass_utils import run_bass_kernel_spmd as _run

    a = {k: _np.asarray(v) for k, v in inputs.items()}
    inv0 = (_np.float32(1.0) / _np.power(_np.float32(10000.0), _np.arange(0, D0, 2, dtype=_np.float32) / _np.float32(D0))).astype(_np.float32)
    ang0 = _np.arange(TOK, dtype=_np.float32)[:, None] * inv0[None, :]
    c0, s0 = _np.cos(ang0), _np.sin(ang0)
    rope0 = _np.stack([_np.concatenate([c0, c0], 1), _np.concatenate([-s0, s0], 1)], 1).astype(_np.float32)
    rope0 = rope0.reshape(NT, P, 2, D0).transpose(1, 0, 2, 3)
    inv1 = (_np.float32(1.0) / _np.power(_np.float32(10000.0), _np.arange(0, D1, 2, dtype=_np.float32) / _np.float32(D1))).astype(_np.float32)
    ang1 = (_np.arange(TOK, dtype=_np.float32)[:, None] * inv1[None, :]).T
    c1, s1 = _np.cos(ang1), _np.sin(ang1)
    consts = {
        "ident": _np.eye(P, dtype=_np.float32),
        "rope0": rope0,
        "cos1": _np.concatenate([c1, c1], 0),
        "sin1": _np.concatenate([-s1, s1], 0),
        "dist": (_np.arange(P)[:, None] - _np.arange(TOK)[None, :]).astype(_np.float32),
        "iota": _np.tile(_np.arange(NE, dtype=_np.float32), (P, 1)),
    }

    def blocks(w):
        return w.T.reshape(w.shape[1], NJ, P, 2).transpose(1, 0, 3, 2).reshape(NJ, w.shape[1], 2 * P)

    def rows(v):
        return _np.repeat(v, P // v.shape[1], axis=1)

    def heads(w, n):
        return w.reshape(P, NC, n, D1 // 2, 2).transpose(2, 0, 1, 4, 3).reshape(n, P, NC * D1)

    def chunks(w):
        return w.transpose(0, 2, 1).reshape(len(w), P, D)

    def with_shared(name):
        return _np.concatenate([a[f"L1_ffn_{name}_w"], a[f"L1_ffn_shared_{name}_w"][None]], 0)

    wq, wk = heads(a["L1_attn_Wq"], H1), heads(a["L1_attn_Wk"], G1)
    feeds = {
        "x": a["L0_attn_x"].reshape(TOK, D), "wqkv": a["L0_attn_w_qkv"], "wout": a["L0_attn_w_out"],
        "lns": a["L0_attn_ln_scale"], "lnb": a["L0_attn_ln_bias"],
        "packed": _np.stack([blocks(a["L0_ffn_gate_W_packed"]), blocks(a["L0_ffn_up_W_packed"]),
                             a["L0_ffn_down_W_packed"].T.reshape(NJ, P, D)], 2),
        "scales": _np.stack([rows(blocks(a["L0_ffn_gate_scales"])), rows(blocks(a["L0_ffn_up_scales"])),
                             rows(a["L0_ffn_down_scales"].T.reshape(NJ, D // BLK, D))], 2),
        "wqk": _np.stack([(wq if kind == "q" else wk)[i] for kind, i in PROJ]), "wv": a["L1_attn_Wv"],
        "wo": a["L1_attn_Wo"], "bo": a["L1_attn_bo"],
        "rw": a["L1_ffn_router_w"].T.reshape(P, NC, NE), "eb": a["L1_ffn_expert_bias"],
        "experts": _np.stack([chunks(with_shared("gate")), chunks(with_shared("up")),
                              with_shared("down").transpose(0, 2, 1)], 2),
        **consts,
    }
    nc = _bacc.Bacc("TRN2", target_bir_lowering=False, num_devices=1)
    arrays, args = {}, []
    for name, v in feeds.items():
        v = _np.ascontiguousarray(v)
        arrays[f"in_{name}"] = v
        args.append(nc.dram_tensor(f"in_{name}", v.shape, _mybir.dt.from_np(v.dtype), kind="ExternalInput").ap())
    out = nc.dram_tensor("out", (1, TOK, D), F32, kind="ExternalOutput").ap()
    build_program(nc, *args, out)
    r = _run(nc, [arrays], core_ids=[0])
    return r.results[0]["out"]
```

```python
from contextlib import ExitStack

import numpy as np

import concourse.bass as bass
from concourse import mybir

ALU = mybir.AluOpType
ACT = mybir.ActivationFunctionType
F32 = mybir.dt.float32
F32R = mybir.dt.float32r
BF16 = mybir.dt.bfloat16
I32 = mybir.dt.int32
U32 = mybir.dt.uint32
AX_X = mybir.AxisListType.X

P = 128
TOK = 1024
NT = TOK // P
D = 256
NC = D // P
HALF = 512
NHALF = TOK // HALF
LN_EPS = 1e-5

H0, D0 = 16, 16
STK = 4 * D0
SPLIT = 3
HIGH_AT, LOW_AT, OWN_AT, LAG = (2, 4), (2, 4), 5, 1
QUAD = 4
MLP = 2048
NJ = MLP // (2 * P)
U0 = MLP // P
BLK = 32
GELU_C, GELU_K = 0.7978845608028654, 0.044715
H1, G1, D1 = 16, 4, 128
REP = H1 // G1
CAP = 30.0
PAIR = 2
NE, TOPK, ALPHA = 32, 4, 7.0
U1 = NE + 1

OFF = [sum((NT - i) * P for i in range(j)) for j in range(NT + 1)]
TRI = OFF[NT]


def block_at(s, k):
    J = (s - k) // 4 + 2
    return J if (s - k) % 4 == 0 and 1 <= J < NJ else 0


def tile_at(s, k):
    t = (s - k) // 4 * 2 + (s - k) % 4
    return t if s >= k and (s - k) % 4 < 2 and t < NT else None


def spans(width):
    return [(a, min(a + HALF, width)) for a in range(0, width, HALF)]



def build_program(nc, x_in, wqkv_in, wout_in, lns_in, lnb_in, packed_in, scales_in,
                  wqk_in, wv_in, wo_in, bo_in, rw_in, eb_in, experts_in,
                  ident_in, rope0_in, cos1_in, sin1_in, dist_in, iota_in, out):
    gates_dram = nc.dram_tensor("gates_scratch", (NE, TOK), F32, kind="Internal").ap()

    with ExitStack() as ctx:
        def sem(name):
            return ctx.enter_context(nc.semaphore(name))

        def alloc(scope):
            return lambda name, shape, dt=F32: scope.enter_context(nc.sbuf_tensor(name, shape, dt))

        sb = alloc(ctx)
        ident = sb("ident", [P, P])
        x_tok = sb("x_tok", [P, NT, D])
        xn_tok = sb("xn_tok", [P, NT, D])
        xT_hi = sb("xT_hi", [P, NC, TOK], F32R)
        xT_lo = sb("xT_lo", [P, NC, TOK], F32R)
        s_tok = sb("s_tok", [P, NT, D])
        ln_stats = sb("ln_stats", [P, 2, 6])
        ln_mv = sb("ln_mv", [P, NT, 2])
        ln_var = sb("ln_var", [P, NT])
        ln_sd = sb("ln_sd", [P, NT])
        ln_r = sb("ln_r", [P, NT])
        ln_t = sb("ln_t", [P, NT])
        consts = sb("consts", [P, 1])

        l0 = ExitStack()
        sb = alloc(l0)
        V0 = sb("V0", [P, NT, H0, D0 + 1])
        qk_tok = sb("qk_tok", [P, NT, 2 * D])
        wout = sb("wout", [P, NC, D])
        wout_hi = sb("wout_hi", [P, NC, D], F32R)
        wout_lo = sb("wout_lo", [P, NC, D], F32R)
        rope0 = sb("rope0", [P, NT, 2, D0])
        hv = sb("hv", [P, NT, 2 * H0])
        hsd = sb("hsd", [P, NT, 2 * H0])
        hr = sb("hr", [P, NT, 2 * H0])
        ht = sb("ht", [P, NT, 2 * H0])
        hm = sb("hm", [P, 2, 2 * H0])
        lns = sb("lns", [P, 2, D0])
        o_raw = sb("o_raw", [P, TOK])
        o_rden = sb("o_rden", [P, NT, QUAD, 1])
        mix0_a = sb("mix0_a", [P, 2, D])
        mix0_b = sb("mix0_b", [P, 2, D])
        g0_tok = s_tok
        o_tok = xn_tok
        oT_hi, oT_lo = xT_hi, xT_lo

        l0m = ExitStack()
        sb = alloc(l0m)
        rope_a = sb("rope_a", [P, 2, 2 * D])
        rope_b = sb("rope_b", [P, 2, 2 * D])
        pk = sb("pk", [P, 2, 3, 2 * P], I32)
        pks = sb("pks", [P, 2, 3, 2 * P])
        mag = sb("mag", [P, 3, 2, 2 * P], I32)
        sgn = sb("sgn", [P, 3, 2, 2 * P], I32)
        dq_a = sb("dq_a", [P, 3, 2, 2 * P], BF16)
        dq_b = sb("dq_b", [P, 3, 2, 2 * P], BF16)
        dq_m = sb("dq_m", [P, 3, 2, 2 * P], BF16)
        dq_s = sb("dq_s", [P, 3, 2, 2 * P], BF16)
        w0 = sb("w0", [P, 2, 2, 2 * P])
        w0_hi = sb("w0_hi", [P, 3, 2, 2, 2 * P], F32R)
        w0_lo = sb("w0_lo", [P, 3, 2, 2, 2 * P], F32R)
        w0_dn = sb("w0_dn", [P, 3, 2, 2 * P])
        l0w = ExitStack()
        sb = alloc(l0w)
        wqkv = sb("wqkv", [P, NC, 3 * D])
        wqkv_hi = sb("wqkv_hi", [P, NC, 3 * D], F32R)
        wqkv_lo = sb("wqkv_lo", [P, NC, 3 * D], F32R)
        l0w.close()
        l0w = ExitStack()
        sb = alloc(l0w)
        e0_gu = sb("e0_gu", [P, 3, 2, HALF])
        e0_a = sb("e0_a", [P, 2, HALF])
        e0_b = sb("e0_b", [P, 3, HALF])
        e0_p = sb("e0_p", [P, 3, HALF])
        h0 = sb("h0", [P, 3, HALF])
        f0T = sb("f0T", [P, NC, TOK])
        l0w.close()
        l0m.close()

        l0a = ExitStack()
        sb = alloc(l0a)
        stack = sb("stack", [P, 2, 2, H0, 4, D0])
        QT = sb("QT", [P, H0 // 2, TOK], F32R)
        KT = sb("KT", [P, H0 // 2, TOK], F32R)
        A0 = sb("A0", [P, 2, TRI - OFF[SPLIT]])
        A0_lo = sb("A0_lo", [P, 2, OFF[SPLIT]], F32R)
        A0_raw = qk_tok[:].rearrange("p t n -> p (t n)")
        stack_flat = stack[:].rearrange("p b m h a d -> p (b m h a d)").bitcast(F32R)
        xT_flat = [xT_hi[:].rearrange("p c n -> p (c n)"), xT_lo[:].rearrange("p c n -> p (c n)")]
        VW = SPLIT * H0 * (D0 + 1)
        V0_hi, V0_lo = (v[:, v.shape[1] - VW:].rearrange("p (t h d) -> p t h d", t=SPLIT, h=H0)
                        for v in (xT_flat[1], stack_flat))

        def A0_row(h, j):
            if j < SPLIT:
                return A0_raw[:, OFF[j]:OFF[j + 1]]
            return A0[:, h % 2, OFF[j] - OFF[SPLIT]:OFF[j + 1] - OFF[SPLIT]]

        def A0_hi(h, j, a, e):
            if h % 2:
                return stack_flat[:, OFF[j] + a:OFF[j] + e]
            o = OFF[j] - (OFF[2] if j >= 2 else 0)
            return xT_flat[j // 2][:, o + a:o + e]
        l0a.close()
        l0.close()

        l1 = ExitStack()
        sb = alloc(l1)
        eraw = sb("eraw", [P, 3, 3, D])
        l1a = ExitStack()
        sb = alloc(l1a)
        cos1 = sb("cos1", [P, TOK])
        sin1 = sb("sin1", [P, TOK])
        dist = sb("dist", [P, TOK])
        wqk = sb("wqk", [P, 2, NC, D1])
        wqk_hi = sb("wqk_hi", [P, 2, NC, D1], F32R)
        wqk_lo = sb("wqk_lo", [P, 2, NC, D1], F32R)
        q_hi = sb("q_hi", [P, 2, TOK], F32R)
        q_lo = sb("q_lo", [P, 2, TOK], F32R)
        k_hi = sb("k_hi", [P, 2, TOK], F32R)
        k_lo = sb("k_lo", [P, 2, TOK], F32R)
        V1 = sb("V1", [P, NT, G1, D1 + 1])
        P1 = sb("P1", [P, 2, TRI])
        cap = sb("cap", [P, 2, TOK])
        swap = sb("swap", [P, 2, HALF])
        rot = sb("rot", [P, 3, HALF])
        c_rden = sb("c_rden", [P, 3, 1])
        ctx_tok = sb("ctx_tok", [P, 2, NT, D1])
        cT_hi = sb("cT_hi", [P, PAIR, TOK], F32R)
        cT_lo = sb("cT_lo", [P, PAIR, TOK], F32R)
        wo = sb("wo", [P, 2, PAIR, D])
        wo_hi = sb("wo_hi", [P, PAIR, D], F32R)
        wo_lo = sb("wo_lo", [P, PAIR, D], F32R)
        bo = sb("bo", [P, D])
        wv = P1[:, 0, 0:NC * G1 * D1].rearrange("p (c n) -> p c n", c=NC)
        wv_hi = q_hi[:, 1, :].rearrange("p (c n) -> p c n", c=NC)
        wv_lo = q_lo[:, 1, :].rearrange("p (c n) -> p c n", c=NC)
        rw = sb("rw", [P, NC, NE])
        rw_hi = sb("rw_hi", [P, NC, NE], F32R)
        rw_lo = sb("rw_lo", [P, NC, NE], F32R)
        ebias = sb("ebias", [P, NE])
        iota = sb("iota", [P, NE])
        lg, r_a, r_b, r_c, r_d = (xn_tok[:, i, :].rearrange("p (t e) -> p t e", t=NT) for i in range(5))
        lgT = s_tok[0:NE, 0:4, :].rearrange("e t n -> e (t n)")
        gT = xn_tok[0:NE, 0:4, :].rearrange("e t n -> e (t n)")
        top = sb("top", [P, NT, 8])
        topi = sb("topi", [P, NT, 8], U32)
        topf = sb("topf", [P, NT, 8])
        r_sum = sb("r_sum", [P, NT, 1])
        r_inv = sb("r_inv", [P, NT, 1])
        l1a.close()

        l1b = ExitStack()
        sb = alloc(l1b)
        pb = sb("pb", [P, 2, TOK])
        e_hi = sb("e_hi", [P, 3, 3, D], F32R)
        e_lo = sb("e_lo", [P, 3, 3, D], F32R)
        gu = sb("gu", [P, 2, 2, HALF])
        e1_a = sb("e1_a", [P, 2, HALF])
        e1_b = sb("e1_b", [P, 2, HALF])
        h1 = sb("h1", [P, 2, HALF])
        h1_hi = sb("h1_hi", [P, 3, HALF], F32R)
        h1_lo = sb("h1_lo", [P, 3, HALF], F32R)
        f1T = sb("f1T", [P, NC, TOK])
        mix1_a = sb("mix1_a", [P, 4, D])
        mix1_b = sb("mix1_b", [P, 4, D])
        l1b.close()
        l1.close()

        ps = ctx.enter_context(nc.psum_tensor("ps", [P, 8, HALF], F32))
        psf = ps[:, :, :].rearrange("p b n -> p (b n)")

        in_x, in_const, in_wqkv, in_l0c = [sem("in_x0"), sem("in_x1")], sem("in_const"), sem("in_wqkv"), sem("in_l0c")
        in_wout, in_pk, in_l1c = sem("in_wout"), [sem("in_pk0"), sem("in_pk1")], sem("in_l1c")
        in_wqk, in_wo, in_wv = [sem("in_wqk0"), sem("in_wqk1")], [sem("in_wo0"), sem("in_wo1")], sem("in_wv")
        in_router = sem("in_router")
        in_ew = [sem("in_ew0"), sem("in_ew1"), sem("in_ew2")]
        in_pb = [sem("in_pb0"), sem("in_pb1")]
        vec = sem("vec")
        pool_step = sem("pool_step")
        act_step = sem("act_step")
        consts_ready = sem("consts_ready")
        var_ready, sd_ready, xn_ready = sem("var_ready"), sem("sd_ready"), sem("xn_ready")
        xT_ps, xT_hi_ready, xT_ready = sem("xT_ps"), sem("xT_hi_ready"), sem("xT_ready")
        wqkv_hi_ready, wqkv_ready = sem("wqkv_hi_ready"), sem("wqkv_ready")
        qkv_ps = sem("qkv_ps")
        hvar_ready, hsd_ready = sem("hvar_ready"), sem("hsd_ready")
        qk_ready, stk_hi, stk_ready, stk_ps = sem("qk_ready"), sem("stk_hi"), sem("stk_ready"), sem("stk_ps")
        s0_ps, s0_sq, s0_four, s0_mask = sem("s0_ps"), sem("s0_sq"), sem("s0_four"), sem("s0_mask")
        a0_hi, a0_ready, a0_own = sem("a0_hi"), sem("a0_ready"), sem("a0_own")
        v0_hi_ready, v0_ready = sem("v0_hi_ready"), sem("v0_ready")
        o0_ps, o0_copied, o0_turned, o0_ready = sem("o0_ps"), sem("o0_copied"), sem("o0_turned"), sem("o0_ready")
        wout_hi_ready, wout_ready = sem("wout_hi_ready"), sem("wout_ready")
        oT_ps, oT_hi_ready, oT_ready = sem("oT_ps"), sem("oT_hi_ready"), sem("oT_ready")
        so_ps = sem("so_ps")
        qk_split, qk_centred, qk_squared, qk_scaled = (sem("qk_split"), sem("qk_centred"), sem("qk_squared"),
                                                      sem("qk_scaled"))
        qk_var = sem("qk_var")
        ladder_ready, gated_ready = sem("ladder_ready"), sem("gated_ready")
        nib_ready, num_ready, w0_ready, w0_hi_ready, w0_lo_ready = (
            sem("nib_ready"), sem("num_ready"), sem("w0_ready"), sem("w0_hi_ready"), sem("w0_lo_ready"))
        gu0_copied, square_ready, g0_ready = sem("gu0_copied"), sem("square_ready"), sem("g0_ready")
        stk_k_ready, xn_act_ready = sem("stk_k_ready"), sem("xn_act_ready")
        stk_read_act, stk_read_dve = sem("stk_read_act"), sem("stk_read_dve")
        qk_copied, v0_copied = sem("qk_copied"), sem("v0_copied")
        gu0_ps, inner_ready, th0_ready, h0_ready, dn0_ps = (
            sem("gu0_ps"), sem("inner_ready"), sem("th0_ready"), sem("h0_ready"), sem("dn0_ps"))
        fT_ready, f_ps, fth_ready, x_ready = sem("fT_ready"), sem("f_ps"), sem("fth_ready"), sem("x_ready")
        table_ready = sem("table_ready")
        mixed, shift_ready = sem("mixed"), sem("shift_ready")
        wv_hi_ready, wv_ready, v_ps, v_read = sem("wv_hi_ready"), sem("wv_ready"), sem("v_ps"), sem("v_read")
        wqk_hi_ready, wqk_ready = sem("wqk_hi_ready"), sem("wqk_ready")
        pj_ps, pj_cos, pj_rot = sem("pj_ps"), sem("pj_cos"), sem("pj_rot")
        parts_hi, parts_ready = sem("parts_hi"), sem("parts_ready")
        s1_ps, s1_bias, s1_exp, s1_mask = sem("s1_ps"), sem("s1_bias"), sem("s1_exp"), sem("s1_mask")
        c_ps, c_ready = sem("c_ps"), sem("c_ready")
        cT_ps, cT_read = sem("cT_ps"), sem("cT_read")
        wo_hi_ready, wo_ready = sem("wo_hi_ready"), sem("wo_ready")
        s_ps, s_added = sem("s_ps"), sem("s_added")
        lgT_ps, lgT_copied = sem("lgT_ps"), sem("lgT_copied")
        rw_hi_ready, rw_ready, lg_ps, lg_read = sem("rw_hi_ready"), sem("rw_ready"), sem("lg_ps"), sem("lg_read")
        sp_a, sp_b, gates_ready = sem("sp_a"), sem("sp_b"), sem("gates_ready")
        gT_ps, gT_ready, gates_out = sem("gT_ps"), sem("gT_ready"), sem("gates_out")
        e_hi_ready, e_ready, h1_hi_ready, h1_parts_ready = (sem("e_hi_ready"), sem("e_ready"), sem("h1_hi_ready"),
                                                            sem("h1_parts_ready"))
        gu1_ps, clip_ready, th1_ready, up_ready, h1_ready, dn1_ps = (
            sem("gu1_ps"), sem("clip_ready"), sem("th1_ready"), sem("up_ready"), sem("h1_ready"), sem("dn1_ps"))
        out_sent = sem("out_sent")

        block = ctx.enter_context(nc.Block())

        @block.sync
        def _(sp):
            def to_all(v, n):
                return v.rearrange("(a n) -> a n", a=1).to_broadcast((P, n))

            for i in range(2):
                sp.dma_start(x_tok[:, 4 * i:4 * i + 4, :], x_in[i * HALF:(i + 1) * HALF, :].rearrange("(t p) d -> p t d", p=P))\
                    .then_inc(in_x[i], 16)
            sp.dma_start(ident[:], ident_in).then_inc(in_const, 16)
            sp.dma_start(wqkv[:], wqkv_in.rearrange("(p c) n -> p c n", c=NC)).then_inc(in_wqkv, 16)
            for J in range(NJ):
                if J >= 2:
                    sp.wait_ge(w0_ready, J - 1)
                b = J % 2
                sp.dma_start(pk[:, b], packed_in[J]).then_inc(in_pk[b], 16)
                sp.dma_start(pks[:, b], scales_in[J]).then_inc(in_pk[b], 16)
                if J == 1:
                    sp.dma_start(rope0[:], rope0_in).then_inc(in_l0c, 16)
                    sp.dma_start(lns[:, 0, :], to_all(lns_in, D0)).then_inc(in_l0c, 16)
                    sp.dma_start(lns[:, 1, :], to_all(lnb_in, D0)).then_inc(in_l0c, 16)
                    sp.dma_start(wout[:], wout_in.rearrange("(c p) n -> p c n", p=P)).then_inc(in_wout, 16)
            sp.wait_ge(x_ready, NT)
            for n in range(2):
                sp.dma_start(wqk[:, n], wqk_in[n]).then_inc(in_wqk[n], 16)
            sp.dma_start(rw[:], rw_in).then_inc(in_router, 16)
            sp.dma_start(ebias[:], to_all(eb_in, NE)).then_inc(in_router, 16)
            sp.dma_start(iota[:], iota_in).then_inc(in_router, 16)
            sp.dma_start(wv, wv_in.rearrange("(p c) n -> p c n", c=NC)).then_inc(in_wv, 16)
            sp.dma_start(cos1[:], cos1_in).then_inc(in_l1c, 16)
            sp.dma_start(sin1[:], sin1_in).then_inc(in_l1c, 16)
            sp.dma_start(dist[:], dist_in).then_inc(in_l1c, 16)
            sp.dma_start(bo[:], to_all(bo_in, D)).then_inc(in_l1c, 16)
            for u in range(3):
                sp.dma_start(eraw[:, u], experts_in[u]).then_inc(in_ew[u], 16)

            def load_wo(m):
                if m >= 2:
                    sp.wait_ge(wo_ready, m - 1)
                sp.dma_start(wo[:, m % 2], wo_in[m * PAIR * D1:(m + 1) * PAIR * D1, :].rearrange("(h p) n -> p h n", p=P))\
                    .then_inc(in_wo[m % 2], 16)

            for n, (kind, i) in enumerate(PROJ):
                if n >= 2:
                    sp.wait_ge(wqk_ready, n - 1)
                    sp.dma_start(wqk[:, n % 2], wqk_in[n]).then_inc(in_wqk[n % 2], 16)
                if kind == "q" and i % PAIR == 0 and i >= PAIR:
                    load_wo(i // PAIR - 1)
            load_wo(H1 // PAIR - 1)
            sp.wait_ge(gT_ready, 2)
            sp.dma_start(gates_dram, gT).then_inc(gates_out, 16)
            sp.wait_ge(gates_out, 16)
            sp.wait_ge(s1_exp, NT * H1)
            for u in range(U1):
                if u < NE:
                    if u >= 2:
                        sp.wait_ge(up_ready, 2 * (u - 1))
                    sp.dma_start(pb[:, u % 2], gates_dram[u:u + 1, :].to_broadcast((P, TOK))).then_inc(in_pb[u % 2], 16)
                if u + 3 < U1:
                    sp.wait_ge(e_ready, u + 1)
                    sp.dma_start(eraw[:, u % 3], experts_in[u + 3]).then_inc(in_ew[u % 3], 16)
            for t in range(NT):
                sp.wait_ge(x_ready, NT + t + 1)
                sp.dma_start(out[0, t * P:(t + 1) * P, :], x_tok[:, t, :]).then_inc(out_sent, 16)
            sp.wait_ge(out_sent, 16 * NT)

        @block.tensor
        def _(pe):
            def mm3(o, l_hi, l_lo, r_hi, r_lo, start, stop):
                pe.matmul(o, l_hi, r_hi, start=start, stop=False)
                pe.matmul(o, l_lo, r_hi, start=False, stop=False)
                return pe.matmul(o, l_hi, r_lo, start=False, stop=stop)

            def transpose_x(layer):
                for k in range(2 * NHALF):
                    half, c = k // NC, k % NC
                    pe.wait_ge(xn_ready if half == 0 else xn_act_ready, 4 * layer + 4)
                    for i in range(4):
                        t = 4 * half + i
                        last = pe.transpose(ps[:, k, i * P:(i + 1) * P], xn_tok[:, t, c::NC], ident[:])
                    last.then_inc(xT_ps, 1)

            def qkv0():
                pe.wait_ge(wqkv_ready, 1)
                for t in range(NT):
                    pe.wait_ge(xT_ready, 2 * (t // 4 + 1))
                    if t >= 2:
                        pe.wait_ge(qk_copied, t - 1)
                        pe.wait_ge(v0_copied, t - 1)
                    b = 4 + 2 * (t % 2)
                    tk = slice(t * P, (t + 1) * P)
                    for o, cols in ((ps[:, b, :], slice(0, 2 * D)), (ps[:, b + 1, 0:D], slice(2 * D, 3 * D))):
                        for c in range(NC):
                            last = mm3(o, xT_hi[:, c, tk], xT_lo[:, c, tk], wqkv_hi[:, c, cols], wqkv_lo[:, c, cols],
                                       c == 0, c == NC - 1)
                    last.then_inc(qkv_ps, 1)

            def turn_stack(t):
                pe.wait_ge(stk_ready, t + 1)
                for q in range(4):
                    if q == 2:
                        pe.wait_ge(stk_k_ready, t + 1)
                    if t >= 1:
                        pe.wait_ge(stk_read_act if q % 2 == 0 else stk_read_dve, 2 * (t - 1) + q // 2 + 1)
                    for i in range(4):
                        h = 2 * (4 * (q % 2) + i)
                        src = stack[:, t % 2, q // 2, h:h + 2].rearrange("p h a d -> p (h a d)")
                        last = pe.transpose(ps[:, q, i * P:(i + 1) * P], src, ident[:])
                    last.then_inc(stk_ps, 1)

            def turn_f0(t):
                if t >= 2:
                    pe.wait_ge(g0_ready, t - 1)
                for c in range(NC):
                    last = pe.transpose(ps[:, 6 + t % 2, c * P:(c + 1) * P], f0T[:, c, t * P:(t + 1) * P], ident[:])
                last.then_inc(f_ps, 1)

            def scores0(h, j):
                n = h * NT + j
                if n == 0:
                    pe.wait_ge(stk_read_act, 2 * NT)
                    pe.wait_ge(stk_read_dve, 2 * NT)
                if n >= 2:
                    pe.wait_ge(s0_sq, n - 1)
                rows = slice(64 * (h % 2), 64 * (h % 2) + STK)
                o = 1024 * (n % 2)
                for a, e in spans((NT - j) * P):
                    last = pe.matmul(psf[:, o + a:o + e], KT[rows, h // 2, j * P:(j + 1) * P],
                                     QT[rows, h // 2, j * P + a:j * P + e], start=True, stop=True)
                last.then_inc(s0_ps, 1)

            def out0(h, j):
                if j == 0:
                    if h == 0:
                        pe.wait_ge(g0_ready, NT)
                    if h >= 2:
                        pe.wait_ge(o0_copied, h - 1)
                    if h % QUAD == 1 and h >= QUAD:
                        pe.wait_ge(o0_ready, h // QUAD)
                if j < SPLIT - 1:
                    pe.wait_ge(a0_ready, (SPLIT - 1) * h + j + 1)
                elif j == SPLIT - 1:
                    pe.wait_ge(a0_own, 2 * h + 2)
                else:
                    pe.wait_ge(s0_mask, h * NT + j + 1)
                if h == 0 and j == 0:
                    pe.wait_ge(v0_ready, 1)
                for half in range(NHALF):
                    a, e = max(j * P, half * HALF), (half + 1) * HALF
                    if a < e:
                        o = ps[0:D0 + 1, 4 + 2 * (h % 2) + half, a - half * HALF:HALF]
                        if j < SPLIT:
                            last = mm3(o, V0_hi[:, j, h, :], V0_lo[:, j, h, :], A0_hi(h, j, a - j * P, e - j * P),
                                       A0_lo[:, h % 2, OFF[j] + a - j * P:OFF[j] + e - j * P], j == 0, False)
                        else:
                            last = pe.matmul(o, V0[:, j, h, :], A0_row(h, j)[:, a - j * P:e - j * P], start=False,
                                             stop=(j == 4 * half + 3))
                if j == NT - 1:
                    last.then_inc(o0_ps, 1)

            def turn_out0(g):
                pe.wait_ge(o0_copied, QUAD * (g + 1))
                for t in range(NT):
                    last = pe.transpose(psf[:, 3072 + t * P:3072 + (t + 1) * P], o_raw[:, t * P:(t + 1) * P], ident[:])
                last.then_inc(o0_turned, 1)

            def project_out0():
                pe.wait_ge(o0_ready, H0 // QUAD)
                for k in range(2 * NHALF):
                    half, c = k // NC, k % NC
                    for i in range(4):
                        last = pe.transpose(ps[:, k, i * P:(i + 1) * P], o_tok[:, 4 * half + i, c * P:(c + 1) * P],
                                            ident[:])
                    last.then_inc(oT_ps, 1)
                pe.wait_ge(oT_ready, 2 * NC)
                pe.wait_ge(wout_ready, 1)
                for t in range(NT):
                    if t >= 2:
                        pe.wait_ge(x_ready, t - 1)
                    tk = slice(t * P, (t + 1) * P)
                    for c in range(NC):
                        last = mm3(ps[:, 4 + t % 2, 0:D], oT_hi[:, c, tk], oT_lo[:, c, tk], wout_hi[:, c], wout_lo[:, c],
                                   c == 0, c == NC - 1)
                    last.then_inc(so_ps, 1)

            def gate_up(s, w_hi, w_lo, done):
                half = s % 2
                tk = slice(half * HALF, (half + 1) * HALF)
                for m in range(2):
                    for c in range(NC):
                        last = mm3(ps[:, 2 * (s % 2) + m, :], w_hi(m, c), w_lo(m, c), xT_hi[:, c, tk],
                                   xT_lo[:, c, tk], c == 0, c == NC - 1)
                last.then_inc(done, 1)

            pe.wait_ge(in_const, 16)
            transpose_x(0)
            qkv0()
            for s in range(2 * U0 + 2):
                if s < 2 * U0:
                    J, col = s // 4, (s // 2) % 2 * P
                    if s % 4 == 0:
                        pe.wait_ge(w0_lo_ready, J + 1)
                    if s == 0:
                        pe.wait_ge(qk_copied, NT)
                        pe.wait_ge(v0_copied, NT)
                    if s >= 2:
                        pe.wait_ge(gu0_copied, s - 1)
                    gate_up(s, lambda m, c: w0_hi[:, J % 3, m, c, col:col + P],
                            lambda m, c: w0_lo[:, J % 3, m, c, col:col + P], gu0_ps)
                if s >= 2:
                    r = s - 2
                    u, half = r // 2, r % 2
                    pe.wait_ge(h0_ready, r + 1)
                    for c in range(NC):
                        last = pe.matmul(ps[:, 4 + 2 * c + half, :], w0_dn[:, (u // 2) % 3, u % 2, c * P:(c + 1) * P],
                                         h0[:, r % 3, :], start=(u == 0), stop=(u == U0 - 1))
                    last.then_inc(dn0_ps, 1)
            pe.wait_ge(fT_ready, 2 * NC)
            for t in range(NT):
                turn_stack(t)
                turn_f0(t)
            for n in range((H0 + 1) * NT + LAG):
                h, j = n // NT, n % NT
                if h < H0:
                    scores0(h, j)
                if n >= NT + LAG:
                    out0((n - LAG) // NT - 1, (n - LAG) % NT)
                if h >= QUAD and h % QUAD == 1 and j == 3:
                    turn_out0(h // QUAD - 1)
            turn_out0(H0 // QUAD - 1)
            project_out0()

            pe.wait_ge(x_ready, NT)
            transpose_x(1)

            def values1(t):
                pe.wait_ge(xT_ready, 4 * NC)
                pe.wait_ge(wv_ready, 1)
                if t >= 2:
                    pe.wait_ge(v_read, t - 1)
                tk = slice(t * P, (t + 1) * P)
                for c in range(NC):
                    last = mm3(ps[:, 4 + t % 2, :], xT_hi[:, c, tk], xT_lo[:, c, tk], wv_hi[:, c], wv_lo[:, c],
                               c == 0, c == NC - 1)
                last.then_inc(v_ps, 1)

            def side_slot():
                n = side[0]
                side[0] += 1
                if n >= 2:
                    name, a, b = SIDE[n - 2]
                    if name == "project":
                        pe.wait_ge(pj_cos, 2 * a + b + 1)
                    elif name == "turn":
                        pe.wait_ge(cT_read, 2 * a + b + 1)
                    elif name == "out":
                        pe.wait_ge(s_added, NT * a + b + 1)
                    elif name == "logits":
                        pe.wait_ge(lgT_copied, b + 1)
                    elif name == "turn_logits":
                        pe.wait_ge(lg_read, 1)
                    else:
                        pe.wait_ge(gT_ready, b + 1)
                return ps[:, 6 + n % 2, :]
            side = [0]

            def project(n, half):
                pe.wait_ge(wqk_ready, n + 1)
                if n == 0:
                    pe.wait_ge(xT_ready, 2 * NC + NC * (half + 1))
                o = side_slot()
                tk = slice(half * HALF, (half + 1) * HALF)
                for c in range(NC):
                    last = mm3(o, wqk_hi[:, n % 2, c], wqk_lo[:, n % 2, c], xT_hi[:, c, tk], xT_lo[:, c, tk],
                               c == 0, c == NC - 1)
                last.then_inc(pj_ps, 1)

            def scores1(h, j):
                n = h * NT + j
                if j == 0:
                    pe.wait_ge(parts_ready, part_of["project", PROJ.index(("q", h)), 1] + 1)
                if n >= 2:
                    pe.wait_ge(s1_bias, n - 1)
                g = h // REP
                o = 1024 * (n % 2)
                kk = slice(j * P, (j + 1) * P)
                for a, e in spans((NT - j) * P):
                    qq = slice(j * P + a, j * P + e)
                    last = mm3(psf[:, o + a:o + e], k_hi[:, g % 2, kk], k_lo[:, g % 2, kk], q_hi[:, h % 2, qq],
                               q_lo[:, h % 2, qq], True, True)
                last.then_inc(s1_ps, 1)

            def context(h, t):
                r = 3 * h + t // 3
                if r == 0:
                    pe.wait_ge(v_read, NT)
                if t % 3 == 0 and r >= 2:
                    pe.wait_ge(c_ready, r - 1)
                pe.wait_ge(s1_mask, h * NT + t + 1)
                o = (D1 + 1) * (t % 3)
                for j in range(t + 1):
                    a = OFF[j] + (t - j) * P
                    last = pe.matmul(ps[:, 4 + r % 2, o:o + D1 + 1], P1[:, h % 2, a:a + P], V1[:, j, h // REP, :],
                                     start=(j == 0), stop=(j == t))
                if t % 3 == 2 or t == NT - 1:
                    last.then_inc(c_ps, 1)

            def turn_context(h, half):
                pe.wait_ge(c_ready, 3 * h + (2 if half == 0 else 3))
                o = side_slot()
                for i in range(4):
                    last = pe.transpose(o[:, i * P:(i + 1) * P], ctx_tok[:, h % 2, 4 * half + i, :], ident[:])
                last.then_inc(cT_ps, 1)

            def project_out1(m, t):
                if t == 0:
                    pe.wait_ge(parts_ready, part_of["turn", PAIR * m + PAIR - 1, 1] + 1)
                    pe.wait_ge(wo_ready, m + 1)
                o = side_slot()
                tk = slice(t * P, (t + 1) * P)
                for i in range(PAIR):
                    last = mm3(o[:, 0:D], cT_hi[:, i, tk], cT_lo[:, i, tk], wo_hi[:, i], wo_lo[:, i], i == 0, i == PAIR - 1)
                last.then_inc(s_ps, 1)

            def logits(_, half):
                pe.wait_ge(rw_ready, 1)
                o = side_slot()
                tk = slice(half * HALF, (half + 1) * HALF)
                for c in range(NC):
                    last = mm3(o[0:NE, :], rw_hi[:, c], rw_lo[:, c], xT_hi[:, c, tk], xT_lo[:, c, tk], c == 0, c == NC - 1)
                last.then_inc(lgT_ps, 1)

            def turn_logits(*_):
                pe.wait_ge(lgT_copied, 2)
                o = side_slot()
                for t in range(NT):
                    last = pe.transpose(o[:, t * NE:(t + 1) * NE], lgT[:, t * P:(t + 1) * P], ident[0:NE, 0:NE])
                last.then_inc(lg_ps, 1)

            def turn_gates(_, half):
                pe.wait_ge(gates_ready, 1)
                o = side_slot()
                for i in range(4):
                    last = pe.transpose(o[0:NE, i * P:(i + 1) * P], r_d[:, 4 * half + i, :], ident[:])
                last.then_inc(gT_ps, 1)

            def gate_up1(s):
                u = s // 2
                pe.wait_ge(e_ready, u + 1)
                if s < 2:
                    pe.wait_ge(s1_bias, NT * H1)
                else:
                    pe.wait_ge(clip_ready, s - 1)
                gate_up(s, lambda m, c: e_hi[:, u % 3, m, c * P:(c + 1) * P],
                        lambda m, c: e_lo[:, u % 3, m, c * P:(c + 1) * P], gu1_ps)

            for step in STEPS1:
                {"project": project, "scores": scores1, "context": context, "turn": turn_context, "values": values1,
                 "experts": gate_up1, "out": project_out1, "logits": logits, "turn_logits": turn_logits, "gates": turn_gates}[step[0]](*step[1:])

            pe.wait_ge(s_added, (H1 // PAIR) * NT)
            for s in range(2 * U1 + 2):
                if 2 <= s < 2 * U1:
                    gate_up1(s)
                if s >= 2:
                    r = s - 2
                    u, half = r // 2, r % 2
                    pe.wait_ge(h1_parts_ready, r + 1)
                    for c in range(NC):
                        cc = slice(c * P, (c + 1) * P)
                        last = mm3(ps[:, 4 + 2 * c + half, :], e_hi[:, u % 3, 2, cc], e_lo[:, u % 3, 2, cc],
                                   h1_hi[:, r % 3, :], h1_lo[:, r % 3, :], u == 0, u == U1 - 1)
                    last.then_inc(dn1_ps, 1)
            pe.wait_ge(fT_ready, 4 * NC)
            for t in range(NT):
                if t >= 4:
                    pe.wait_ge(x_ready, NT + t - 3)
                for c in range(NC):
                    last = pe.transpose(ps[:, t % 4, c * P:(c + 1) * P], f1T[:, c, t * P:(t + 1) * P], ident[:])
                last.then_inc(f_ps, 1)

        @block.scalar
        def _(act):
            def layernorm_sd(layer):
                act.wait_ge(var_ready, layer + 1)
                act.activation(ln_sd[:], ln_var[:], ACT.Sqrt).then_inc(sd_ready, 1)

            def layernorm_norm(layer):
                act.wait_ge(shift_ready, layer + 1)
                for t in range(NT // 2, NT):
                    act.activation(xn_tok[:, t, :], x_tok[:, t, :], ACT.Identity, bias=ln_t[:, t:t + 1],
                                   scale=ln_r[:, t:t + 1]).then_inc(xn_act_ready, 1)

            def layernorm_hi(layer):
                for k in range(2 * NHALF):
                    half, c = k // NC, k % NC
                    act.wait_ge(xT_ps, 4 * layer + k + 1)
                    act.activation(xT_hi[:, c, half * HALF:(half + 1) * HALF], ps[:, k, :], ACT.Copy)\
                        .then_inc(xT_hi_ready, 1)

            def collect_f(n_dn, dn_done, fT):
                act.wait_ge(dn_done, n_dn)
                for c in range(NC):
                    act.activation(fT[:, c, 0:HALF], ps[:, 4 + 2 * c, :], ACT.Copy).then_inc(fT_ready, 1)

            def numbers(J, part):
                if part == 1:
                    act.activation(dq_s[:], sgn[:], ACT.Identity, bias=consts[:, 0:1], scale=-0.125).then_inc(num_ready, 1)
                    return
                act.wait_ge(nib_ready, 2 * (J + 1))
                if J >= 1:
                    act.wait_ge(ladder_ready, J)
                act.activation(dq_m[:], mag[:], ACT.Copy).then_inc(num_ready, 1)

            def high0(J):
                act.wait_ge(w0_ready, J + 1)
                if J >= 3:
                    act.wait_ge(gu0_ps, 4 * (J - 2))
                act.activation(w0_hi[:, J % 3], w0[:], ACT.Copy).then_inc(w0_hi_ready, 1)

            act.wait_ge(consts_ready, 1)
            act.activation(ln_sd[:, 0:1], consts[:, 0:1], ACT.Sqrt).then_inc(table_ready, 1)
            act.wait_ge(table_ready, 1)
            act.wait_ge(in_wqkv, 16)
            act.activation(wqkv_hi[:], wqkv[:], ACT.Copy).then_inc(wqkv_hi_ready, 1)
            layernorm_sd(0)
            layernorm_norm(0)
            layernorm_hi(0)
            numbers(0, 0)
            numbers(0, 1)
            for t in range(NT):
                act.wait_ge(qkv_ps, t + 1)
                act.activation(qk_tok[:, t, :], ps[:, 4 + 2 * (t % 2), :], ACT.Copy).then_inc(qk_copied, 1)
                if t == 3:
                    high0(0)
                if t == 5:
                    numbers(1, 0)
                    numbers(1, 1)

            for s in range(2 * U0 + 1):
                if s < 2 * U0:
                    act.wait_ge(gu0_ps, s + 1)
                    if s >= 3:
                        act.wait_ge(h0_ready, s - 2)
                    act.activation(e0_gu[:, s % 3].rearrange("p m n -> p (m n)"),
                                   psf[:, 1024 * (s % 2):1024 * (s % 2) + 1024], ACT.Copy).then_inc(gu0_copied, 1)
                    act.wait_ge(gu0_copied, s + 1)
                    if s >= 2:
                        act.wait_ge(inner_ready, s - 1)
                    act.activation(e0_a[:, s % 2, :], e0_gu[:, s % 3, 0, :], ACT.Square).then_inc(square_ready, 1)
                if s >= 1:
                    r = s - 1
                    act.wait_ge(inner_ready, r + 1)
                    act.activation(e0_b[:, r % 3, :], e0_b[:, r % 3, :], ACT.Tanh, scale=GELU_C * GELU_K)\
                        .then_inc(th0_ready, 1)
                if block_at(s, 6):
                    high0(block_at(s, 6))
                for i in range(2):
                    if block_at(s, 2 + i) and block_at(s, 2 + i) >= 2:
                        numbers(block_at(s, 2 + i), i)
                t = tile_at(s, 2)
                if t is not None:
                    act.wait_ge(qk_centred, t + 1)
                    act.activation(rope_b[:, t % 2, :], qk_tok[:, t, :], ACT.Square).then_inc(qk_squared, 1)
                if s == VAR_STEP:
                    act.wait_ge(hvar_ready, 1)
                    act.activation(hsd[:], hv[:], ACT.Sqrt).then_inc(hsd_ready, 1)
            collect_f(2 * U0, dn0_ps, f0T)
            for t in range(NT + 1):
                if t < NT:
                    act.wait_ge(qk_ready, t + 1)
                    if t >= 2:
                        act.wait_ge(stk_ps, 4 * (t - 1))
                    for m, places in ((0, slice(0, 4, 2)), (1, slice(0, 2))):
                        src = qk_tok[:, t, m * D:(m + 1) * D].rearrange("p (h a d) -> p h a d", h=H0, a=1)
                        act.activation(stack[:, t % 2, m, :, places, :].bitcast(F32R),
                                       src.to_broadcast((P, H0, 2, D0)), ACT.Copy).then_inc(stk_hi, 1)
                if t >= 1:
                    r = t - 1
                    for q in (0, 2):
                        act.wait_ge(stk_ps, 4 * r + q + 1)
                        act.activation((QT, KT)[q // 2][:, 0:4, r * P:(r + 1) * P],
                                       ps[:, q, :].rearrange("p (i n) -> p i n", i=4), ACT.Copy).then_inc(stk_read_act, 1)
                    act.wait_ge(f_ps, t)
                    if r >= 2:
                        act.wait_ge(g0_ready, r - 1)
                    act.activation(mix0_a[:, r % 2, :], ps[:, 6 + r % 2, 0:D], ACT.Tanh, scale=0.25).then_inc(fth_ready, 1)
            def copy_out0(h):
                act.wait_ge(o0_ps, h + 1)
                if h >= QUAD and h % QUAD == 0:
                    act.wait_ge(o0_turned, h // QUAD)
                act.activation(o_raw[32 * (h % QUAD):32 * (h % QUAD) + D0 + 1, :],
                               psf[0:D0 + 1, 2048 + 1024 * (h % 2):3072 + 1024 * (h % 2)], ACT.Copy).then_inc(o0_copied, 1)

            for h in range(H0):
                for j in range(NT):
                    n = h * NT + j
                    act.wait_ge(s0_ps, n + 1)
                    if j == 0 and h >= 2:
                        act.wait_ge(o0_ps, h - 1)
                    w = (NT - j) * P
                    if h >= 1 and j < SPLIT - 1:
                        act.wait_ge(a0_ready, (SPLIT - 1) * (h - 1) + j + 1)
                    if h >= 1 and j == SPLIT - 1:
                        act.wait_ge(a0_own, 2 * h)
                    act.activation(A0_row(h, j), psf[:, 1024 * (n % 2):1024 * (n % 2) + w],
                                   ACT.Square).then_inc(s0_sq, 1)
                    if h >= 2 and j == 1:
                        copy_out0(h - 2)
                    if j in HIGH_AT:
                        i = HIGH_AT.index(j)
                        act.wait_ge(s0_mask, h * NT + i + 1)
                        act.activation(A0_hi(h, i, 0, (NT - i) * P), A0_row(h, i), ACT.Copy)\
                            .then_inc(a0_hi, 1)
                if h == 0:
                    act.wait_ge(in_wout, 16)
                    act.activation(wout_hi[:], wout[:], ACT.Copy).then_inc(wout_hi_ready, 1)
            copy_out0(H0 - 2)
            copy_out0(H0 - 1)
            for k in range(2 * NHALF):
                half, c = k // NC, k % NC
                act.wait_ge(oT_ps, k + 1)
                act.activation(oT_hi[:, c, half * HALF:(half + 1) * HALF], ps[:, k, :], ACT.Copy).then_inc(oT_hi_ready, 1)

            layernorm_sd(1)
            layernorm_norm(1)
            act.wait_ge(in_router, 48)
            act.activation(rw_hi[:], rw[:], ACT.Copy).then_inc(rw_hi_ready, 1)
            act.wait_ge(in_wv, 16)
            act.activation(wv_hi, wv, ACT.Copy).then_inc(wv_hi_ready, 1)

            def split_wqk(n):
                act.wait_ge(in_wqk[n % 2], 16 * (n // 2 + 1))
                if n >= 2:
                    act.wait_ge(pj_ps, 2 * (n - 1))
                act.activation(wqk_hi[:, n % 2], wqk[:, n % 2], ACT.Copy).then_inc(wqk_hi_ready, 1)

            split_wqk(0)
            split_wqk(1)
            layernorm_hi(1)

            def split_wo(m):
                act.wait_ge(in_wo[m % 2], 16 * (m // 2 + 1))
                if m >= 1:
                    act.wait_ge(s_ps, NT * m)
                act.activation(wo_hi[:], wo[:, m % 2], ACT.Copy).then_inc(wo_hi_ready, 1)

            def project_part(n, half):
                act.wait_ge(pj_rot, 2 * n + half + 1)
                kind, hd = PROJ[n]
                if kind == "q" and hd >= 2:
                    act.wait_ge(s1_ps, NT * (hd - 1))
                if kind == "k" and hd >= 2:
                    act.wait_ge(s1_ps, NT * REP * (hd - 1))
                dst = (q_hi if kind == "q" else k_hi)[:, hd % 2, half * HALF:(half + 1) * HALF]
                act.activation(dst, rot[:, part_of["project", n, half] % 3], ACT.Copy).then_inc(parts_hi, 1)

            def scores(h, j):
                n = h * NT + j
                w = (NT - j) * P
                act.wait_ge(s1_bias, n + 1)
                act.activation(cap[:, n % 2, 0:w], cap[:, n % 2, 0:w], ACT.Tanh, scale=1.0 / (CAP * float(D1) ** 0.5))\
                    .then_inc(act_step, 1)
                act.wait_ge(act_step, n + 1)
                if j == 0 and h >= 2:
                    act.wait_ge(c_ps, 3 * (h - 1))
                act.activation(P1[:, h % 2, OFF[j]:OFF[j] + w], cap[:, n % 2, 0:w], ACT.Exp, scale=CAP)\
                    .then_inc(s1_exp, 1)

            def turn_part(h, half):
                act.wait_ge(cT_read, 2 * h + half + 1)
                if h >= PAIR:
                    act.wait_ge(s_ps, NT * (h // PAIR))
                act.activation(cT_hi[:, h % PAIR, half * HALF:(half + 1) * HALF],
                               rot[:, part_of["turn", h, half] % 3], ACT.Copy).then_inc(parts_hi, 1)

            def router(part):
                if part == 0:
                    act.wait_ge(lg_read, 1)
                    act.activation(r_b[:], r_a[:], ACT.Exp, scale=-1.0).then_inc(sp_a, 1)
                elif part == 1:
                    act.wait_ge(sp_b, 1)
                    act.activation(r_d[:], r_c[:], ACT.Ln).then_inc(sp_a, 1)
                elif part == 2:
                    act.wait_ge(sp_b, 2)
                    act.activation(r_b[:], r_a[:], ACT.Sqrt).then_inc(sp_a, 1)

            def split_expert(u):
                act.wait_ge(in_ew[u % 3], 16 * (u // 3 + 1))
                if u >= 3:
                    act.wait_ge(dn1_ps, 2 * (u - 2))
                act.activation(e_hi[:, u % 3], eraw[:, u % 3], ACT.Copy).then_inc(e_hi_ready, 1)

            for step in ACT_STEPS1:
                {"project_part": project_part, "scores": scores, "turn_part": turn_part, "split_wqk": split_wqk,
                 "split_wo": split_wo, "split_expert": split_expert, "router": router}[step[0]](*step[1:])

            act.wait_ge(s_added, (H1 // PAIR) * NT)
            for s in range(2 * U1 + 1):
                if s < 2 * U1:
                    act.wait_ge(clip_ready, s + 1)
                    if s >= 2:
                        act.wait_ge(h1_ready, s - 1)
                    act.activation(e1_a[:, s % 2, :], gu[:, s % 2, 0, :], ACT.Tanh, scale=0.5).then_inc(th1_ready, 1)
                if s >= 1:
                    r = s - 1
                    act.wait_ge(h1_ready, r + 1)
                    if r >= 3:
                        act.wait_ge(dn1_ps, r - 2)
                    act.activation(h1_hi[:, r % 3, :], h1[:, r % 2, :], ACT.Copy).then_inc(h1_hi_ready, 1)
                if s % 2 == 1 and s // 2 + 2 < U1:
                    split_expert(s // 2 + 2)
            collect_f(2 * U1, dn1_ps, f1T)
            for t in range(NT):
                act.wait_ge(f_ps, NT + t + 1)
                if t >= 4:
                    act.wait_ge(x_ready, NT + t - 3)
                act.activation(mix1_a[:, t % 4, :], ps[:, t % 4, 0:D], ACT.Tanh, scale=0.5).then_inc(fth_ready, 1)

        @block.vector
        def _(dve):
            steps = [0]

            def link(ins):
                steps[0] += 1
                ins.then_inc(vec, 1)
                dve.wait_ge(vec, steps[0])

            def rsqrt(sd, var, r, t):
                link(dve.reciprocal(r, sd))
                link(dve.tensor_tensor(t, r, r, ALU.mult))
                link(dve.tensor_tensor(t, t, var, ALU.mult))
                link(dve.tensor_scalar(t, t, -0.5, 1.5, ALU.mult, ALU.add))
                link(dve.tensor_tensor(r, r, t, ALU.mult))

            def layernorm_stats(layer):
                if layer == 0:
                    for t in range(NT):
                        if t % 4 == 0:
                            dve.wait_ge(in_x[t // 4], 16)
                        link(dve.bn_stats(ln_stats[:, t % 2, :], x_tok[:, t, :]))
                        link(dve.bn_aggr(ln_mv[:, t, :], ln_stats[:, t % 2, :]))
                dve.tensor_scalar(ln_var[:], ln_mv[:, :, 1], LN_EPS, None, ALU.add).then_inc(var_ready, 1)

            def tile_stats(t):
                dve.wait_ge(x_ready, t + 1)
                link(dve.bn_stats(ln_stats[:, t % 2, :], x_tok[:, t, :]))
                link(dve.bn_aggr(ln_mv[:, t, :], ln_stats[:, t % 2, :]))

            def layernorm_norm(layer):
                dve.wait_ge(sd_ready, layer + 1)
                rsqrt(ln_sd[:], ln_var[:], ln_r[:], ln_t[:])
                dve.scalar_tensor_tensor(out=ln_t[:], in0=ln_mv[:, :, 0], scalar=-1.0, in1=ln_r[:], op0=ALU.mult,
                                         op1=ALU.mult).then_inc(shift_ready, 1)
                for t in range(NT // 2):
                    dve.tensor_scalar(xn_tok[:, t, :], x_tok[:, t, :], ln_mv[:, t, 0:1], ln_r[:, t:t + 1],
                                      ALU.subtract, ALU.mult).then_inc(xn_ready, 1)

            def layernorm_lo(layer):
                for k in range(2 * NHALF):
                    half, c = k // NC, k % NC
                    dve.wait_ge(xT_hi_ready, 4 * layer + k + 1)
                    tk = slice(half * HALF, (half + 1) * HALF)
                    dve.tensor_tensor(xT_lo[:, c, tk], ps[:, k, :], xT_hi[:, c, tk].bitcast(F32), ALU.subtract)\
                        .then_inc(xT_ready, 1)

            dve.memset(o_raw[:], 0.0)
            for i, v in enumerate((0.5,)):
                last = dve.memset(consts[:, i:i + 1], v)
            last.then_inc(consts_ready, 1)
            dve.memset(V0[:, :, :, D0:D0 + 1], 1.0)

            def nibbles(J, i):
                dve.wait_ge(in_pk[J % 2], 32 * (J // 2 + 1))
                if J >= 1:
                    dve.wait_ge(num_ready, 2 * J)
                src = pk[:, J % 2]
                dve.tensor_scalar(mag[:, :, i, :], src, 4 * i, 7, ALU.logical_shift_right, ALU.bitwise_and)
                dve.tensor_scalar(sgn[:, :, i, :], src, 4 * i, 8, ALU.logical_shift_right, ALU.bitwise_and)\
                    .then_inc(nib_ready, 1)

            def ladder(J, part):
                if part == 1:
                    dve.wait_ge(num_ready, 2 * J + 2)
                    link(dve.tensor_tensor(dq_a[:], dq_a[:], dq_m[:], ALU.add))
                    dve.tensor_tensor(dq_a[:], dq_a[:], dq_s[:], ALU.mult).then_inc(ladder_ready, 1)
                    return
                dve.wait_ge(num_ready, 2 * J + 1)
                if J >= 1:
                    dve.wait_ge(w0_ready, J)
                dve.tensor_scalar(dq_b[:], dq_m[:], 6.0, 2.0, ALU.max, ALU.mult)
                link(dve.tensor_scalar(dq_a[:], dq_m[:], 4.0, -16.0, ALU.max, ALU.add))
                link(dve.tensor_tensor(dq_a[:], dq_a[:], dq_b[:], ALU.add))

            layernorm_stats(0)
            layernorm_norm(0)
            nibbles(0, 0)
            nibbles(0, 1)
            layernorm_lo(0)
            for t in range(NT):
                dve.wait_ge(qkv_ps, t + 1)
                dve.tensor_copy(V0[:, t, :, 0:D0], ps[:, 5 + 2 * (t % 2), 0:D].rearrange("p (h d) -> p h d", h=H0))\
                    .then_inc(v0_copied, 1)
                if t in (1, 2):
                    ladder(0, t - 1)
                if t in (3, 4):
                    nibbles(1, t - 3)
            ladder(1, 0)
            ladder(1, 1)

            def collect_f(n_dn, dn_done, fT):
                dve.wait_ge(dn_done, n_dn)
                for c in range(NC):
                    dve.tensor_copy(fT[:, c, HALF:TOK], ps[:, 5 + 2 * c, :]).then_inc(fT_ready, 1)

            hd = dict(h=2 * H0)

            def centre_tile(t):
                ra = rope_a[:, t % 2, :].rearrange("p (h d) -> p h d", **hd)
                qd = qk_tok[:, t, :].rearrange("p (h d) -> p h d", **hd)
                dve.wait_ge(qk_split, t + 1)
                link(dve.tensor_tensor(rope_a[:, t % 2, :], rope_a[:, t % 2, :], rope_b[:, t % 2, :], ALU.add))
                link(dve.tensor_reduce(hm[:, 0, :], ra, AX_X, ALU.add))
                link(dve.tensor_scalar(hm[:, 1, :], hm[:, 0, :], 1.0 / D0, None, ALU.mult))
                mean = hm[:, 1, :].rearrange("p (h a) -> p h a", a=1).to_broadcast((P, 2 * H0, D0))
                dve.tensor_tensor(qd, ra, mean, ALU.subtract).then_inc(qk_centred, 1)

            def variance_tile(t):
                dve.wait_ge(qk_squared, t + 1)
                dve.tensor_reduce(hv[:, t, :], rope_b[:, t % 2, :].rearrange("p (h d) -> p h d", **hd), AX_X, ALU.add)\
                    .then_inc(qk_var, 1)

            def norm_tile(t):
                qd = qk_tok[:, t, :].rearrange("p (h d) -> p h d", **hd)
                rs = hr[:, t, :].rearrange("p (h a) -> p h a", a=1).to_broadcast((P, 2 * H0, D0))
                link(dve.tensor_tensor(qd, qd, rs, ALU.mult))
                dve.tensor_tensor(qd, qd, lns[:, 0:1, :].to_broadcast((P, 2 * H0, D0)), ALU.mult).then_inc(qk_scaled, 1)

            dve.wait_ge(in_l0c, 48)
            for s in range(2 * U0 + 1):
                if s < 2 * U0:
                    dve.wait_ge(square_ready, s + 1)
                    if s >= 3:
                        dve.wait_ge(h0_ready, s - 2)
                    dve.scalar_tensor_tensor(out=e0_b[:, s % 3, :], in0=e0_a[:, s % 2, :], scalar=1.0 / GELU_K,
                                             in1=e0_gu[:, s % 3, 0, :], op0=ALU.add, op1=ALU.mult).then_inc(inner_ready, 1)
                if s >= 1:
                    r = s - 1
                    dve.wait_ge(th0_ready, r + 1)
                    dve.wait_ge(gated_ready, r + 1)
                    if r >= 3:
                        dve.wait_ge(dn0_ps, r - 2)
                    dve.scalar_tensor_tensor(out=h0[:, r % 3, :], in0=e0_b[:, r % 3, :], scalar=1.0,
                                             in1=e0_p[:, r % 3, :], op0=ALU.add, op1=ALU.mult).then_inc(h0_ready, 1)
                for i in range(2):
                    if block_at(s, i) and block_at(s, i) >= 2:
                        nibbles(block_at(s, i), i)
                for i in range(2):
                    if block_at(s, 3 + i) and block_at(s, 3 + i) >= 2:
                        ladder(block_at(s, 3 + i), i)
                if tile_at(s, 1) is not None:
                    centre_tile(tile_at(s, 1))
                if tile_at(s, 3) is not None:
                    variance_tile(tile_at(s, 3))
                if s == VAR_STEP:
                    dve.wait_ge(qk_var, NT)
                    dve.tensor_scalar(hv[:], hv[:], 1.0 / D0, LN_EPS, ALU.mult, ALU.add).then_inc(hvar_ready, 1)
                if s == VAR_STEP + 2:
                    dve.wait_ge(hsd_ready, 1)
                    rsqrt(hsd[:], hv[:], hr[:], ht[:])
                if s > VAR_STEP + 2 and s - VAR_STEP - 3 < NT:
                    norm_tile(s - VAR_STEP - 3)

            collect_f(2 * U0, dn0_ps, f0T)
            for t in range(NT + 1):
                if t < NT:
                    dve.wait_ge(qk_ready, t + 1)
                    dve.wait_ge(stk_hi, 2 * t + 1)
                    src = qk_tok[:, t, 0:D].rearrange("p (h a d) -> p h a d", h=H0, a=1)
                    dve.tensor_tensor(stack[:, t % 2, 0, :, 1:4:2, :].bitcast(F32R), src.to_broadcast((P, H0, 2, D0)),
                                      stack[:, t % 2, 0, :, 0:4:2, :], ALU.subtract).then_inc(stk_ready, 1)
                if t >= 1:
                    r = t - 1
                    for q in (1, 3):
                        dve.wait_ge(stk_ps, 4 * r + q + 1)
                        dve.tensor_copy((QT, KT)[q // 2][:, 4:8, r * P:(r + 1) * P],
                                        ps[:, q, :].rearrange("p (i n) -> p i n", i=4)).then_inc(stk_read_dve, 1)
                    dve.wait_ge(fth_ready, t)
                    dve.scalar_tensor_tensor(out=g0_tok[:, r, :], in0=mix0_a[:, r % 2, :], scalar=1.0,
                                             in1=ps[:, 6 + r % 2, 0:D], op0=ALU.add, op1=ALU.mult).then_inc(g0_ready, 1)

            def read_out0(g):
                dve.wait_ge(o0_turned, g + 1)
                if g >= 1:
                    dve.wait_ge(o0_ready, g)
                o = psf[:, 3072:4096].rearrange("p (t h d) -> p t h d", t=NT, h=QUAD)
                link(dve.reciprocal(o_rden[:], o[:, :, :, D0:D0 + 1]))
                dst = o_tok[:, :, g * QUAD * D0:(g + 1) * QUAD * D0].rearrange("p t (h d) -> p t h d", h=QUAD)
                dve.tensor_tensor(dst, o[:, :, :, 0:D0], o_rden[:].to_broadcast((P, NT, QUAD, D0)), ALU.mult)\
                    .then_inc(o0_ready, 1)

            dve.wait_ge(stk_ready, NT)
            dve.wait_ge(stk_k_ready, NT)
            dve.tensor_copy(V0_hi, V0[:, 0:SPLIT]).then_inc(v0_hi_ready, 1)
            dve.wait_ge(v0_hi_ready, 1)
            dve.tensor_tensor(V0_lo, V0[:, 0:SPLIT], V0_hi.bitcast(F32), ALU.subtract).then_inc(v0_ready, 1)
            for h in range(H0):
                for j in range(NT):
                    n = h * NT + j
                    dve.wait_ge(s0_sq, n + 1)
                    a = A0_row(h, j)
                    dve.tensor_tensor(a, a, a, ALU.mult).then_inc(s0_four, 1)
                    if j == OWN_AT:
                        i = SPLIT - 1
                        w, hi = A0_row(h, i), A0_hi(h, i, 0, (NT - i) * P)
                        dve.wait_ge(s0_mask, h * NT + i + 1)
                        dve.tensor_copy(hi, w).then_inc(a0_own, 1)
                        dve.wait_ge(a0_own, 2 * h + 1)
                        dve.tensor_tensor(A0_lo[:, h % 2, OFF[i]:OFF[i + 1]], w, hi.bitcast(F32), ALU.subtract).then_inc(a0_own, 1)
                    if h >= QUAD and h % QUAD == 1 and j == 5:
                        read_out0(h // QUAD - 1)
                if h == 0:
                    dve.wait_ge(wout_hi_ready, 1)
                    dve.tensor_tensor(wout_lo[:], wout[:], wout_hi[:].bitcast(F32), ALU.subtract).then_inc(wout_ready, 1)
            read_out0(H0 // QUAD - 1)
            for k in range(2 * NHALF):
                half, c = k // NC, k % NC
                tk = slice(half * HALF, (half + 1) * HALF)
                dve.wait_ge(oT_hi_ready, k + 1)
                dve.tensor_tensor(oT_lo[:, c, tk], ps[:, k, :], oT_hi[:, c, tk].bitcast(F32), ALU.subtract)\
                    .then_inc(oT_ready, 1)
            for t in range(NT):
                dve.wait_ge(so_ps, t + 1)
                if t >= 2:
                    dve.wait_ge(x_ready, t - 1)
                dve.scalar_tensor_tensor(out=mix0_b[:, t % 2, :], in0=ps[:, 4 + t % 2, 0:D], scalar=0.25,
                                         in1=g0_tok[:, t, :], op0=ALU.mult, op1=ALU.mult).then_inc(mixed, 1)
                if t >= 1:
                    tile_stats(t - 1)
            tile_stats(NT - 1)

            layernorm_stats(1)
            layernorm_norm(1)
            dve.memset(V1[:, :, :, D1:D1 + 1], 1.0)
            layernorm_lo(1)

            def logits(_, half):
                dve.wait_ge(lgT_ps, half + 1)
                dve.tensor_copy(lgT[:, half * HALF:(half + 1) * HALF], ps[0:NE, 6 + side_of["logits", 0, half] % 2, :])\
                    .then_inc(lgT_copied, 1)

            def turn_logits(*_):
                dve.wait_ge(lg_ps, 1)
                o = ps[:, 6 + side_of["turn_logits", 0, 0] % 2, 0:NT * NE]
                link(dve.tensor_copy(lg[:], o.rearrange("p (t e) -> p t e", t=NT)))
                link(dve.tensor_scalar(r_a[:], lg[:], -1.0, None, ALU.mult))
                dve.tensor_tensor(r_a[:], r_a[:], lg[:], ALU.max).then_inc(lg_read, 1)

            def values(t):
                dve.wait_ge(v_ps, t + 1)
                dve.tensor_copy(V1[:, t, :, 0:D1], ps[:, 4 + t % 2, :].rearrange("p (g d) -> p g d", g=G1))\
                    .then_inc(v_read, 1)

            dve.wait_ge(in_l1c, 64)

            def project(n, half):
                i = 2 * n + half
                tk = slice(half * HALF, (half + 1) * HALF)
                b = ps[:, 6 + side_of["project", n, half] % 2, :]
                dve.wait_ge(pj_ps, i + 1)
                k = part_of["project", n, half]
                if k >= 3:
                    dve.wait_ge(parts_ready, k - 2)
                if i >= 2:
                    dve.wait_ge(pj_rot, i - 1)
                dve.tensor_tensor(rot[:, k % 3], b, cos1[:, tk], ALU.mult)
                for to, frm in ((slice(0, 64), slice(64, 128)), (slice(64, 128), slice(0, 64))):
                    last = dve.tensor_tensor(swap[to, i % 2, :], b[frm, :], sin1[frm, tk], ALU.mult)
                last.then_inc(pj_cos, 1)

            def scores(h, j):
                n = h * NT + j
                w = (NT - j) * P
                dve.wait_ge(s1_ps, n + 1)
                if n >= 2:
                    dve.wait_ge(s1_exp, n - 1)
                slope = float(np.float32(2.0) ** np.float32(-(h + 1) * 8.0 / H1))
                dve.scalar_tensor_tensor(out=cap[:, n % 2, 0:w], in0=dist[:, 0:w], scalar=slope,
                                         in1=psf[:, 1024 * (n % 2):1024 * (n % 2) + w], op0=ALU.mult, op1=ALU.add)\
                    .then_inc(s1_bias, 1)

            def context(h, r):
                k = 3 * h + r
                tiles = min(3, NT - 3 * r)
                dve.wait_ge(c_ps, k + 1)
                if k >= 1:
                    dve.wait_ge(c_ready, k)
                if h >= 2 and r == 0:
                    dve.wait_ge(cT_ps, 2 * (h - 1))
                o = ps[:, 4 + k % 2, 0:tiles * (D1 + 1)].rearrange("p (t d) -> p t d", t=tiles)
                link(dve.reciprocal(c_rden[:, 0:tiles], o[:, :, D1:D1 + 1]))
                dve.tensor_tensor(ctx_tok[:, h % 2, 3 * r:3 * r + tiles, :], o[:, :, 0:D1],
                                  c_rden[:, 0:tiles].to_broadcast((P, tiles, D1)), ALU.mult).then_inc(c_ready, 1)

            def turn(h, half):
                k = part_of["turn", h, half]
                dve.wait_ge(cT_ps, 2 * h + half + 1)
                if k >= 3:
                    dve.wait_ge(parts_ready, k - 2)
                dve.tensor_copy(rot[:, k % 3], ps[:, 6 + side_of["turn", h, half] % 2, :]).then_inc(cT_read, 1)

            def add_out(m, t):
                dve.wait_ge(s_ps, NT * m + t + 1)
                if m >= 1 and t == 0:
                    dve.wait_ge(s_added, NT * m)
                dve.tensor_tensor(s_tok[:, t, :], ps[:, 6 + side_of["out", m, t] % 2, 0:D],
                                  bo[:] if m == 0 else s_tok[:, t, :], ALU.add).then_inc(s_added, 1)

            def router(part):
                if part == 0:
                    dve.wait_ge(sp_a, 1)
                    dve.tensor_scalar(r_c[:], r_b[:], 1.0, None, ALU.add).then_inc(sp_b, 1)
                    dve.wait_ge(sp_b, 1)
                    link(dve.tensor_scalar(r_a[:], r_c[:], 1.0, None, ALU.is_equal))
                elif part == 1:
                    dve.wait_ge(sp_a, 2)
                    link(dve.tensor_scalar(r_c[:], r_c[:], -1.0, None, ALU.add))
                    link(dve.tensor_tensor(r_c[:], r_c[:], r_a[:], ALU.add))
                    link(dve.tensor_tensor(r_d[:], r_d[:], r_a[:], ALU.add))
                    link(dve.reciprocal(r_a[:], r_c[:]))
                    link(dve.tensor_tensor(r_d[:], r_d[:], r_b[:], ALU.mult))
                elif part == 2:
                    link(dve.tensor_tensor(r_d[:], r_d[:], r_a[:], ALU.mult))
                    link(dve.tensor_scalar(r_c[:], lg[:], 0.0, None, ALU.max))
                    dve.tensor_tensor(r_a[:], r_d[:], r_c[:], ALU.add).then_inc(sp_b, 1)
                elif part == 3:
                    dve.wait_ge(sp_b, 2)
                    dve.wait_ge(sp_a, 3)
                    link(dve.tensor_scalar(r_c[:], r_b[:], 1e-30, None, ALU.max))
                    link(dve.reciprocal(r_d[:], r_c[:]))
                    link(dve.tensor_tensor(r_d[:], r_d[:], r_a[:], ALU.mult))
                    link(dve.tensor_tensor(r_d[:], r_d[:], r_b[:], ALU.add))
                    link(dve.tensor_scalar(r_b[:], r_d[:], 0.5, None, ALU.mult))
                    eb = ebias[:].rearrange("p (t e) -> p t e", t=1).to_broadcast((P, NT, NE))
                    link(dve.tensor_tensor(r_a[:], r_b[:], eb, ALU.add))
                elif part < 8:
                    for t in (2 * (part - 4), 2 * (part - 4) + 1):
                        link(dve.max(top[:, t, :], r_a[:, t, :]))
                        link(dve.max_index(topi[:, t, :], top[:, t, :], r_a[:, t, :]))
                elif part == 8:
                    link(dve.tensor_copy(topf[:], topi[:]))
                elif part < 9 + TOPK:
                    k = part - 9
                    it = iota[:].rearrange("p (t e) -> p t e", t=1).to_broadcast((P, NT, NE))
                    dst = r_d if k == 0 else r_c
                    link(dve.tensor_tensor(dst[:], it, topf[:, :, k:k + 1].to_broadcast((P, NT, NE)), ALU.is_equal))
                    if k:
                        link(dve.tensor_tensor(r_d[:], r_d[:], r_c[:], ALU.add))
                else:
                    link(dve.tensor_tensor(r_d[:], r_d[:], r_b[:], ALU.mult))
                    link(dve.tensor_reduce(r_sum[:], r_d[:], AX_X, ALU.add))
                    link(dve.tensor_scalar(r_sum[:], r_sum[:], 1e-20, None, ALU.add))
                    link(dve.reciprocal(r_inv[:], r_sum[:]))
                    link(dve.tensor_scalar(r_inv[:], r_inv[:], 0.5, None, ALU.mult))
                    dve.tensor_tensor(r_d[:], r_d[:], r_inv[:].to_broadcast((P, NT, NE)), ALU.mult)\
                        .then_inc(gates_ready, 1)

            def gates(_, half):
                dve.wait_ge(gT_ps, half + 1)
                dve.tensor_copy(gT[:, half * HALF:(half + 1) * HALF], ps[0:NE, 6 + side_of["gates", 0, half] % 2, :])\
                    .then_inc(gT_ready, 1)

            for step in DVE_STEPS1:
                {"project": project, "scores": scores, "turn": turn, "context": context, "out": add_out,
                 "values": values, "logits": logits, "turn_logits": turn_logits, "router": router,
                 "gates": gates}[step[0]](*step[1:])

            for s in range(2 * U1):
                b = s % 2
                dve.wait_ge(gu1_ps, s + 1)
                if s >= 2:
                    dve.wait_ge(th1_ready, s - 1)
                    dve.wait_ge(up_ready, s - 1)
                dve.tensor_scalar(gu[:, b].rearrange("p m n -> p (m n)"), psf[:, 1024 * b:1024 * b + 1024], ALPHA, -ALPHA,
                                  ALU.min, ALU.max).then_inc(clip_ready, 1)
                dve.wait_ge(th1_ready, s + 1)
                link(dve.scalar_tensor_tensor(out=e1_a[:, b, :], in0=e1_a[:, b, :], scalar=1.0, in1=gu[:, b, 0, :],
                                              op0=ALU.add, op1=ALU.mult))
                dve.wait_ge(up_ready, s + 1)
                if s >= 2:
                    dve.wait_ge(h1_parts_ready, s - 1)
                dve.tensor_tensor(h1[:, b, :], e1_a[:, b, :], e1_b[:, b, :], ALU.mult).then_inc(h1_ready, 1)
            collect_f(2 * U1, dn1_ps, f1T)
            for t in range(NT):
                dve.wait_ge(fth_ready, NT + t + 1)
                b = t % 4
                if t >= 4:
                    dve.wait_ge(x_ready, NT + t - 3)
                link(dve.scalar_tensor_tensor(out=mix1_b[:, b, :], in0=mix1_a[:, b, :], scalar=1.0,
                                              in1=ps[:, b, 0:D], op0=ALU.add, op1=ALU.mult))
                dve.scalar_tensor_tensor(out=mix1_b[:, b, :], in0=mix1_b[:, b, :], scalar=0.5,
                                         in1=s_tok[:, t, :], op0=ALU.mult, op1=ALU.mult).then_inc(mixed, 1)

        @block.gpsimd
        def _(pool):
            steps = [0]

            def link(ins):
                steps[0] += 1
                ins.then_inc(pool_step, 1)
                pool.wait_ge(pool_step, steps[0])

            def causal(block_ap, ready, n, done):
                pool.wait_ge(ready, n + 1)
                pool.affine_select(out=block_ap, in_=block_ap, compare_op=ALU.is_ge, fill=0.0, base=0,
                                   pattern=[[1, P]], channel_multiplier=-1).then_inc(done, 1)

            def scale0(J):
                pool.wait_ge(ladder_ready, J + 1)
                if J >= 1:
                    pool.wait_ge(w0_lo_ready, J)
                if J >= 3:
                    pool.wait_ge(dn0_ps, 4 * (J - 2))
                for m in range(3):
                    sc = pks[:, J % 2, m:m + 1, :].to_broadcast((P, 2, 2 * P))
                    dst = w0[:, m] if m < 2 else w0_dn[:, J % 3]
                    last = pool.tensor_tensor(dst, dq_a[:, m], sc, ALU.mult)
                last.then_inc(w0_ready, 1)

            def low0(J):
                pool.wait_ge(w0_hi_ready, J + 1)
                pool.tensor_tensor(w0_lo[:, J % 3], w0[:], w0_hi[:, J % 3].bitcast(F32), ALU.subtract)\
                    .then_inc(w0_lo_ready, 1)

            def rotate_tile(t):
                qd = qk_tok[:, t, :].rearrange("p (h d) -> p h d", h=2 * H0)
                ra, rb = (r[:, t % 2, :].rearrange("p (h d) -> p h d", h=2 * H0) for r in (rope_a, rope_b))
                hf = D0 // 2
                pool.wait_ge(qk_copied, t + 1)
                if t >= 2:
                    pool.wait_ge(qk_centred, t - 1)
                    pool.wait_ge(qk_var, t - 1)
                pool.tensor_tensor(ra, qd, rope0[:, t, 0:1, :].to_broadcast((P, 2 * H0, D0)), ALU.mult)
                pool.tensor_tensor(rb[:, :, 0:hf], qd[:, :, hf:], rope0[:, t, 1:2, 0:hf].to_broadcast((P, 2 * H0, hf)),
                                   ALU.mult)
                pool.tensor_tensor(rb[:, :, hf:], qd[:, :, 0:hf], rope0[:, t, 1:2, hf:].to_broadcast((P, 2 * H0, hf)),
                                   ALU.mult).then_inc(qk_split, 1)

            def shift_tile(t):
                qd = qk_tok[:, t, :].rearrange("p (h d) -> p h d", h=2 * H0)
                pool.wait_ge(qk_scaled, t + 1)
                pool.tensor_tensor(qd, qd, lns[:, 1:2, :].to_broadcast((P, 2 * H0, D0)), ALU.add).then_inc(qk_ready, 1)

            pool.wait_ge(wqkv_hi_ready, 1)
            pool.tensor_tensor(wqkv_lo[:], wqkv[:], wqkv_hi[:].bitcast(F32), ALU.subtract).then_inc(wqkv_ready, 1)
            scale0(0)
            low0(0)
            pool.wait_ge(in_l0c, 48)
            for s in range(2 * U0 + 1):
                if s < 2 * U0:
                    pool.wait_ge(gu0_copied, s + 1)
                    if s >= 3:
                        pool.wait_ge(h0_ready, s - 2)
                    pool.tensor_tensor(e0_p[:, s % 3, :], e0_gu[:, s % 3, 0, :], e0_gu[:, s % 3, 1, :], ALU.mult)\
                        .then_inc(gated_ready, 1)
                if block_at(s, 5):
                    scale0(block_at(s, 5))
                if block_at(s, 6):
                    low0(block_at(s, 6))
                if tile_at(s, 0) is not None:
                    rotate_tile(tile_at(s, 0))
                if s >= VAR_STEP + 4 and s - VAR_STEP - 4 < NT:
                    shift_tile(s - VAR_STEP - 4)

            for t in range(NT):
                pool.wait_ge(stk_hi, 2 * t + 2)
                src = qk_tok[:, t, D:2 * D].rearrange("p (h a d) -> p h a d", h=H0, a=1)
                pool.tensor_tensor(stack[:, t % 2, 1, :, 2:4, :].bitcast(F32R), src.to_broadcast((P, H0, 2, D0)),
                                   stack[:, t % 2, 1, :, 0:2, :], ALU.subtract).then_inc(stk_k_ready, 1)
            for h in range(H0):
                for j in range(NT):
                    causal(A0_row(h, j)[:, 0:P], s0_four, h * NT + j, s0_mask)
                    if j in LOW_AT:
                        i = LOW_AT.index(j)
                        pool.wait_ge(a0_hi, (SPLIT - 1) * h + i + 1)
                        pool.tensor_tensor(A0_lo[:, h % 2, OFF[i]:OFF[i + 1]], A0_row(h, i),
                                           A0_hi(h, i, 0, (NT - i) * P).bitcast(F32), ALU.subtract).then_inc(a0_ready, 1)
            for t in range(NT):
                pool.wait_ge(mixed, t + 1)
                pool.tensor_tensor(x_tok[:, t, :], x_tok[:, t, :], mix0_b[:, t % 2, :], ALU.add).then_inc(x_ready, 1)

            pool.wait_ge(rw_hi_ready, 1)
            pool.tensor_tensor(rw_lo[:], rw[:], rw_hi[:].bitcast(F32), ALU.subtract).then_inc(rw_ready, 1)
            pool.wait_ge(wv_hi_ready, 1)
            pool.tensor_tensor(wv_lo, wv, wv_hi.bitcast(F32), ALU.subtract).then_inc(wv_ready, 1)

            def scores(h, j):
                causal(P1[:, h % 2, OFF[j]:OFF[j] + P], s1_exp, h * NT + j, s1_mask)

            def split_wqk(n):
                pool.wait_ge(wqk_hi_ready, n + 1)
                pool.tensor_tensor(wqk_lo[:, n % 2], wqk[:, n % 2], wqk_hi[:, n % 2].bitcast(F32), ALU.subtract)\
                    .then_inc(wqk_ready, 1)

            def split_wo(m):
                pool.wait_ge(wo_hi_ready, m + 1)
                pool.tensor_tensor(wo_lo[:], wo[:, m % 2], wo_hi[:].bitcast(F32), ALU.subtract).then_inc(wo_ready, 1)

            def project(n, half):
                i = 2 * n + half
                r = rot[:, part_of["project", n, half] % 3]
                pool.wait_ge(pj_cos, i + 1)
                pool.tensor_tensor(r, r, swap[:, i % 2, :], ALU.add).then_inc(pj_rot, 1)

            def low_part(step, hi, lo):
                pool.wait_ge(parts_hi, part_of[step] + 1)
                pool.tensor_tensor(lo, rot[:, part_of[step] % 3], hi.bitcast(F32), ALU.subtract).then_inc(parts_ready, 1)

            def project_part(n, half):
                kind, hd = PROJ[n]
                hi, lo = ((q_hi, q_lo) if kind == "q" else (k_hi, k_lo))
                tk = slice(half * HALF, (half + 1) * HALF)
                low_part(("project", n, half), hi[:, hd % 2, tk], lo[:, hd % 2, tk])

            def turn_part(h, half):
                tk = slice(half * HALF, (half + 1) * HALF)
                low_part(("turn", h, half), cT_hi[:, h % PAIR, tk], cT_lo[:, h % PAIR, tk])

            def split_expert(u):
                pool.wait_ge(e_hi_ready, u + 1)
                pool.tensor_tensor(e_lo[:, u % 3], eraw[:, u % 3], e_hi[:, u % 3].bitcast(F32), ALU.subtract)\
                    .then_inc(e_ready, 1)

            split_wqk(0)
            split_wqk(1)
            for step in POOL_STEPS1:
                {"project": project, "project_part": project_part, "scores": scores, "turn_part": turn_part,
                 "split_wqk": split_wqk, "split_wo": split_wo, "split_expert": split_expert}[step[0]](*step[1:])

            def low_h(r):
                pool.wait_ge(h1_hi_ready, r + 1)
                pool.tensor_tensor(h1_lo[:, r % 3, :], h1[:, r % 2, :], h1_hi[:, r % 3, :].bitcast(F32), ALU.subtract)\
                    .then_inc(h1_parts_ready, 1)

            for s in range(2 * U1 + 1):
                if s < 2 * U1:
                    b, u, half = s % 2, s // 2, s % 2
                    pool.wait_ge(clip_ready, s + 1)
                    if s >= 2:
                        pool.wait_ge(h1_ready, s - 1)
                    if u < NE:
                        pool.wait_ge(in_pb[u % 2], 16 * (u // 2 + 1))
                        pool.tensor_tensor(e1_b[:, b, :], gu[:, b, 1, :], pb[:, u % 2, half * HALF:(half + 1) * HALF],
                                           ALU.mult).then_inc(up_ready, 1)
                    else:
                        pool.tensor_scalar(e1_b[:, b, :], gu[:, b, 1, :], 0.5, None, ALU.mult).then_inc(up_ready, 1)
                if s >= 1:
                    low_h(s - 1)
                if s % 2 == 1 and s // 2 + 2 < U1:
                    split_expert(s // 2 + 2)
            for t in range(NT):
                pool.wait_ge(mixed, NT + t + 1)
                pool.tensor_tensor(x_tok[:, t, :], x_tok[:, t, :], mix1_b[:, t % 4, :], ALU.add).then_inc(x_ready, 1)


VAR_STEP = 2 * NT + 1
ROUTER = {"act": [6, 10, 16], "dve": [8, 12, 14, 18] + [20 + 2 * i for i in range(10)]}
GATES_AT = 6
PROJ = [("k", 0)] + [p for h in range(H1) for p in ([("q", h)] + [("k", h // REP + 1)] * (h % REP == 2 and h // REP + 1 < G1))]


def schedule():
    steps = []
    first = PROJ.index(("q", 0))
    for i, n in enumerate(range(first + 1)):
        steps += [("project", n, 0)] + [("values", 2 * i)] * i + [("values", 2 * i + 1)] * i
        steps += [("project", n, 1)] + [("values", 0), ("values", 1)] * (i == 0)
    steps += [("values", t) for t in range(4, NT)]
    for h in range(H1 + 1):
        todo = []
        if h + 1 < H1:
            at = PROJ.index(("q", h + 1))
            if h % REP == 2 and h // REP + 1 < G1:
                todo += [("project", at - 1, 1)]
            todo += [("project", at, 0), ("project", at, 1)]
            if h % REP == 1 and h // REP + 1 < G1:
                todo += [("project", at + 1, 0)]
        if h == 0:
            todo += [("logits", 0, 0), ("logits", 0, 1), ("turn_logits", 0, 0)]
        for j in range(NT):
            if h < H1:
                steps.append(("scores", h, j))
            if h >= 1:
                steps.append(("context", h - 1, j))
            outs = [("out", (h - 2) // PAIR - 1, 1 + 2 * j + i) for i in (0, 1) if 1 + 2 * j + i < NT]
            outs = outs if h >= PAIR + 2 and (h - 2) % PAIR == 0 else []
            steps += outs[:1]
            if todo:
                steps.append(todo.pop(0))
            steps += outs[1:]
            if h >= 2 and j in (3, 4):
                steps.append(("turn", h - 2, j - 3))
            if h >= PAIR + 1 and (h - 2) % PAIR == PAIR - 1 and j == 7:
                steps += [("out", (h - 2) // PAIR, 0)]
            if h == GATES_AT and j in (6, 7):
                steps.append(("gates", 0, j - 6))
    steps += [("turn", H1 - 1, 0), ("turn", H1 - 1, 1)]
    steps += [("experts", 0), ("experts", 1)]
    steps += [("out", H1 // PAIR - 1, t) for t in range(NT)]
    return steps


STEPS1 = schedule()
SIDE = [s for s in STEPS1 if s[0] in ("project", "turn", "out", "logits", "turn_logits", "gates")]
side_of = {s: n for n, s in enumerate(SIDE)}
part_of = {s: n for n, s in enumerate([s for s in STEPS1 if s[0] in ("project", "turn")])}


def follow(engine):
    out, later = [], []
    for n, s in enumerate(STEPS1):
        name = s[0]
        if name == "scores" and s[2] == 0:
            out += later
            later = []
        if name == "scores":
            out.append(s)
            if engine in ROUTER and NT * s[1] + s[2] in ROUTER[engine]:
                out.append(("router", ROUTER[engine].index(NT * s[1] + s[2])))
        elif name == "context":
            if engine != "dve" and s[1] == H1 - 1 and s[2] in (2, 4):
                out.append(("split_expert", s[2] // 2 - 1))
            if engine == "dve" and (s[2] % 3 == 2 or s[2] == NT - 1):
                out.append(("context", s[1], s[2] // 3))
        elif name in ("project", "turn"):
            if engine == "dve" or (engine == "pool" and name == "project"):
                out.append(s)
            if engine != "dve":
                later.append((name + "_part", *s[1:]))
                if name == "project" and s[2] == 1 and s[1] + 2 < len(PROJ):
                    later.append(("split_wqk", s[1] + 2))
                if s == ("turn", 0, 0):
                    later.append(("split_wo", 0))
        elif name in ("out", "logits", "turn_logits", "gates", "values"):
            if engine == "dve":
                out.append(s)
            elif name == "out" and s[2] == NT - 1 and s[1] + 1 < H1 // PAIR:
                later.append(("split_wo", s[1] + 1))
        if name == "scores" or not any(x[0] == "scores" for x in STEPS1[:n]) or \
                not any(x[0] == "scores" for x in STEPS1[n:]):
            out += later
            later = []
    return out


ACT_STEPS1 = follow("act")
DVE_STEPS1 = follow("dve")
POOL_STEPS1 = follow("pool")


def kernel(**inputs):
    import numpy as _np
    import concourse.bacc as _bacc
    from concourse import mybir as _mybir
    from concourse.bass_utils import run_bass_kernel_spmd as _run

    a = {k: _np.asarray(v) for k, v in inputs.items()}
    inv0 = (_np.float32(1.0) / _np.power(_np.float32(10000.0), _np.arange(0, D0, 2, dtype=_np.float32) / _np.float32(D0))).astype(_np.float32)
    ang0 = _np.arange(TOK, dtype=_np.float32)[:, None] * inv0[None, :]
    c0, s0 = _np.cos(ang0), _np.sin(ang0)
    rope0 = _np.stack([_np.concatenate([c0, c0], 1), _np.concatenate([-s0, s0], 1)], 1).astype(_np.float32)
    rope0 = rope0.reshape(NT, P, 2, D0).transpose(1, 0, 2, 3)
    inv1 = (_np.float32(1.0) / _np.power(_np.float32(10000.0), _np.arange(0, D1, 2, dtype=_np.float32) / _np.float32(D1))).astype(_np.float32)
    ang1 = (_np.arange(TOK, dtype=_np.float32)[:, None] * inv1[None, :]).T
    c1, s1 = _np.cos(ang1), _np.sin(ang1)
    consts = {
        "ident": _np.eye(P, dtype=_np.float32),
        "rope0": rope0,
        "cos1": _np.concatenate([c1, c1], 0),
        "sin1": _np.concatenate([s1, -s1], 0),
        "dist": (_np.arange(P)[:, None] - _np.arange(TOK)[None, :]).astype(_np.float32),
        "iota": _np.tile(_np.arange(NE, dtype=_np.float32), (P, 1)),
    }

    def blocks(w):
        return w.T.reshape(w.shape[1], NJ, P, 2).transpose(1, 0, 3, 2).reshape(NJ, w.shape[1], 2 * P)

    def rows(v):
        return _np.repeat(v, P // v.shape[1], axis=1)

    def heads(w, n):
        return w.reshape(P, NC, n, D1 // 2, 2).transpose(2, 0, 1, 4, 3).reshape(n, P, NC * D1)

    def chunks(w):
        return w.transpose(0, 2, 1).reshape(len(w), P, D)

    def with_shared(name):
        return _np.concatenate([a[f"L1_ffn_{name}_w"], a[f"L1_ffn_shared_{name}_w"][None]], 0)

    wq, wk = heads(a["L1_attn_Wq"], H1), heads(a["L1_attn_Wk"], G1)
    feeds = {
        "x": a["L0_attn_x"].reshape(TOK, D), "wqkv": a["L0_attn_w_qkv"], "wout": a["L0_attn_w_out"],
        "lns": a["L0_attn_ln_scale"], "lnb": a["L0_attn_ln_bias"],
        "packed": _np.stack([blocks(a["L0_ffn_gate_W_packed"]), blocks(a["L0_ffn_up_W_packed"]),
                             a["L0_ffn_down_W_packed"].T.reshape(NJ, P, D)], 2),
        "scales": _np.stack([rows(blocks(a["L0_ffn_gate_scales"])), rows(blocks(a["L0_ffn_up_scales"])),
                             rows(a["L0_ffn_down_scales"].T.reshape(NJ, D // BLK, D))], 2),
        "wqk": _np.stack([(wq if kind == "q" else wk)[i] for kind, i in PROJ]), "wv": a["L1_attn_Wv"],
        "wo": a["L1_attn_Wo"], "bo": a["L1_attn_bo"],
        "rw": a["L1_ffn_router_w"].T.reshape(P, NC, NE), "eb": a["L1_ffn_expert_bias"],
        "experts": _np.stack([chunks(with_shared("gate")), chunks(with_shared("up")),
                              with_shared("down").transpose(0, 2, 1)], 2),
        **consts,
    }
    nc = _bacc.Bacc("TRN2", target_bir_lowering=False, num_devices=1)
    arrays, args = {}, []
    for name, v in feeds.items():
        v = _np.ascontiguousarray(v)
        arrays[f"in_{name}"] = v
        args.append(nc.dram_tensor(f"in_{name}", v.shape, _mybir.dt.from_np(v.dtype), kind="ExternalInput").ap())
    out = nc.dram_tensor("out", (1, TOK, D), F32, kind="ExternalOutput").ap()
    build_program(nc, *args, out)
    r = _run(nc, [arrays], core_ids=[0])
    return r.results[0]["out"]
```
